# Optimizing a Trainium2 kernel written in Bass

```python
import numpy as np
import jax
import jax.numpy as jnp

def _softmax(x, axis=-1):
    return jax.nn.softmax(x, axis=axis)

def _gelu(x):
    return jax.nn.gelu(x, approximate=True)

def _silu(x):
    return jax.nn.silu(x)

def _sigmoid(x):
    return jax.nn.sigmoid(x)

def _layernorm(x, axis=-1, eps=1e-05):
    m = jnp.mean(x, axis=axis, keepdims=True)
    v = jnp.var(x, axis=axis, keepdims=True)
    return (x - m) / jnp.sqrt(v + eps)

def _scatter_add(tgt, idx, src, axis=0):
    return tgt.at[idx].add(src)

def _segment_sum(src, seg, n):
    return jax.ops.segment_sum(src, seg, n)
kernel_name = 'mk_lm_tower_d1_tok_ids1024_r4_37292a'

def setup_inputs(seed: int=0):
    np.random.seed(seed)
    _w = jnp.asarray

    def _rec_inputs():
        import jax
        import jax.numpy as jnp
        _rk = jax.random.key(seed)
        x = jax.random.randint(jax.random.fold_in(_rk, 1), (4, 512), 0, 12564, jnp.int32)
        return x
    x = _rec_inputs()

    def _L0_tok_setup():
        import jax, jax.numpy as jnp
        import numpy as np
        VOCAB = 50257
        D_MODEL = 256
        N_BASES = 4
        B, S = (8, 2048)
        key = jax.random.key(seed)
        k1, k2, k3, k4 = jax.random.split(key, 4)
        x = jax.random.randint(k1, (B, S), 0, VOCAB, dtype=jnp.int32).astype(jnp.int64)
        coeff_weight = jax.random.normal(k2, (VOCAB, N_BASES), dtype=jnp.float32)
        base_embed_weight = jax.random.normal(k3, (N_BASES, D_MODEL), dtype=jnp.float32)
        lang_bias = jax.random.normal(k4, (N_BASES, D_MODEL), dtype=jnp.float32)
        return {'x': x, 'lang_id': 2, 'coeff_weight': coeff_weight, 'base_embed_weight': base_embed_weight, 'lang_bias': lang_bias}
    _L0_tok_all = _L0_tok_setup()
    _L0_tok_in = {k: v for k, v in _L0_tok_all.items() if k in ('coeff_weight', 'base_embed_weight', 'lang_bias')}
    del _L0_tok_all

    def _L0_attn_setup():
        import jax, jax.numpy as jnp
        import numpy as np
        N_HEAD = 16
        key = jax.random.key(seed)
        k1, k2, k3 = jax.random.split(key, 3)
        b, t, c = (4, 512, 256)
        x = jax.random.normal(k1, (b, t, c), dtype=jnp.float32)
        w_qkv = jax.random.normal(k2, (c, 3 * c), dtype=jnp.float32) * c ** (-0.5)
        w_proj = jax.random.normal(k3, (c, c), dtype=jnp.float32) * c ** (-0.5)
        return {'x': x, 'w_qkv': w_qkv, 'w_proj': w_proj}
    _L0_attn_all = _L0_attn_setup()
    _L0_attn_in = {k: v for k, v in _L0_attn_all.items() if k in ('w_qkv', 'w_proj')}
    del _L0_attn_all

    def _L0_ffn_setup():
        import jax, jax.numpy as jnp
        import numpy as np
        key = jax.random.key(seed)
        ks = jax.random.split(key, 6)
        B, L, D, E = (4, 512, 256, 4)
        H = 4 * D
        x = jax.random.normal(ks[0], (B, L, D), dtype=jnp.float32)
        rW1 = jax.random.normal(ks[1], (D, 2 * D), dtype=jnp.float32) * (2.0 / D) ** 0.5
        rb1 = jnp.zeros((2 * D,), dtype=jnp.float32)
        rW2 = jax.random.normal(ks[2], (2 * D, E), dtype=jnp.float32) * (2.0 / (2 * D)) ** 0.5
        rb2 = jnp.zeros((E,), dtype=jnp.float32)
        We1 = jax.random.normal(ks[3], (E, D, H), dtype=jnp.float32) * (2.0 / D) ** 0.5
        be1 = jnp.zeros((E, H), dtype=jnp.float32)
        We2 = jax.random.normal(ks[4], (E, H, D), dtype=jnp.float32) * (2.0 / H) ** 0.5
        be2 = jnp.zeros((E, D), dtype=jnp.float32)
        return {'x': x, 'rW1': rW1, 'rb1': rb1, 'rW2': rW2, 'rb2': rb2, 'We1': We1, 'be1': be1, 'We2': We2, 'be2': be2}
    _L0_ffn_all = _L0_ffn_setup()
    _L0_ffn_in = {k: v for k, v in _L0_ffn_all.items() if k in ('rW1', 'rb1', 'rW2', 'rb2', 'We1', 'be1', 'We2', 'be2')}
    del _L0_ffn_all
    return {'x': x, 'L0_tok_coeff_weight': _L0_tok_in['coeff_weight'], 'L0_tok_base_embed_weight': _L0_tok_in['base_embed_weight'], 'L0_tok_lang_bias': _L0_tok_in['lang_bias'], 'L0_attn_w_qkv': _L0_attn_in['w_qkv'], 'L0_attn_w_proj': _L0_attn_in['w_proj'], 'L0_ffn_rW1': _L0_ffn_in['rW1'], 'L0_ffn_rb1': _L0_ffn_in['rb1'], 'L0_ffn_rW2': _L0_ffn_in['rW2'], 'L0_ffn_rb2': _L0_ffn_in['rb2'], 'L0_ffn_We1': _L0_ffn_in['We1'], 'L0_ffn_be1': _L0_ffn_in['be1'], 'L0_ffn_We2': _L0_ffn_in['We2'], 'L0_ffn_be2': _L0_ffn_in['be2']}

def reference(x, L0_tok_coeff_weight, L0_tok_base_embed_weight, L0_tok_lang_bias, L0_attn_w_qkv, L0_attn_w_proj, L0_ffn_rW1, L0_ffn_rb1, L0_ffn_rW2, L0_ffn_rb2, L0_ffn_We1, L0_ffn_be1, L0_ffn_We2, L0_ffn_be2):
    import jax
    import jax.numpy as jnp

    def _L0_tok_ref(x, lang_id, coeff_weight, base_embed_weight, lang_bias):
        import jax, jax.numpy as jnp
        import numpy as np
        VOCAB = 50257
        D_MODEL = 256
        N_BASES = 4
        B, S = (8, 2048)
        coeff = jax.nn.softmax(coeff_weight[x], axis=-1)
        bases = base_embed_weight + lang_bias
        scale = jnp.sqrt(jnp.asarray(bases.shape[1], dtype=bases.dtype))
        out = jnp.einsum('bsn,nd->bsd', coeff, bases) * scale
        out = out + lang_bias[lang_id] * 0.1
        return out

    def _L0_attn_ref(x, w_qkv, w_proj):
        import jax, jax.numpy as jnp
        import numpy as np
        N_HEAD = 16
        b, t, c = x.shape
        h = N_HEAD
        d = c // h
        qkv = x @ w_qkv
        q, k, v = jnp.split(qkv, 3, axis=-1)
        q = q.reshape(b, t, h, d).transpose(0, 2, 1, 3)
        k = k.reshape(b, t, h, d).transpose(0, 2, 1, 3)
        v = v.reshape(b, t, h, d).transpose(0, 2, 1, 3)
        att = jnp.einsum('bhqd,bhkd->bhqk', q, k) * d ** (-0.5)
        causal = jnp.tril(jnp.ones((t, t), dtype=bool))
        att = jnp.where(causal[None, None, :, :], att, -jnp.inf)
        att = jax.nn.softmax(att, axis=-1)
        y = jnp.einsum('bhqk,bhkd->bhqd', att, v)
        y = y.transpose(0, 2, 1, 3).reshape(b, t, c)
        return y @ w_proj

    def _L0_ffn_ref(x, rW1, rb1, rW2, rb2, We1, be1, We2, be2):
        import jax, jax.numpy as jnp
        import numpy as np
        E = We1.shape[0]
        top_k = min(2, E)
        rh = jax.nn.gelu(x @ rW1 + rb1, approximate=False)
        router_logits = rh @ rW2 + rb2
        router_probs = jax.nn.softmax(router_logits, axis=-1)
        expert_weights, expert_indices = jax.lax.top_k(router_probs, top_k)
        one_hot = jax.nn.one_hot(expert_indices, E, dtype=x.dtype)
        token_mask = one_hot.sum(axis=2)
        combine_w = (one_hot * expert_weights[..., None]).sum(axis=2)
        out = jnp.zeros_like(x)
        for e in range(E):
            xi = x * token_mask[..., e:e + 1]
            h = jax.nn.gelu(xi @ We1[e] + be1[e], approximate=False)
            yo = h @ We2[e] + be2[e]
            out = out + yo * combine_w[..., e:e + 1]
        return out
    h = _L0_tok_ref(x, 2, L0_tok_coeff_weight, L0_tok_base_embed_weight, L0_tok_lang_bias)
    h = h + _L0_attn_ref(_layernorm(h, axis=-1), L0_attn_w_qkv, L0_attn_w_proj)
    h = h + _L0_ffn_ref(_layernorm(h, axis=-1), L0_ffn_rW1, L0_ffn_rb1, L0_ffn_rW2, L0_ffn_rb2, L0_ffn_We1, L0_ffn_be1, L0_ffn_We2, L0_ffn_be2)
    return h

_drawn_inputs = setup_inputs


def setup_inputs(seed=0):
    import zlib

    import numpy as np

    out = dict(_drawn_inputs(seed))
    spreads = {'L0_ffn_rb1': (0.0, 0.8),
     'L0_ffn_rb2': (0.0, 0.8),
     'L0_ffn_be1': (0.0, 0.8),
     'L0_ffn_be2': (0.0, 0.8)}
    factors = {}
    for name, (base, spread) in spreads.items():
        noise = np.random.default_rng([zlib.crc32(name.encode()), seed]).standard_normal(out[name].shape)
        drawn = base * np.exp(spread * noise) if base else spread * noise
        out[name] = jnp.asarray(drawn.astype(out[name].dtype))
    for name, factor in factors.items():
        out[name] = (out[name] * factor).astype(out[name].dtype)
    return out
```

```python
import numpy as np
import concourse.bass as bass
from concourse import mybir

F32, F32R, BF16, I32 = mybir.dt.float32, mybir.dt.float32r, mybir.dt.bfloat16, mybir.dt.int32
ALU, ACT, AX = mybir.AluOpType, mybir.ActivationFunctionType, mybir.AxisListType

P = 128
BATCH, SEQ, D = 4, 512, 256
NB = 4
HEADS, DH = 16, 16
E, HID, RHID = 4, 1024, 512
TB = SEQ // P
NT = BATCH * TB
KD = D // P
UNITS = 2 * BATCH
UH = 8
ROWS = P // UH
ZF = 4 * HEADS + NB
ZR = ZF + ZF // 2
EB, RB = HID // P, RHID // P
PT = 1280
EPS = 1e-5
SCALE_D, LANG = 16.0, 2
NEG = -1e30
PV_ORDER = (0, 1, 3, 2)

KB_AT = {0: (0, 512), 1: (512, 896), 2: (1024, 1280), 3: (896, 1024)}


AT = dict(M=0.28, McT=3.76, fold00=6.44, fold10=9.39, fold11=9.61, fold20=15.67, fold21=19.72, w20=30.63,
          soft=-38, mix=-35.58, CT=-32, H0=-30.1, H1=-28, rstd=-27.03, keys=-22.04, KT=-19.21, variants=-13.05,
          QA0=-7.57, QA1=5.16, values=7.61, max=20.73, shift=23.02, T=26, PV=38, PVstep=2, Zs=74.38, ZT=78,
          ZF=81.8, H20=85.8, H21=88.58, rstd2=88.77, zab=93.74, ZA0=97.56, ZA1=100.72, up=201.84, upc=9,
          ups=1.5, logits=9, LT=10.95, ex=238.85, down=2.28, comb=5.23, route=3.3, FZ=5.34, w21=16.21,
          foldE=1.33, w2E=15.14)
AT1 = {('ZA1', 3): 100.69, ('rstd2', 0): 90.98, ('zab', 0): 93.68, ('ZA0', 0): 95.63, ('ZA1', 0): 98.85,
       ('QA1', 2): 6.46, ('CT', 3): -32.13, ('QA0', 2): -12.35, ('values', 2): 4.61, ('H0', 0): -25.44,
       ('H1', 0): -22.81, ('rstd', 0): -22.6, ('QA0', 3): -13.4, ('ZF', 0): 79.74, ('QA1', 0): 4.92,
       ('ZF', 1): 80.03, ('values', 1): 4.51, ('zab', 3): 94.2, ('H21', 1): 88.05, ('ZT', 2): 77.38,
       ('mix', 2): -35.41, ('H21', 3): 87.84, ('ZA0', 2): 97.7, ('mix', 0): -32.95, ('CT', 0): -29.95,
       ('ZA0', 3): 98.36, ('mix', 1): -34.29, ('QA1', 3): 6.25, ('ZT', 1): 77.09, ('H20', 2): 85.98,
       ('H21', 2): 88.24, ('rstd2', 2): 88.76, ('zab', 2): 93.77, ('keys', 2): -21.79, ('values', 3): 8.05,
       ('variants', 0): -15.22, ('H20', 1): 84.5, ('KT', 0): -17.99, ('rstd2', 3): 88.73, ('soft', 1): -37.48,
       ('H20', 3): 87.59, ('H1', 1): -29.64, ('mix', 3): -35.88, ('H0', 2): -30.4, ('rstd2', 1): 89.28,
       ('zab', 1): 94.28, ('ZA0', 1): 96.76, ('ZA1', 2): 104.88, ('soft', 0): -37.96, ('soft', 2): -38.0,
       ('keys', 0): -21.82, ('QA0', 0): -13.06, ('ZF', 3): 83.48, ('ZT', 0): 77.35, ('rstd', 2): -26.86,
       ('variants', 2): -15.32, ('variants', 3): -13.85, ('Zs', 3): 74.63, ('ZT', 3): 79.87, ('H0', 3): -27.12,
       ('H1', 3): -25.02, ('rstd', 3): -24.05}


def step_order():
    at = []

    def put(when, *item):
        at.append((when, len(at), item))

    A = AT
    put(-60, "BcT"), put(-59, "QKV"), put(-58, "Arep")
    put(A["M"], "M"), put(A["McT"], "McT")
    for f, ch in ((0, 0), (1, 0), (1, 1), (2, 0), (2, 1)):
        put(A[f"fold{f}{ch}"], "fold", f, ch)
    put(A["w20"], "w2", 0)
    for b in range(BATCH):
        def a(name):
            return 40 * b + AT1.get((name, b), A[name])
        put(a("soft"), "soft", b), put(a("mix"), "mix", b), put(a("CT"), "CT", b)
        put(a("H0"), "H", b, 0), put(a("H1"), "H", b, 1), put(a("rstd"), "rstd", b)
        put(a("keys"), "keys", b), put(a("KT"), "KT", b)
        put(a("variants"), "variants", b)
        put(a("QA0"), "QA", b, 0)
        put(a("QA1"), "QA", b, 1)
        put(a("values"), "values", b)
        put(a("Zs"), "Zs", b), put(a("ZT"), "ZT", b), put(a("ZF"), "ZF", b), put(a("H20"), "H2", b, 0)
        put(a("H21"), "H2", b, 1), put(a("rstd2"), "rstd2", b), put(a("zab"), "zab", b)
        put(a("ZA0"), "ZA", b, 0), put(a("ZA1"), "ZA", b, 1)
    for u in range(UNITS):
        for k in range(20):
            put(20 * u + k, "S", u, k)
        put(20 * u + A["max"], "max", u)
        put(20 * u + A["shift"], "shift", u)
        for k in range(12):
            put(20 * u + A["T"] + k * 20 / 12, "T", u, k)
    for q in range(2 * UNITS):
        for n, kb in enumerate(PV_ORDER):
            put(10 * q + A["PV"] + A["PVstep"] * n, "PV", q, kb)

    for c in range(BATCH):
        for b in range(RB):
            put(A["up"] + A["upc"] * c + A["ups"] * b, "up", RB * c + b)
        put(A["up"] + A["upc"] * c + A["logits"], "logits", c), put(A["up"] + A["upc"] * c + A["LT"], "LT", c)
    t0, n = A["ex"], E * BATCH * EB
    for j in range(n):
        put(t0 + j, "up", RB * BATCH + j), put(t0 + j + 0.1, "split", j), put(t0 + j + A["down"], "down", j)
        if j % EB == EB - 1:
            put(t0 + j + A["comb"], "combine", j // EB)
    put(t0 + A["route"], "route")
    for c in range(BATCH):
        for k, what in enumerate((("FZ", c), ("FH", c, 0), ("FH", c, 1))):
            put(t0 + 8 * c + A["FZ"] + k, *what)
    put(t0 + A["w21"], "w2", 1)
    for e in (2, 3):
        put(t0 + 32 * (e - 1) + A["foldE"], "fold", e + 1, 0), put(t0 + 32 * (e - 1) + A["foldE"] + 2, "fold", e + 1, 1)
        put(t0 + 32 * (e - 1) + A["w2E"], "w2", e)
    return [item for _, _, item in sorted(at)]


MISC = ("BcT", "QKV", "Arep", "CT", "H", "KT", "QA", "M", "McT", "fold", "shift", "ZT", "ZF", "H2", "ZA",
        "LT", "FZ", "FH")


def tower_kernel(nc, x, coeff_w, base_w, lang_w, w_qkv, w_proj, rW1, rb1, rW2, rb2, We1, be1, We2, be2, out):
    order = step_order()
    misc_at = {item: n for n, item in enumerate(i for i in order if i[0] in MISC)}

    at = [(nc.sbuf_base + 31) // 32 * 32]

    def place(name, shape, dt=F32, over=None):
        size = int(np.prod(shape[1:])) * (2 if dt == BF16 else 4)
        size = (size + 31) // 32 * 32
        here = at if over is None else over
        t = nc.alloc_sbuf_tensor_at(name, shape, dt, offset=here[0])
        here[0] += size
        return t

    ident = place("ident", [P, P])
    ident_b = place("ident_b", [P, P], BF16)
    neg_mask = place("neg_mask", [P, 2 * P], BF16)
    head_mask = place("head_mask", [P, UH])
    head_mask_q = place("head_mask_q", [P, UH])
    lo_rows8 = place("lo_rows8", [P, UH])
    neg_lo_rows = place("neg_lo_rows", [P, 1])
    tri = place("tri", [P, NT, E, E])
    minus_half = place("minus_half", [P, TB])
    idx = place("idx", [P, NT], I32)
    gathered = place("gathered", [P, NT, NB])
    raw_b = place("raw_b", [P, 3, D])
    rows_b = place("rows_b", [P, 2, D])
    Bcr = place("Bcr", [P, D])
    wqkv = place("wqkv", [P, KD, 3 * D])
    wproj = place("wproj", [P, KD, D])
    BcT = place("BcT", [P, KD, NB])
    qkvb = place("qkvb", [P, 6, NB])
    KBexp = place("KBexp", [P, 2, UH, ROWS])
    QBpad = place("QBpad", [P, 2, P])
    Arep = place("Arep", [P, 2, P])
    VBexp = place("VBexp", [P, 2, 2 * UH * NB])
    M2 = place("M2", [P, D])
    M2c = place("M2c", [P, D])
    McT = place("McT", [P, KD, ZF])
    stat = place("stat", [P, 8])
    soft_e = place("soft_e", [P, TB, NB])
    soft_x = place("soft_x", [P, TB, NB])
    soft_s = place("soft_s", [P, 3, TB])
    CP = place("CP", [P, TB, P])
    cts_at = list(at)
    CTs = place("CTs", [P, SEQ])
    RQh = place("RQh", [P, SEQ], F32R, over=cts_at)
    sq = place("sq", [P, TB])
    rstd = place("rstd", [P, 2, TB])
    U = place("U", [P, TB, NB])
    KE = place("KE", [P, TB, ROWS])
    KE8 = place("KE8", [P, TB, UH, ROWS])
    KTs = place("KTs", [P, SEQ])
    Vst = [place(f"Vst{i}", [P, TB, 160]) for i in range(2)]
    RQ1 = [place(f"RQ1_{i}", [P, SEQ], F32R) for i in range(2)]
    RQ2 = [place(f"RQ2_{i}", [P, SEQ], F32R) for i in range(2)]
    maxp = [place(f"maxp{i}", [P, UH, 10]) for i in range(2)]
    nm = place("nm", [P, TB, UH])
    mexp = place("mexp", [P, TB, UH, ROWS])
    Zs = place("Zs", [P, SEQ])
    rec = place("rec", [P, TB, HEADS])
    Z = place("Z", [P, NT, P])
    ZTs = place("ZTs", [P, SEQ])
    sq2 = place("sq2", [P, TB])
    rstd2 = place("rstd2", [P, 2, TB])
    Zr = place("Zr", [P, TB, ZF])
    zab = place("zab", [P, TB, 2, P])
    ZAB = place("ZAB", [P, 2, NT * P], F32R)
    raw1 = place("raw1", [P, KD, HID])
    rawr = place("rawr", [P, KD, RHID])
    flo = place("flo", [ZF, HID], F32R)
    W1 = [place(f"W1_{i}", [P, 2, EB, P], F32R) for i in range(2)]
    WR = place("WR", [P, 2, RB, P], F32R)
    rW2p = place("rW2p", [P, RB, 32])
    b1r = place("b1r", [P, RB])
    b1e = place("b1e", [P, E, EB])
    rb2b = place("rb2b", [P, E])
    lo_at = [at[0] + EB * D * 4]
    W2 = [place("W2_0", [P, 2, EB, D], F32R)]
    raw2 = [place("raw2_0", [P, EB, D], over=lo_at)]
    L = place("L", [P, NT, E])
    Lx = place("Lx", [P, NT, E])
    Ls = place("Ls", [P, 2, NT])
    prob = place("prob", [P, NT, E])
    rank = place("rank", [P, NT, E])
    wgt = place("wgt", [P, NT, E])
    over_k, over_p = [at[0]], [at[0] + 2 * UH * SEQ * 4]
    UK = [place(f"UK{i}", [P, UH, SEQ], F32R) for i in range(2)]
    PQ = [place(f"PQ{i}", [P, 4, PT]) for i in range(2)]
    acc = place("acc", [P, NT, D], over=over_k)
    lo_at = [over_k[0] + EB * D * 4]
    W2.append(place("W2_1", [P, 2, EB, D], F32R, over=over_k))
    raw2.append(place("raw2_1", [P, EB, D], over=lo_at))
    rh = [place(f"rh{i}", [P, RB, SEQ], over=over_p) for i in range(2)]
    hbuf = [place(f"h{i}", [P, SEQ], over=over_p) for i in range(2)]
    hl = [place(f"hl{i}", [P, 2, SEQ], F32R, over=over_p) for i in range(3)]
    LG = place("LG", [P, SEQ], over=over_p)
    cmp_a = place("cmp_a", [P, NT, E, E], over=over_p)
    cmp_b = place("cmp_b", [P, NT, E, E], over=over_p)
    assert over_k[0] <= at[0] - 2 * 4 * PT * 4 and over_p[0] <= at[0]


    psS = nc.alloc_psum_tensor("psS", [P, 2, 512], F32)
    psT = nc.alloc_psum_tensor("psT", [P, 4, 512], F32)
    psV = nc.alloc_psum_tensor("psV", [P, 512], F32)
    psM = nc.alloc_psum_tensor("psM", [P, 512], F32)
    psM4 = psM[:, :].rearrange("p (t c) -> p t c", c=P)
    psM2 = psM[:, :].rearrange("p (t c) -> p t c", c=D)

    sem = lambda name: nc.alloc_semaphore(name)
    idx_in, bases_in, wqkv_in, wproj_in = sem("idx_in"), sem("bases_in"), sem("wqkv_in"), sem("wproj_in")
    rawr_in, raw1_in, raw2_in, small_in = sem("rawr_in"), sem("raw1_in"), sem("raw2_in"), sem("small_in")
    be2_in = sem("be2_in")
    rows_in = [sem(f"rows_in{b}") for b in range(BATCH)]
    consts = sem("consts")
    zeroed = sem("zeroed")
    dve_link = sem("dve_link")
    pool_link = sem("pool_link")
    bases_ready = sem("bases_ready")
    misc_written, misc_read = sem("misc_written"), sem("misc_read")
    logit_shift, base_exp, coeff_ready = sem("logit_shift"), sem("base_exp"), sem("coeff_ready")
    rstd_ready, ke_ready, vst_ready = sem("rstd_ready"), sem("ke_ready"), sem("vst_ready")
    keys_ready, qh_ready = sem("keys_ready"), sem("qh_ready")
    s_ready, max_done, mexp_ready = sem("s_ready"), sem("max_done"), sem("mexp_ready")
    t_ready, exp_done, mask_done, pv_done = sem("t_ready"), sem("exp_done"), sem("mask_done"), sem("pv_done")
    zs_done, rstd2_ready, zab_ready = sem("zs_done"), sem("rstd2_ready"), sem("zab_ready")
    hi_ready, lo_ready = sem("hi_ready"), sem("lo_ready")
    w1_filled = [sem(f"w1_filled{f}") for f in range(E + 1)]
    w2_hi, w2_lo = sem("w2_hi"), sem("w2_lo")
    up_ready, gelu_done, logits_ready, lg_done = sem("up_ready"), sem("gelu_done"), sem("logits_ready"), sem("lg_done")
    rl_ready, rexp_done, w_ready = sem("rl_ready"), sem("rexp_done"), sem("w_ready")
    split_done, down_done, comb_done = sem("split_done"), sem("down_done"), sem("comb_done")
    stored = sem("stored")

    N_UP_R = RB * BATCH
    fold_before = {("fold", f, ch): n for n, (_, f, ch) in enumerate(i for i in misc_at if i[0] == "fold")}

    with nc.Block() as block:

        @block.sync
        def _(sp):
            with nc.allow_non_contiguous_dma("token ids by tile; small vectors"):
                sp.dma_start(idx[:, :], x.rearrange("b (t p) -> p (b t)", p=P)).then_inc(idx_in, 16)
                for p0 in (0, 4 * HEADS):
                    sp.dma_start(raw_b[p0:p0 + NB, 0, :], base_w).then_inc(bases_in, 16)
                    sp.dma_start(raw_b[p0:p0 + NB, 1, :], lang_w).then_inc(bases_in, 16)
                    sp.dma_start(raw_b[p0:p0 + NB, 2, :],
                                 lang_w[LANG:LANG + 1, :].broadcast_to([NB, D])).then_inc(bases_in, 16)
                sp.dma_start(wqkv[:, :, :], w_qkv.rearrange("(k p) n -> p k n", p=P)).then_inc(wqkv_in, 16)
                sp.dma_start(wproj[:, :, :], w_proj.rearrange("(k p) n -> p k n", p=P)).then_inc(wproj_in, 16)
                sp.dma_start(rawr[:, :, :], rW1.rearrange("(k p) n -> p k n", p=P)).then_inc(rawr_in, 16)
                sp.dma_start(raw1[:, :, :], We1[0].rearrange("(k p) n -> p k n", p=P)).then_inc(raw1_in, 16)
                sp.wait_ge(zeroed, 2)
                sp.dma_start(M2[ZF:ZF + E, :], be2).then_inc(be2_in, 16)
                sp.dma_start(rW2p[:, :, 0:E], rW2.rearrange("(p b) n -> p b n", b=RB)).then_inc(small_in, 16)
                sp.dma_start(b1r[:, :], rb1.rearrange("(p b) -> p b", b=RB)).then_inc(small_in, 16)
                sp.dma_start(b1e[:, :, :], be1.rearrange("e (p b) -> p e b", b=EB)).then_inc(small_in, 16)
                sp.dma_start(rb2b[:, :], rb2.rearrange("(o n) -> o n", o=1).broadcast_to([P, E])).then_inc(small_in, 16)
                sp.dma_start(raw2[0][:, :, :], We2[0].rearrange("(p b) n -> p b n", b=EB)).then_inc(raw2_in, 16)
            for f in range(E + 1):
                e = f - 1
                dst = (WR if f == 0 else W1[e % 2])
                chunks = 1 if f == 0 else 2
                done = 1 + 2 * e if f else 0
                sp.wait_ge(lo_ready, done + chunks)
                width = chunks * 512
                d = dst[:, :, :, :].rearrange("p a b c -> p a (b c)").bitcast(F32)
                src = flo[:, 0:width].bitcast(F32)
                sp.dma_start(d[0:ZF, 1, :], d[0:ZF, 0, :]).then_inc(w1_filled[f], 16)
                sp.dma_start(d[ZF:ZR, 0, :], src[0:ZF // 2, :]).then_inc(w1_filled[f], 16)
                sp.dma_start(d[ZF:ZR, 1, :], src[ZF // 2:ZF, :]).then_inc(w1_filled[f], 16)
                if 1 <= f < E:
                    sp.dma_start(raw1[:, :, :], We1[e + 1].rearrange("(k p) n -> p k n", p=P)).then_inc(raw1_in, 16)
                    if e == 0:
                        sp.wait_ge(t_ready, 12 * UNITS)
                    else:
                        sp.wait_ge(down_done, BATCH * EB * e)
                    sp.dma_start(raw2[(e + 1) % 2][:, :, :], We2[e + 1].rearrange("(p b) n -> p b n", b=EB)).then_inc(raw2_in, 16)
            out_t = out.rearrange("b (t p) d -> b p t d", p=P)
            for c in range(BATCH):
                sp.wait_ge(comb_done, TB * ((E - 1) * BATCH + c + 1))
                sp.dma_start(out_t[c], acc[:, TB * c:TB * (c + 1), :]).then_inc(stored, 16)
            sp.wait_ge(stored, 16 * BATCH)

        @block.gpsimd
        def _(pool):
            links = [0]

            def link(ins):
                links[0] += 1
                ins.then_inc(pool_link, 1)
                pool.wait_ge(pool_link, links[0])

            pool.wait_ge(idx_in, 16)
            for b in range(BATCH):
                for t in range(TB * b, TB * (b + 1)):
                    pool.indirect_dma_start(gathered[:, t, :], None, coeff_w,
                                            bass.IndirectOffsetOnAxis(ap=idx[:, t:t + 1], axis=0)
                                            ).then_inc(rows_in[b], 16)
                if b:
                    continue
                g = nc.gpsimd
                link(g.memset(ident[:, :], 0.0))
                g.affine_select(out=ident[:, :], in_=ident[:, :], compare_op=ALU.not_equal, fill=1.0, base=0,
                                pattern=[[-1, P]], channel_multiplier=1).then_inc(consts, 1)
                link(g.memset(head_mask[:, :], 1.0))
                link(g.affine_select(out=head_mask[:, :], in_=head_mask[:, :], compare_op=ALU.is_ge, fill=0.0, base=0,
                                     pattern=[[-ROWS, UH]], channel_multiplier=1))
                g.affine_select(out=head_mask[:, :], in_=head_mask[:, :], compare_op=ALU.is_ge, fill=0.0,
                                base=ROWS - 1, pattern=[[ROWS, UH]], channel_multiplier=-1).then_inc(consts, 1)
                link(g.memset(lo_rows8[:, :], 1.0))
                link(g.affine_select(out=lo_rows8[:, :], in_=lo_rows8[:, :], compare_op=ALU.is_ge, fill=0.0,
                                     base=-2 * NB, pattern=[[-ROWS, UH]], channel_multiplier=1))
                g.affine_select(out=lo_rows8[:, :], in_=lo_rows8[:, :], compare_op=ALU.is_ge, fill=0.0,
                                base=3 * NB - 1, pattern=[[ROWS, UH]], channel_multiplier=-1).then_inc(consts, 1)
                link(g.memset(minus_half[:, :], -0.5))
                link(g.memset(ident_b[:, :], 0.0))
                link(g.affine_select(out=ident_b[:, :], in_=ident_b[:, :], compare_op=ALU.not_equal, fill=1.0, base=0,
                                     pattern=[[-1, P]], channel_multiplier=1))
                link(g.memset(neg_mask[:, :], 0.0))
                g.affine_select(out=neg_mask[:, :], in_=neg_mask[:, :], compare_op=ALU.is_ge, fill=NEG, base=0,
                                pattern=[[0, 2], [-1, P]], channel_multiplier=1).then_inc(consts, 1)
                link(g.memset(tri[:, :, :, :], 1.0))
                g.affine_select(out=tri[:, :, :, :], in_=tri[:, :, :, :], compare_op=ALU.is_ge, fill=0.0, base=-1,
                                pattern=[[0, NT], [1, E], [-1, E]], channel_multiplier=0).then_inc(consts, 1)

            def inverse_root(pair, src, scale):
                link(nc.gpsimd.tensor_scalar(pair[:, 0, :], src, scale, EPS, ALU.mult, ALU.add))
                return nc.gpsimd.tensor_tensor(pair[:, 1, :], pair[:, 0, :], minus_half[:, :], ALU.pow)

            for item in order:
                kind = item[0]
                if kind == "rstd":
                    b = item[1]
                    pool.wait_ge(misc_read, misc_at[("H", b, 1)] + 1)
                    if b:
                        pool.wait_ge(ke_ready, b)
                    inverse_root(rstd, sq[:, :], 1.0 / D).then_inc(rstd_ready, 1)
                elif kind == "rstd2":
                    b = item[1]
                    pool.wait_ge(misc_read, misc_at[("H2", b, 1)] + 1)
                    if b:
                        pool.wait_ge(zab_ready, b)
                    inverse_root(rstd2, sq2[:, :], 1.0 / D).then_inc(rstd2_ready, 1)
                elif kind == "variants":
                    b = item[1]
                    pool.wait_ge(misc_read, misc_at[("KT", b)] + 1)
                    if b >= 2:
                        pool.wait_ge(t_ready, 12 * 2 * (b - 1))
                    for h in range(UH):
                        nc.gpsimd.tensor_scalar(UK[b % 2][:, h, :], KTs[:, :], head_mask[:, h:h + 1], 1.0,
                                                ALU.mult, ALU.mult).then_inc(keys_ready, 1)
                elif kind == "T" and item[2] % 3:
                    _, u, k = item
                    q, j = 2 * u + k // 6, 2 * ((k % 6) // 3)
                    pool.wait_ge(exp_done, 12 * u + k + 1)
                    for kb in PV_ORDER[:3] if k % 3 == 1 else PV_ORDER[3:]:
                        d = PQ[q % 2][:, j:j + 2, KB_AT[kb][0]:KB_AT[kb][0] + P]
                        nc.gpsimd.affine_select(out=d, in_=d, compare_op=ALU.is_ge, fill=0.0, base=0,
                                                pattern=[[0, 2], [1, P]], channel_multiplier=-1
                                                ).then_inc(mask_done, 1)
                elif kind == "w2":
                    e = item[1]
                    pool.wait_ge(w2_hi, e + 1)
                    nc.gpsimd.tensor_tensor(W2[e % 2][:, 1, :, :], raw2[e % 2][:, :, :], W2[e % 2][:, 0, :, :].bitcast(F32),
                                            ALU.subtract).then_inc(w2_lo, 1)

        @block.tensor
        def _(pe):
            mm = nc.tensor.matmul

            def misc_begin(item):
                if misc_at[item]:
                    pe.wait_ge(misc_read, misc_at[item])

            def turn(src, rows, cols, n=TB):
                for t in range(n):
                    last = nc.tensor.transpose(psM[0:cols, P * t:P * t + rows], src(t), ident[0:rows, 0:rows])
                return last

            pe.wait_ge(consts, 1)
            for item in order:
                kind = item[0]
                if kind in MISC:
                    misc_begin(item)
                if kind == "BcT":
                    pe.wait_ge(bases_ready, 2)
                    for k in range(KD):
                        last = nc.tensor.transpose(psM[:, P * k:P * k + NB], Bcr[0:NB, P * k:P * (k + 1)],
                                                   ident[0:NB, 0:NB])
                    last.then_inc(misc_written, 1)
                elif kind == "QKV":
                    pe.wait_ge(wqkv_in, 16)
                    for j in range(6):
                        for k in range(KD):
                            last = mm(psM[:, NB * j:NB * j + NB], wqkv[:, k, P * j:P * (j + 1)], BcT[:, k, :],
                                      start=(k == 0), stop=(k == KD - 1))
                    last.then_inc(misc_written, 1)
                elif kind == "Arep":
                    pe.wait_ge(bases_ready, 3)
                    for g in range(2):
                        last = mm(psM4[:, g, :], QBpad[:, g, :], KBexp[:, g, :, :].rearrange("p h r -> p (h r)"),
                                  start=True, stop=True)
                    last.then_inc(misc_written, 1)
                elif kind == "M":
                    pe.wait_ge(wproj_in, 16)
                    pe.wait_ge(bases_ready, 4)
                    for g in range(2):
                        last = mm(psM[0:4 * HEADS, 0:D], VBexp[:, g, :], wproj[:, g, :], start=(g == 0), stop=(g == 1))
                    last.then_inc(misc_written, 1)
                elif kind == "McT":
                    pe.wait_ge(bases_ready, 5)
                    turn(lambda k: M2c[0:ZF, P * k:P * (k + 1)], ZF, P, KD).then_inc(misc_written, 1)
                elif kind == "fold":
                    _, f, ch = item
                    if f == 0:
                        pe.wait_ge(rawr_in, 16)
                        src = rawr
                    else:
                        pe.wait_ge(raw1_in, 16 * f)
                        src = raw1
                    for k in range(KD):
                        last = mm(psM[0:ZF, :], McT[:, k, :], src[:, k, 512 * ch:512 * (ch + 1)],
                                  start=(k == 0), stop=(k == KD - 1))
                    last.then_inc(misc_written, 1)
                elif kind == "CT":
                    pe.wait_ge(coeff_ready, item[1] + 1)
                    turn(lambda t: CP[:, t, :], P, P).then_inc(misc_written, 1)
                elif kind == "H":
                    for t in range(2):
                        c0 = P * (2 * item[2] + t)
                        last = mm(psM2[:, t, :], CTs[:, c0:c0 + P], Bcr[:, :], start=True, stop=True)
                    last.then_inc(misc_written, 1)
                elif kind == "KT":
                    pe.wait_ge(ke_ready, item[1] + 1)
                    turn(lambda t: KE8[:, t, :, :].rearrange("p h r -> p (h r)"), P, P).then_inc(misc_written, 1)
                elif kind == "QA":
                    mm(psM[:, :], Arep[:, item[2], :], KTs[:, :], start=True, stop=True).then_inc(misc_written, 1)
                elif kind == "shift":
                    pe.wait_ge(mexp_ready, item[1] + 1)
                    turn(lambda t: mexp[:, t, :, :].rearrange("p h r -> p (h r)"), P, P).then_inc(misc_written, 1)
                elif kind == "ZT":
                    pe.wait_ge(zs_done, item[1] + 1)
                    turn(lambda t: Zs[:, P * t:P * (t + 1)], P, P).then_inc(misc_written, 1)
                elif kind == "ZF":
                    turn(lambda t: Z[:, TB * item[1] + t, :], P, P).then_inc(misc_written, 1)
                elif kind in ("H2", "FH"):
                    pe.wait_ge(be2_in, 16)
                    for t in range(2):
                        c0 = P * (2 * item[2] + t)
                        last = mm(psM2[:, t, :], ZTs[:, c0:c0 + P], (M2c if kind == "H2" else M2)[:, :], start=True, stop=True)
                    last.then_inc(misc_written, 1)
                elif kind == "ZA":
                    if item[2] == 0:
                        pe.wait_ge(zab_ready, item[1] + 1)
                    turn(lambda t: zab[:, t, item[2], 0:ZR], P, ZR).then_inc(misc_written, 1)
                elif kind == "S":
                    _, u, k = item
                    b, g = u // 2, u % 2
                    n = 20 * u + k
                    if k == 0:
                        pe.wait_ge(misc_read, misc_at[("QA", b, g)] + 1)
                        if u == 0:
                            pe.wait_ge(consts, 4)
                    if n >= 2:
                        pe.wait_ge(max_done, n - 1)
                    ps = psS[:, n % 2, :]
                    h = 4 * (k // 10) + 2 * ((k % 10) // 5)
                    kk = k % 5
                    if g == 0:
                        pe.wait_ge(keys_ready, UH * b + min(h + 1 + kk // 2, h + 2))

                    def score(cols, head, qb, width, start):
                        mm(cols, RQ1[g][:, P * qb:P * (qb + 1)], UK[b % 2][:, head, 0:width], start=start, stop=False,
                           skip_group_check=True)
                    def diagonal(cols):
                        return mm(cols, ident_b[:, :], neg_mask[:, 0:P], start=False, stop=True, skip_group_check=True)

                    if kk in (0, 2):
                        score(ps, h + kk // 2, 3, 512, True)
                        last = diagonal(ps[:, 384:512])
                    elif kk in (1, 3):
                        score(ps[:, 0:256], h + kk // 2, 0, 256, True)
                        diagonal(ps[:, 0:128])
                        score(ps[:, 128:512], h + kk // 2, 2, 384, True)
                        last = diagonal(ps[:, 384:512])
                    else:
                        score(ps[:, 0:256], h, 1, 256, True)
                        score(ps[:, 256:512], h + 1, 1, 256, False)
                        ends = ps.rearrange("p (n c) -> p n c", c=P)[:, 1:4:2, :]
                        last = mm(ends, ident_b[:, :], neg_mask[:, :].rearrange("p (n c) -> p n c", c=P),
                                  start=False, stop=True, skip_group_check=True)
                    last.then_inc(s_ready, 1)
                elif kind == "T":
                    _, u, k = item
                    b, g = u // 2, u % 2
                    n = 12 * u + k
                    if k == 0:
                        pe.wait_ge(misc_read, misc_at[("shift", u)] + 1)
                    if n >= 2:
                        pe.wait_ge(exp_done, n - 1)
                    ps = psT[:, 2 * (n % 2):2 * (n % 2) + 2, :]
                    h = 4 * (k // 6) + 2 * ((k % 6) // 3)

                    def score(cols, head, kb, q0):
                        return mm(cols, UK[b % 2][:, head, P * kb:P * (kb + 1)], RQ2[g][:, q0:SEQ], start=True,
                                  stop=True, skip_group_check=True)
                    if k % 3 < 2:
                        h += k % 3
                        score(ps[:, 0, :], h, 0, 0)
                        score(ps[:, 1, 256:512], h, 3, 256)
                        last = score(ps[:, 1, 0:384], h, 1, 128)
                    else:
                        score(ps[:, 0, 0:256], h, 2, 256)
                        last = score(ps[:, 0, 256:512], h + 1, 2, 256)
                    last.then_inc(t_ready, 1)
                elif kind == "PV":
                    _, q, kb = item
                    b, r = q // 4, q % 4
                    n = PV_ORDER.index(kb)
                    pe.wait_ge(mask_done, 8 * q + 4 + n + 1)
                    if kb == 0:
                        pe.wait_ge(vst_ready, b + 1)
                        if r == 0 and b:
                            pe.wait_ge(zs_done, b)
                    c0, c1 = KB_AT[kb]
                    for j in range(4):
                        last = mm(psV[32 * j:32 * j + 32, P * kb:SEQ], Vst[b % 2][:, kb, 32 * r:32 * r + 32],
                                  PQ[q % 2][:, j, c0:c1], start=(r == 0 and kb == 0), stop=(r == 3 and n == 3),
                                  skip_group_check=True)
                    if n == 3:
                        last.then_inc(pv_done, 1)
                elif kind == "up":
                    i = item[1]
                    if i == 0:
                        pe.wait_ge(max_done, 20 * UNITS)
                    if i < N_UP_R:
                        c, b, w = i // RB, i % RB, WR
                        if b == 0:
                            pe.wait_ge(misc_read, misc_at[("ZA", c, 1)] + 1)
                        if i == 0:
                            pe.wait_ge(w1_filled[0], 48)
                    else:
                        j = i - N_UP_R
                        e, c, b = j // (BATCH * EB), j // EB % BATCH, j % EB
                        w = W1[e % 2]
                        if c == 0 and b == 0:
                            pe.wait_ge(w1_filled[e + 1], 48)
                    if i >= 2:
                        pe.wait_ge(gelu_done, i - 1)
                    for a in range(2):
                        last = mm(psS[:, i % 2, :], w[0:ZR, a, b, :], ZAB[0:ZR, a, SEQ * c:SEQ * (c + 1)],
                                  start=(a == 0), stop=(a == 1))
                    last.then_inc(up_ready, 1)
                elif kind == "logits":
                    c = item[1]
                    pe.wait_ge(gelu_done, RB * (c + 1))
                    if c == 0:
                        pe.wait_ge(small_in, 64)
                        pe.wait_ge(exp_done, 12 * UNITS)
                    for b in range(RB):
                        last = mm(psT[32 * b:32 * b + 32, c, :], rW2p[:, b, :], rh[c % 2][:, b, :], start=True, stop=True)
                    last.then_inc(logits_ready, 1)
                elif kind == "LT":
                    pe.wait_ge(lg_done, item[1] + 1)
                    turn(lambda t: LG[:, P * t:P * (t + 1)], P, P).then_inc(misc_written, 1)
                elif kind == "FZ":
                    pe.wait_ge(w_ready, 1)
                    turn(lambda t: Z[:, TB * item[1] + t, :], P, P).then_inc(misc_written, 1)
                elif kind == "down":
                    j = item[1]
                    e, ec, b = j // (BATCH * EB), j // EB, j % EB
                    pe.wait_ge(split_done, j + 1)
                    if b == 0:
                        if ec % BATCH == 0:
                            pe.wait_ge(w2_lo, e + 1)
                        if ec == 0:
                            pe.wait_ge(lg_done, BATCH)
                        if ec >= 2:
                            pe.wait_ge(comb_done, TB * (ec - 1))
                    hi, lo = hl[j % 3][:, 0, :], hl[j % 3][:, 1, :]
                    w = W2[e % 2]
                    for t in range(TB):
                        o = psT[:, 2 * (ec % 2) + t // 2, D * (t % 2):D * (t % 2 + 1)]
                        c0 = P * t
                        mm(o, hi[:, c0:c0 + P], w[:, 0, b, :], start=(b == 0 and t % 2 == 0), stop=False,
                           skip_group_check=True)
                        mm(o, hi[:, c0:c0 + P], w[:, 1, b, :], start=False, stop=False, skip_group_check=True)
                        last = mm(o, lo[:, c0:c0 + P], w[:, 0, b, :], start=False, stop=(b == EB - 1),
                                  skip_group_check=True)
                    last.then_inc(down_done, 1)

        @block.scalar
        def _(act):
            A = nc.scalar.activation

            def out_of_misc(item, dst, src):
                act.wait_ge(misc_written, misc_at[item] + 1)
                A(dst, src, ACT.Copy).then_inc(misc_read, 1)

            for item in order:
                kind = item[0]
                if kind == "soft":
                    act.wait_ge(logit_shift, item[1] + 1)
                    A(soft_x[:, :, :], soft_e[:, :, :], ACT.Exp).then_inc(base_exp, 1)
                elif kind == "CT":
                    out_of_misc(item, CTs[:, :], psM[:, :])
                elif kind == "H":
                    act.wait_ge(misc_written, misc_at[item] + 1)
                    if item[1] and item[2] == 0:
                        act.wait_ge(rstd_ready, item[1])
                    for t in range(2):
                        last = A(psM2[:, t, :], psM2[:, t, :], ACT.Square,
                                 accum_out=sq[:, 2 * item[2] + t:2 * item[2] + t + 1])
                    last.then_inc(misc_read, 1)
                elif kind == "KT":
                    if item[1]:
                        act.wait_ge(keys_ready, UH * item[1])
                    out_of_misc(item, KTs[:, :], psM[:, :])
                elif kind == "QA":
                    act.wait_ge(misc_written, misc_at[item] + 1)
                    A(RQh[:, :], psM[:, :], ACT.Copy).then_inc(qh_ready, 1)
                elif kind == "fold":
                    _, f, ch = item
                    n = fold_before[item]
                    act.wait_ge(misc_written, misc_at[item] + 1)
                    if f >= 3 and ch == 0:
                        act.wait_ge(up_ready, N_UP_R + BATCH * EB * (f - 2))
                    nb = RB if f == 0 else EB
                    dst = WR if f == 0 else W1[(f - 1) % 2]
                    np_ = 512 // nb
                    A(dst[0:ZF, 0, :, np_ * ch:np_ * (ch + 1)],
                      psM[0:ZF, :].rearrange("z (p b) -> z b p", b=nb), ACT.Copy).then_inc(hi_ready, 1)
                elif kind == "T":
                    _, u, k = item
                    n, q = 12 * u + k, 2 * u + k // 6
                    act.wait_ge(t_ready, n + 1)
                    if k % 6 == 0 and q >= 2:
                        act.wait_ge(pv_done, q - 1)
                    j = 2 * ((k % 6) // 3)
                    ps = psT[:, 2 * (n % 2):2 * (n % 2) + 2, :]
                    if k % 3 < 2:
                        A(PQ[q % 2][:, j + k % 3, 0:1024], ps.rearrange("p n c -> p (n c)"), ACT.Exp
                          ).then_inc(exp_done, 1)
                    else:
                        A(PQ[q % 2][:, j:j + 2, 1024:PT], ps[:, 0, :].rearrange("p (n c) -> p n c", c=256), ACT.Exp
                          ).then_inc(exp_done, 1)
                elif kind == "Zs":
                    b = item[1]
                    act.wait_ge(pv_done, 4 * (b + 1))
                    if b:
                        act.wait_ge(misc_written, misc_at[("ZT", b - 1)] + 1)
                    A(Zs[:, :], psV[:, :], ACT.Copy).then_inc(zs_done, 1)
                elif kind == "H2":
                    act.wait_ge(misc_written, misc_at[item] + 1)
                    if item[1] and item[2] == 0:
                        act.wait_ge(rstd2_ready, item[1])
                    for t in range(2):
                        last = A(psM2[:, t, :], psM2[:, t, :], ACT.Square,
                                 accum_out=sq2[:, 2 * item[2] + t:2 * item[2] + t + 1])
                    last.then_inc(misc_read, 1)
                elif kind in ("ZF", "FZ"):
                    out_of_misc(item, ZTs[:, :], psM[:, :])
                elif kind == "ZA":
                    out_of_misc(item, ZAB[0:ZR, item[2], SEQ * item[1]:SEQ * (item[1] + 1)], psM[0:ZR, :])
                elif kind == "FH":
                    t0 = TB * item[1] + 2 * item[2]
                    if item[1] == 0 and item[2] == 0:
                        act.wait_ge(t_ready, 12 * UNITS)
                    out_of_misc(item, acc[:, t0:t0 + 2, :], psM2[:, :, :])
                elif kind == "up":
                    i = item[1]
                    act.wait_ge(up_ready, i + 1)
                    if i == 0:
                        act.wait_ge(pv_done, 2 * UNITS)
                        act.wait_ge(small_in, 64)
                    if i < N_UP_R:
                        c, b = i // RB, i % RB
                        if c >= 2 and b == 0:
                            act.wait_ge(logits_ready, c - 1)
                        A(rh[c % 2][:, b, :], psS[:, i % 2, :], ACT.Gelu, bias=b1r[:, b:b + 1]).then_inc(gelu_done, 1)
                    else:
                        j = i - N_UP_R
                        e, b = j // (BATCH * EB), j % EB
                        if j >= 2:
                            act.wait_ge(split_done, j - 1)
                        A(hbuf[j % 2][:, :], psS[:, i % 2, :], ACT.Gelu, bias=b1e[:, e, b:b + 1]).then_inc(gelu_done, 1)
                elif kind == "route":
                    act.wait_ge(rl_ready, 1)
                    A(Lx[:, :, :], L[:, :, :], ACT.Exp).then_inc(rexp_done, 1)

        @block.vector
        def _(dve):
            v = nc.vector
            links = [0]

            def link(ins):
                links[0] += 1
                ins.then_inc(dve_link, 1)
                dve.wait_ge(dve_link, links[0])

            def bc(ap, shape):
                return ap.broadcast_to(shape)

            v.memset(M2[:, :], 0.0).then_inc(zeroed, 1)
            v.memset(rW2p[:, :, :], 0.0).then_inc(zeroed, 1)
            v.memset(Bcr[:, :], 0.0).then_inc(zeroed, 1)
            v.memset(CP[:, :, :], 0.0).then_inc(zeroed, 1)
            v.memset(KE[:, :, :], 0.0).then_inc(zeroed, 1)
            dve.wait_ge(zeroed, 5)
            dve.wait_ge(bases_in, 96)
            for p0 in (0, 4 * HEADS):
                r = slice(p0, p0 + NB)
                v.tensor_tensor(rows_b[r, 0, :], raw_b[r, 0, :], raw_b[r, 1, :], ALU.add)
                link(v.tensor_scalar(rows_b[r, 1, :], raw_b[r, 2, :], 0.1, None, ALU.mult))
                dst = M2[r, :] if p0 else Bcr[r, :]
                link(v.scalar_tensor_tensor(dst, rows_b[r, 0, :], SCALE_D, rows_b[r, 1, :], ALU.mult, ALU.add))

            def centre(dst, src, rows):
                link(v.tensor_reduce(stat[0:rows, 0:1], src, AX.X, ALU.add))
                link(v.tensor_scalar(stat[0:rows, 1:2], stat[0:rows, 0:1], 1.0 / D, None, ALU.mult))
                return v.tensor_scalar(dst, src, stat[0:rows, 1:2], None, ALU.subtract)

            centre(Bcr[0:NB, :], Bcr[0:NB, :], NB).then_inc(bases_ready, 1)
            dve.wait_ge(bases_ready, 1)
            v.memset(QBpad[:, :, :], 0.0).then_inc(bases_ready, 1)
            v.memset(M2c[:, :], 0.0)
            v.memset(KBexp[:, :, :, :], 0.0)
            v.memset(mexp[:, :, :, :], 0.0)
            v.memset(Z[:, :, :], 0.0)
            v.memset(Vst[0][:, :, :], 0.0)
            v.memset(Vst[1][:, :, :], 0.0)
            link(v.memset(KE[:, :, 3 * NB:3 * NB + 2], 1.0))
            for i in range(2):
                link(v.memset(Vst[i][:, :, :].rearrange("p t (r s) -> p t r s", s=40)[:, :, :, NB:NB + 1], 1.0))
            dve.wait_ge(consts, 3)
            link(v.tensor_scalar(head_mask_q[:, :], head_mask[:, :], DH ** -0.5, None, ALU.mult))
            link(v.tensor_reduce(neg_lo_rows[:, :], lo_rows8[:, :], AX.X, ALU.add, negate=True))

            def misc_wait(item):
                dve.wait_ge(misc_written, misc_at[item] + 1)

            for item in order:
                kind = item[0]
                if kind == "BcT":
                    misc_wait(item)
                    v.tensor_copy(BcT[:, :, :], psM[:, 0:2 * P].rearrange("p (k c) -> p k c", c=P)[:, :, 0:NB]
                                  ).then_inc(misc_read, 1)
                elif kind == "QKV":
                    misc_wait(item)
                    v.tensor_copy(qkvb[:, :, :], psM[:, 0:6 * NB].rearrange("p (j n) -> p j n", n=NB)
                                  ).then_inc(misc_read, 1)
                    dve.wait_ge(misc_read, misc_at[item] + 1)
                    for g in range(2):
                        v.tensor_copy(QBpad[:, g, 0:NB], qkvb[:, g, :])
                        v.tensor_copy(QBpad[:, g, NB:2 * NB], qkvb[:, g, :])
                        for part in range(3):
                            v.tensor_tensor(KBexp[:, g, :, NB * part:NB * (part + 1)],
                                            bc(qkvb[:, 2 + g, :].rearrange("p (o n) -> p o n", o=1), [P, UH, NB]),
                                            bc(head_mask_q[:, :].rearrange("p (h o) -> p h o", o=1), [P, UH, NB]),
                                            ALU.mult)
                    v.memset(VBexp[:, :, :], 0.0).then_inc(bases_ready, 1)
                    dve.wait_ge(bases_ready, 3)
                    for g in range(2):
                        last = v.tensor_tensor(
                            VBexp[:, g, 32 * g:32 * g + 32].rearrange("p (h n) -> p h n", n=NB),
                            bc(qkvb[:, 4 + g, :].rearrange("p (o n) -> p o n", o=1), [P, UH, NB]),
                            bc(head_mask[:, :].rearrange("p (h o) -> p h o", o=1), [P, UH, NB]), ALU.mult)
                    last.then_inc(bases_ready, 1)
                elif kind == "Arep":
                    misc_wait(item)
                    v.tensor_copy(Arep[:, :, :], psM4[:, 0:2, :]).then_inc(misc_read, 1)
                elif kind == "M":
                    misc_wait(item)
                    v.tensor_copy(M2[0:4 * HEADS, :], psM[0:4 * HEADS, 0:D]).then_inc(misc_read, 1)
                    dve.wait_ge(misc_read, misc_at[item] + 1)
                    centre(M2c[0:ZF, :], M2[0:ZF, :], ZF).then_inc(bases_ready, 1)
                elif kind == "McT":
                    misc_wait(item)
                    v.tensor_copy(McT[:, :, :], psM4[:, 0:KD, 0:ZF]).then_inc(misc_read, 1)
                elif kind == "fold":
                    _, f, ch = item
                    n = fold_before[item]
                    nb = RB if f == 0 else EB
                    np_ = 512 // nb
                    dst = WR if f == 0 else W1[(f - 1) % 2]
                    dve.wait_ge(hi_ready, n + 1)
                    if f >= 1 and ch == 0:
                        dve.wait_ge(w1_filled[f - 1], 48)
                    lo = flo[:, 0:512 * (1 if f == 0 else 2)].rearrange("z (b p) -> z b p", b=nb)
                    v.tensor_tensor(lo[:, :, np_ * ch:np_ * (ch + 1)],
                                    psM[0:ZF, :].rearrange("z (p b) -> z b p", b=nb),
                                    dst[0:ZF, 0, :, np_ * ch:np_ * (ch + 1)].bitcast(F32), ALU.subtract
                                    ).then_inc(misc_read, 1)
                    dve.wait_ge(misc_read, misc_at[item] + 1)
                    v.memset(stat[:, 4:5], 0.0).then_inc(lo_ready, 1)
                elif kind == "soft":
                    b = item[1]
                    g = gathered[:, TB * b:TB * (b + 1), :]
                    dve.wait_ge(rows_in[b], 16 * TB)
                    if b:
                        dve.wait_ge(base_exp, b)
                    link(v.tensor_reduce(soft_s[:, 0, :], g, AX.X, ALU.max))
                    v.tensor_tensor(soft_e[:, :, :], g, bc(soft_s[:, 0, :].rearrange("p (t o) -> p t o", o=1),
                                                          [P, TB, NB]), ALU.subtract).then_inc(logit_shift, 1)
                elif kind == "mix":
                    b = item[1]
                    dve.wait_ge(base_exp, b + 1)
                    link(v.tensor_reduce(soft_s[:, 1, :], soft_x[:, :, :], AX.X, ALU.add))
                    link(v.reciprocal(soft_s[:, 2, :], soft_s[:, 1, :]))
                    inv = bc(soft_s[:, 2, :].rearrange("p (t o) -> p t o", o=1), [P, TB, NB])
                    v.tensor_tensor(Z[:, TB * b:TB * (b + 1), 4 * HEADS:ZF], soft_x[:, :, :], inv, ALU.mult)
                    if b:
                        dve.wait_ge(misc_written, misc_at[("CT", b - 1)] + 1)
                    v.tensor_tensor(CP[:, :, 0:NB], soft_x[:, :, :], inv, ALU.mult).then_inc(coeff_ready, 1)
                elif kind == "keys":
                    b = item[1]
                    dve.wait_ge(rstd_ready, b + 1)
                    dve.wait_ge(coeff_ready, b + 1)
                    if b:
                        dve.wait_ge(vst_ready, b)
                    link(v.tensor_tensor(U[:, :, :], Z[:, TB * b:TB * (b + 1), 4 * HEADS:ZF],
                                         bc(rstd[:, 1, :].rearrange("p (t o) -> p t o", o=1), [P, TB, NB]), ALU.mult))
                    link(v.tensor_copy(KE[:, :, 0:NB].bitcast(F32R), U[:, :, :]))
                    v.tensor_tensor(KE[:, :, NB:2 * NB], U[:, :, :], KE[:, :, 0:NB], ALU.subtract)
                    link(v.tensor_copy(KE[:, :, 2 * NB:3 * NB], KE[:, :, 0:NB]))
                    if b:
                        dve.wait_ge(misc_written, misc_at[("KT", b - 1)] + 1)
                    v.tensor_copy(KE8[:, :, :, :],
                                  bc(KE[:, :, :].rearrange("p t (o r) -> p t o r", o=1), [P, TB, UH, ROWS])
                                  ).then_inc(ke_ready, 1)
                elif kind == "values":
                    b = item[1]
                    if b >= 2:
                        dve.wait_ge(pv_done, 4 * (b - 1))
                    v.tensor_copy(Vst[b % 2][:, :, :].rearrange("p t (r s) -> p t r s", s=40)[:, :, :, 0:NB],
                                  bc(U[:, :, :].rearrange("p t (o n) -> p t o n", o=1), [P, TB, 4, NB])
                                  ).then_inc(vst_ready, 1)
                elif kind == "QA":
                    b, g = item[1:]
                    u = 2 * b + g
                    dve.wait_ge(qh_ready, u + 1)
                    if u >= 2:
                        dve.wait_ge(s_ready, 20 * (u - 1))
                    v.scalar_tensor_tensor(RQ1[g][:, :], RQh[:, :].bitcast(F32), neg_lo_rows[:, :], psM[:, :],
                                           ALU.mult, ALU.add).then_inc(misc_read, 1)
                elif kind == "S":
                    _, u, k = item
                    n = 20 * u + k
                    h = 4 * (k // 10) + 2 * ((k % 10) // 5)
                    kk = k % 5
                    dve.wait_ge(s_ready, n + 1)
                    m = maxp[u % 2]
                    src = psS[:, n % 2, :].rearrange("p (n c) -> p n c", c=P)
                    if kk < 4:
                        dst = m[:, h + kk // 2, 4 * (kk % 2):4 * (kk % 2) + 4]
                    else:
                        dst = m[:, h:h + 2, 8:10]
                        src = psS[:, n % 2, :].rearrange("p (a n c) -> p a n c", a=2, c=P)
                    v.tensor_reduce(dst, src, AX.X, ALU.max).then_inc(max_done, 1)
                elif kind == "max":
                    u = item[1]
                    m = maxp[u % 2]
                    dve.wait_ge(max_done, 20 * (u + 1))
                    if u:
                        dve.wait_ge(mexp_ready, u)
                    for qb, (a, z) in enumerate([(4, 5), (8, 10), (5, 8), (0, 4)]):
                        last = v.tensor_reduce(nm[:, qb, :], m[:, :, a:z], AX.X, ALU.max, negate=True)
                    link(last)
                    if u:
                        dve.wait_ge(misc_written, misc_at[("shift", u - 1)] + 1)
                    hi = mexp[:, :, :, 3 * NB]
                    link(v.tensor_copy(hi.bitcast(F32R), nm[:, :, :]))
                    v.tensor_tensor(mexp[:, :, :, 3 * NB + 1], nm[:, :, :], hi, ALU.subtract).then_inc(mexp_ready, 1)
                elif kind == "shift":
                    u = item[1]
                    g = u % 2
                    misc_wait(item)
                    if u >= 2:
                        dve.wait_ge(t_ready, 12 * (u - 1))
                    v.tensor_tensor(RQ2[g][:, :], RQ1[g][:, :].bitcast(F32), psM[:, :], ALU.add
                                    ).then_inc(misc_read, 1)
                elif kind == "ZT":
                    b = item[1]
                    misc_wait(item)
                    link(v.reciprocal(rec[:, :, :], psM[:, :].rearrange("p (t h e) -> p t h e", t=TB, e=8)[:, :, :, NB]))
                    for t in range(TB):
                        last = v.tensor_tensor(
                            Z[:, TB * b + t, 0:4 * HEADS].rearrange("p (r j n) -> p j r n", j=4, n=NB),
                            psM4[:, t, :].rearrange("p (j r e) -> p j r e", j=4, e=8)[:, :, :, 0:NB],
                            bc(rec[:, t, :].rearrange("p (j r o) -> p j r o", j=4, o=1), [P, 4, 4, NB]), ALU.mult)
                    last.then_inc(misc_read, 1)
                elif kind == "zab":
                    b = item[1]
                    dve.wait_ge(rstd2_ready, b + 1)
                    link(v.tensor_tensor(Zr[:, :, :], Z[:, TB * b:TB * (b + 1), 0:ZF],
                                         bc(rstd2[:, 1, :].rearrange("p (t o) -> p t o", o=1), [P, TB, ZF]), ALU.mult))
                    if b:
                        dve.wait_ge(misc_written, misc_at[("ZA", b - 1, 1)] + 1)
                    half = ZF // 2
                    link(v.tensor_copy(zab[:, :, 0, 0:ZF].bitcast(F32R), Zr[:, :, :]))
                    v.tensor_copy(zab[:, :, 0, ZF:ZR], zab[:, :, 0, 0:half])
                    v.tensor_copy(zab[:, :, 1, ZF:ZR], zab[:, :, 0, half:ZF])
                    v.tensor_tensor(zab[:, :, 1, 0:ZF], Zr[:, :, :], zab[:, :, 0, 0:ZF], ALU.subtract
                                    ).then_inc(zab_ready, 1)
                elif kind == "w2":
                    e = item[1]
                    dve.wait_ge(raw2_in, 16 * (e + 1))
                    if e == 1:
                        dve.wait_ge(t_ready, 12 * UNITS)
                    if e >= 2:
                        dve.wait_ge(down_done, BATCH * EB * (e - 1))
                    v.tensor_copy(W2[e % 2][:, 0, :, :], raw2[e % 2][:, :, :]).then_inc(w2_hi, 1)
                elif kind == "logits":
                    c = item[1]
                    dve.wait_ge(logits_ready, c + 1)
                    if c:
                        dve.wait_ge(misc_written, misc_at[("LT", c - 1)] + 1)
                    v.tensor_copy(LG[:, :], psT[:, c, :]).then_inc(lg_done, 1)
                elif kind == "LT":
                    c = item[1]
                    misc_wait(item)
                    v.tensor_reduce(L[:, TB * c:TB * (c + 1), :],
                                    psM[:, :].rearrange("p (t b r) -> p t r b", t=TB, r=32)[:, :, 0:E, :],
                                    AX.X, ALU.add).then_inc(misc_read, 1)
                elif kind == "route":
                    dve.wait_ge(misc_read, misc_at[("LT", BATCH - 1)] + 1)
                    link(v.tensor_tensor(L[:, :, :], L[:, :, :],
                                         bc(rb2b[:, :].rearrange("p (o n) -> p o n", o=1), [P, NT, E]), ALU.add))
                    link(v.tensor_reduce(Ls[:, 0, :], L[:, :, :], AX.X, ALU.max))
                    v.tensor_tensor(L[:, :, :], L[:, :, :],
                                    bc(Ls[:, 0, :].rearrange("p (t o) -> p t o", o=1), [P, NT, E]), ALU.subtract
                                    ).then_inc(rl_ready, 1)
                    dve.wait_ge(rexp_done, 1)
                    link(v.tensor_reduce(Ls[:, 0, :], Lx[:, :, :], AX.X, ALU.add))
                    link(v.reciprocal(Ls[:, 1, :], Ls[:, 0, :]))
                    link(v.tensor_tensor(prob[:, :, :], Lx[:, :, :],
                                         bc(Ls[:, 1, :].rearrange("p (t o) -> p t o", o=1), [P, NT, E]), ALU.mult))
                    other = bc(prob[:, :, :].rearrange("p t (o j) -> p t o j", o=1), [P, NT, E, E])
                    own = bc(prob[:, :, :].rearrange("p t (e o) -> p t e o", o=1), [P, NT, E, E])
                    v.tensor_tensor(cmp_a[:, :, :, :], other, own, ALU.is_gt)
                    link(v.tensor_tensor(cmp_b[:, :, :, :], other, own, ALU.is_equal))
                    dve.wait_ge(consts, 5)
                    link(v.tensor_tensor(cmp_b[:, :, :, :], cmp_b[:, :, :, :], tri[:, :, :, :], ALU.mult))
                    link(v.tensor_tensor(cmp_a[:, :, :, :], cmp_a[:, :, :, :], cmp_b[:, :, :, :], ALU.add))
                    link(v.tensor_reduce(rank[:, :, :], cmp_a[:, :, :, :], AX.X, ALU.add))
                    link(v.tensor_scalar(rank[:, :, :], rank[:, :, :], 1.5, None, ALU.is_lt))
                    v.tensor_tensor(wgt[:, :, :], rank[:, :, :], prob[:, :, :], ALU.mult)
                    v.tensor_tensor(Z[:, :, ZF:ZF + E], rank[:, :, :], prob[:, :, :], ALU.mult).then_inc(w_ready, 1)
                elif kind == "split":
                    j = item[1]
                    dve.wait_ge(gelu_done, N_UP_R + j + 1)
                    if j >= 3:
                        dve.wait_ge(down_done, j - 2)
                    link(v.tensor_copy(hl[j % 3][:, 0, :], hbuf[j % 2][:, :]))
                    v.tensor_tensor(hl[j % 3][:, 1, :], hbuf[j % 2][:, :], hl[j % 3][:, 0, :].bitcast(F32), ALU.subtract
                                    ).then_inc(split_done, 1)
                elif kind == "combine":
                    ec = item[1]
                    e, c = ec // BATCH, ec % BATCH
                    dve.wait_ge(down_done, EB * (ec + 1))
                    if e == 0:
                        dve.wait_ge(misc_read, misc_at[("FH", c, 1)] + 1)
                        dve.wait_ge(w_ready, 1)
                    else:
                        dve.wait_ge(comb_done, TB * (ec - BATCH + 1))
                    for t in range(TB):
                        a = acc[:, TB * c + t, :]
                        o = psT[:, 2 * (ec % 2) + t // 2, D * (t % 2):D * (t % 2 + 1)]
                        v.scalar_tensor_tensor(a, o, wgt[:, TB * c + t, e:e + 1], a, ALU.mult, ALU.add
                                               ).then_inc(comb_done, 1)


_INS = ["x", "L0_tok_coeff_weight", "L0_tok_base_embed_weight", "L0_tok_lang_bias", "L0_attn_w_qkv", "L0_attn_w_proj",
        "L0_ffn_rW1", "L0_ffn_rb1", "L0_ffn_rW2", "L0_ffn_rb2", "L0_ffn_We1", "L0_ffn_be1", "L0_ffn_We2", "L0_ffn_be2"]


def kernel(**inputs):
    import concourse.bacc as bacc
    from concourse.bass_utils import run_bass_kernel_spmd

    nc = bacc.Bacc("TRN2", target_bir_lowering=False, num_devices=1)
    arrays, args = {}, []
    for name in _INS:
        a = np.ascontiguousarray(inputs[name])
        arrays[f"in_{name}"] = a
        args.append(nc.dram_tensor(f"in_{name}", a.shape, mybir.dt.from_np(a.dtype), kind="ExternalInput").ap())
    out = nc.dram_tensor("out", (BATCH, SEQ, D), F32, kind="ExternalOutput").ap()
    tower_kernel(nc, *args, out)
    r = run_bass_kernel_spmd(nc, [arrays], core_ids=[0])
    return r.results[0]["out"]
```

```python
import numpy as np
import concourse.bass as bass
from concourse import mybir

F32, F32R, BF16, I32 = mybir.dt.float32, mybir.dt.float32r, mybir.dt.bfloat16, mybir.dt.int32
ALU, ACT, AX = mybir.AluOpType, mybir.ActivationFunctionType, mybir.AxisListType

P = 128
BATCH, SEQ, D = 4, 512, 256
NB = 4
HEADS, DH = 16, 16
E, HID, RHID = 4, 1024, 512
TB = SEQ // P
NT = BATCH * TB
KD = D // P
UNITS = 2 * BATCH
UH = 8
ROWS = P // UH
ZF = 4 * HEADS + NB
ZR = ZF + ZF // 2
EB, RB = HID // P, RHID // P
PT = 1280
TURN = (E - 1, *range(E - 1))
XR = 2 * ZR + E
TS = 2 * P
TOK = NT * P
TILES = TOK // TS
MIN_TILES = 2
FAR = float(1 << 20)
EPS = 1e-5
SCALE_D, LANG = 16.0, 2
NEG = -1e30
PV_ORDER = (0, 1, 3, 2)

KB_AT = {0: (0, 512), 1: (512, 896), 2: (1024, 1280), 3: (896, 1024)}


AT = dict(M=0.28, McT=3.73, fold00=6.11, fold10=9.45, fold11=9.61, fold20=16.53, fold21=18.67, w20=30.63,
          soft=-38.28, mix=-35.84, CT=-32, H0=-30.02, H1=-27.11, rstd=-21.74, keys=-22.04, KT=-19.21,
          variants=-11.99, QA0=-6.82, QA1=-3.16, values=5.97, max=20.73, shift=23.02, T=26, PV=38, PVstep=2,
          Zs=74.38, ZT=73.74, ZF=81.8, H20=85.64, H21=86.62, rstd2=94.14, zab=93.62, ZA0=104.56, ZA1=102.44,
          up=201.84, upc=9, ups=1.95, logits=8.77, LT=11.26, ex=238.85, down=2.28, comb=5.23, route=3.17,
          FZ=5.28, w21=10.91, foldE=1.14, places=5, w2E=18.71)
AT1 = {('ZA1', 3): 100.71, ('rstd2', 0): 91.29, ('zab', 0): 93.94, ('ZA0', 0): 96.61, ('ZA1', 0): 98.85,
       ('QA1', 2): 6.06, ('CT', 3): -30.95, ('QA0', 2): -12.35, ('values', 2): 8.56, ('H0', 0): -25.44,
       ('H1', 0): -22.81, ('rstd', 0): -22.34, ('QA0', 3): -12.78, ('ZF', 0): 80.0, ('QA1', 0): 4.92,
       ('ZF', 1): 80.03, ('values', 1): 8.69, ('zab', 3): 93.43, ('H21', 1): 88.72, ('ZT', 2): 77.38,
       ('mix', 2): -35.41, ('H21', 3): 87.84, ('ZA0', 2): 98.4, ('mix', 0): -32.95, ('CT', 0): -29.95,
       ('ZA0', 3): 98.01, ('mix', 1): -34.29, ('QA1', 3): 6.25, ('ZT', 1): 77.09, ('H20', 2): 87.36,
       ('H21', 2): 88.24, ('rstd2', 2): 88.76, ('zab', 2): 94.64, ('keys', 2): -21.79, ('values', 3): 8.05,
       ('variants', 0): -15.22, ('H20', 1): 84.5, ('KT', 0): -17.49, ('rstd2', 3): 88.71, ('soft', 1): -37.48,
       ('H20', 3): 87.35, ('H1', 1): -29.94, ('mix', 3): -34.7, ('H0', 2): -29.14, ('rstd2', 1): 89.95,
       ('zab', 1): 94.95, ('ZA0', 1): 96.76, ('ZA1', 2): 105.78, ('soft', 0): -37.96, ('soft', 2): -38.0,
       ('keys', 0): -21.82, ('QA0', 0): -13.06, ('ZF', 3): 83.48, ('ZT', 0): 77.61, ('rstd', 2): -26.65,
       ('variants', 2): -15.32, ('variants', 3): -14.27, ('Zs', 3): 75.77, ('ZT', 3): 79.87, ('H0', 3): -27.12,
       ('H1', 3): -26.14, ('rstd', 3): -24.05, ('H20', 0): 85.69, ('CT', 2): -32.27, ('H21', 0): 88.9,
       ('soft', 3): -36.36, ('H0', 1): -30.32, ('rstd', 1): -27.33, ('keys', 1): -21.97, ('KT', 1): -19.14,
       ('variants', 1): -12.98, ('QA0', 1): -7.5, ('QA1', 1): 5.23, ('values', 0): 10.54, ('KT', 2): -19.5,
       ('Zs', 0): 74.64}


def step_order():
    at = []

    def put(when, *item):
        at.append((when, len(at), item))

    A = AT
    put(-60, "BcT"), put(-59, "QKV"), put(-58, "Arep")
    put(A["M"], "M"), put(A["McT"], "McT")
    for f, ch in ((0, 0), (1, 0), (1, 1), (2, 0), (2, 1)):
        put(A[f"fold{f}{ch}"], "fold", f, ch)
    put(A["w20"], "w2", 0)
    for b in range(BATCH):
        def a(name):
            return 40 * b + AT1.get((name, b), A[name])
        put(a("soft"), "soft", b), put(a("mix"), "mix", b), put(a("CT"), "CT", b)
        put(a("H0"), "H", b, 0), put(a("H1"), "H", b, 1), put(a("rstd"), "rstd", b)
        put(a("keys"), "keys", b), put(a("KT"), "KT", b)
        put(a("variants"), "variants", b)
        put(a("QA0"), "QA", b, 0)
        put(a("QA1"), "QA", b, 1)
        put(a("values"), "values", b)
        put(a("Zs"), "Zs", b), put(a("ZT"), "ZT", b), put(a("ZF"), "ZF", b), put(a("H20"), "H2", b, 0)
        put(a("H21"), "H2", b, 1), put(a("rstd2"), "rstd2", b), put(a("zab"), "zab", b)
        put(a("ZA0"), "ZA", b, 0), put(a("ZA1"), "ZA", b, 1)
    for u in range(UNITS):
        for k in range(20):
            put(20 * u + k, "S", u, k)
        put(20 * u + A["max"], "max", u)
        put(20 * u + A["shift"], "shift", u)
        for k in range(12):
            put(20 * u + A["T"] + k * 20 / 12, "T", u, k)
    for q in range(2 * UNITS):
        for n, kb in enumerate(PV_ORDER):
            put(10 * q + A["PV"] + A["PVstep"] * n, "PV", q, kb)

    for c in range(BATCH):
        for b in range(RB):
            put(A["up"] + A["upc"] * c + A["ups"] * b, "up", RB * c + b)
        put(A["up"] + A["upc"] * c + A["logits"], "logits", c), put(A["up"] + A["upc"] * c + A["LT"], "LT", c)
    t0, n = A["ex"], BATCH * EB
    for j in range(n):
        put(t0 + j, "up", RB * BATCH + j), put(t0 + j + 0.1, "split", j), put(t0 + j + A["down"], "down", j)
        if j % EB == EB - 1:
            put(t0 + j + A["comb"], "combine", j // EB)
    put(t0 + A["route"], "route"), put(t0 + A["places"], "places")
    for c in range(BATCH):
        for k, what in enumerate((("FZ", c), ("FH", c, 0), ("FH", c, 1))):
            put(t0 + 8 * c + A["FZ"] + k, *what)
    put(t0 + A["w21"], "w2", 1)
    return [item for _, _, item in sorted(at)]


MISC = ("BcT", "QKV", "Arep", "CT", "H", "KT", "QA", "M", "McT", "fold", "shift", "ZT", "ZF", "H2", "ZA",
        "LT", "FZ", "FH", "places")
LATE = (("fold", 3, 0), ("fold", 3, 1), ("fold", 4, 0), ("fold", 4, 1))


def tower_kernel(nc, x, coeff_w, base_w, lang_w, w_qkv, w_proj, rW1, rb1, rW2, rb2, We1, be1, We2, be2, out):
    order = step_order()
    misc_at = {item: n for n, item in enumerate([i for i in order if i[0] in MISC] + list(LATE))}

    at = [(nc.sbuf_base + 31) // 32 * 32]

    def place(name, shape, dt=F32, over=None):
        size = int(np.prod(shape[1:])) * (2 if dt == BF16 else 4)
        size = (size + 31) // 32 * 32
        here = at if over is None else over
        t = nc.alloc_sbuf_tensor_at(name, shape, dt, offset=here[0])
        here[0] += size
        return t

    ident = place("ident", [P, P])
    ident_b = place("ident_b", [P, P], BF16)
    neg_mask = place("neg_mask", [P, 2 * P], BF16)
    head_mask = place("head_mask", [P, UH])
    head_mask_q = place("head_mask_q", [P, UH])
    lo_rows8 = place("lo_rows8", [P, UH])
    neg_lo_rows = place("neg_lo_rows", [P, 1])
    tri = place("tri", [P, NT, E, E])
    below = place("below", [P, P])
    ones = place("ones", [P, P])
    region_far = place("region_far", [P, NT, E - 1])
    limits = place("limits", [1, E - 1, TILES - MIN_TILES])
    pad = place("pad", [P, 2, XR])
    no_id = place("no_id", [P, 2], I32)
    minus_half = place("minus_half", [P, TB])
    idx = place("idx", [P, NT], I32)
    gathered = place("gathered", [P, NT, NB])
    Bcr = place("Bcr", [P, D])
    rows_at, rows_at0 = list(at), at[0]
    raw_b = place("raw_b", [P, 3, D])
    rows_b = place("rows_b", [P, 2, D])
    wqkv = place("wqkv", [P, KD, 3 * D])
    wproj = place("wproj", [P, KD, D])
    rows_end = at[0]
    rows = place("rows", [P, NT, XR], over=rows_at)
    assert rows_at[0] <= rows_end
    BcT = place("BcT", [P, KD, NB])
    qkvb = place("qkvb", [P, 6, NB])
    KBexp = place("KBexp", [P, 2, UH, ROWS])
    QBpad = place("QBpad", [P, 2, P])
    Arep = place("Arep", [P, 2, P])
    VBexp = place("VBexp", [P, 2, 2 * UH * NB])
    M2 = place("M2", [P, D])
    M2c = place("M2c", [P, D])
    McT = place("McT", [P, KD, ZF])
    stat = place("stat", [P, 8])
    soft_e = place("soft_e", [P, TB, NB])
    soft_x = place("soft_x", [P, TB, NB])
    soft_s = place("soft_s", [P, 3, TB])
    dead_at = list(at)
    CP = place("CP", [P, TB, P])
    cts_at = list(at)
    CTs = place("CTs", [P, SEQ])
    RQh = place("RQh", [P, SEQ], F32R, over=cts_at)
    sq = place("sq", [P, TB])
    rstd = place("rstd", [P, 2, TB])
    U = place("U", [P, TB, NB])
    KE = place("KE", [P, TB, ROWS])
    KE8 = place("KE8", [P, TB, UH, ROWS])
    KTs = place("KTs", [P, SEQ])
    Vst = [place(f"Vst{i}", [P, TB, 160]) for i in range(2)]
    RQ1 = [place(f"RQ1_{i}", [P, SEQ], F32R) for i in range(2)]
    RQ2 = [place(f"RQ2_{i}", [P, SEQ], F32R) for i in range(2)]
    maxp = [place(f"maxp{i}", [P, UH, 10]) for i in range(2)]
    nm = place("nm", [P, TB, UH])
    mexp = place("mexp", [P, TB, UH, ROWS])
    Zs = place("Zs", [P, SEQ])
    rec = place("rec", [P, TB, HEADS])
    dead_end = at[0]
    Z = place("Z", [P, NT, P])
    ZTs = place("ZTs", [P, SEQ])
    sq2 = place("sq2", [P, TB])
    rstd2 = place("rstd2", [P, 2, TB])
    Zr = place("Zr", [P, TB, ZF])
    ZAB = place("ZAB", [P, 2, NT * P], F32R)
    raw1 = place("raw1", [P, KD, HID])
    rawr = place("rawr", [P, KD, RHID])
    flo = place("flo", [ZF, HID], F32R)
    W1 = [place(f"W1_{i}", [P, 2, EB, P], F32R) for i in range(2)]
    WR = place("WR", [P, 2, RB, P], F32R)
    rW2p = place("rW2p", [P, RB, 32])
    b1r = place("b1r", [P, RB])
    b1e = place("b1e", [P, E, EB])
    rb2b = place("rb2b", [P, E])
    lo_at = [at[0] + EB * D * 4]
    W2 = [place("W2_0", [P, 2, EB, D], F32R)]
    raw2 = [place("raw2_0", [P, EB, D], over=lo_at)]
    L = place("L", [P, NT, E])
    Lx = place("Lx", [P, NT, E])
    Ls = place("Ls", [P, 2, NT])
    prob = place("prob", [P, NT, E])
    rank = place("rank", [P, NT, E])
    wgt = place("wgt", [P, NT, E])
    over_k, over_p = [at[0]], [at[0] + 2 * UH * SEQ * 4]
    UK = [place(f"UK{i}", [P, UH, SEQ], F32R) for i in range(2)]
    PQ = [place(f"PQ{i}", [P, 4, PT]) for i in range(2)]
    acc = place("acc", [P, NT, D], over=over_k)
    lo_at = [over_k[0] + EB * D * 4]
    W2.append(place("W2_1", [P, 2, EB, D], F32R, over=over_k))
    raw2.append(place("raw2_1", [P, EB, D], over=lo_at))
    rh_at = list(over_p)
    rh = [place(f"rh{i}", [P, RB, SEQ], over=over_p) for i in range(2)]
    hbuf = [place(f"h{i}", [P, SEQ], over=over_p) for i in range(2)]
    hl = [place(f"hl{i}", [P, 2, SEQ], F32R, over=over_p) for i in range(3)]
    LG = place("LG", [P, SEQ], over=over_p)
    cmp_a = place("cmp_a", [P, NT, E, E], over=over_p)
    cmp_b = place("cmp_b", [P, NT, E, E], over=over_p)
    assert over_k[0] <= at[0] - 2 * 4 * PT * 4 and over_p[0] <= at[0]
    hs = place("hs", [P, EB, 2, TS], F32R, over=rh_at)
    xe = [nc.alloc_sbuf_tensor_at("xe0", [P, NT, XR], F32, offset=rows_at0), place("xe1", [P, NT, XR], over=dead_at)]
    tile_rows = [place(f"tile_rows{i}", [P, 2, 2 * ZR], over=dead_at) for i in range(2)]
    Xt = place("Xt", [P, 2, TS], F32R, over=dead_at)
    Yo = [place(f"Yo{i}", [P, 2, D], over=dead_at) for i in range(2)]
    scrap = place("scrap", [P, 2], over=dead_at)
    ids = place("ids", [P, 2], I32, over=dead_at)
    dest = place("dest", [P, NT, E - 1], over=dead_at)
    dest_s = place("dest_s", [P, 3, NT], over=dead_at)
    dest_i = place("dest_i", [P, 2, NT], I32, over=dead_at)
    more = place("more", [1, E - 1, TILES - MIN_TILES], over=dead_at)
    tiles_f = place("tiles_f", [1, E - 1], over=dead_at)
    last_i = place("last_i", [1, E - 1], I32, over=dead_at)
    assert dead_at[0] <= dead_end
    X = nc.dram_tensor("expert_rows", ((E - 1) * TOK, XR), F32, kind="Internal").ap()
    stream = nc.dram_tensor("stream", (TOK + TS, D), F32, kind="Internal").ap()

    psS = nc.alloc_psum_tensor("psS", [P, 2, 512], F32)
    psT = nc.alloc_psum_tensor("psT", [P, 4, 512], F32)
    psV = nc.alloc_psum_tensor("psV", [P, 512], F32)
    psM = nc.alloc_psum_tensor("psM", [P, 512], F32)
    psM4 = psM[:, :].rearrange("p (t c) -> p t c", c=P)
    psM2 = psM[:, :].rearrange("p (t c) -> p t c", c=D)

    sem = lambda name: nc.alloc_semaphore(name)
    idx_in, bases_in, wqkv_in, wproj_in = sem("idx_in"), sem("bases_in"), sem("wqkv_in"), sem("wproj_in")
    rawr_in, raw1_in, raw2_in, small_in = sem("rawr_in"), sem("raw1_in"), sem("raw2_in"), sem("small_in")
    be2_in, raw2_late = sem("be2_in"), sem("raw2_late")
    rows_in = [sem(f"rows_in{b}") for b in range(BATCH)]
    consts = sem("consts")
    zeroed = sem("zeroed")
    dve_link = sem("dve_link")
    pool_link = sem("pool_link")
    bases_ready = sem("bases_ready")
    misc_written, misc_read = sem("misc_written"), sem("misc_read")
    logit_shift, base_exp, coeff_ready = sem("logit_shift"), sem("base_exp"), sem("coeff_ready")
    rstd_ready, ke_ready, vst_ready = sem("rstd_ready"), sem("ke_ready"), sem("vst_ready")
    keys_ready, qh_ready = sem("keys_ready"), sem("qh_ready")
    s_ready, max_done, mexp_ready = sem("s_ready"), sem("max_done"), sem("mexp_ready")
    t_ready, exp_done, mask_done, pv_done = sem("t_ready"), sem("exp_done"), sem("mask_done"), sem("pv_done")
    zs_done, rstd2_ready, zab_ready = sem("zs_done"), sem("rstd2_ready"), sem("zab_ready")
    hi_ready, lo_ready = sem("hi_ready"), sem("lo_ready")
    w1_filled = [sem(f"w1_filled{f}") for f in range(E + 1)]
    w2_hi, w2_lo = sem("w2_hi"), sem("w2_lo")
    up_ready, gelu_done, logits_ready, lg_done = sem("up_ready"), sem("gelu_done"), sem("logits_ready"), sem("lg_done")
    rl_ready, rexp_done, w_ready = sem("rl_ready"), sem("rexp_done"), sem("w_ready")
    split_done, down_done, comb_done = sem("split_done"), sem("down_done"), sem("comb_done")
    places_ready, rows_ready, tiles_ready = sem("places_ready"), sem("rows_ready"), sem("tiles_ready")
    pads_in, scattered, stream_in = sem("pads_in"), sem("scattered"), sem("stream_in")
    of = lambda name: {e: sem(f"{name}{e}") for e in range(1, E)}
    x_in, xt_written, xt_read = of("x_in"), of("xt_written"), of("xt_read")
    s_up, s_gelu, s_split, s_down = of("s_up"), of("s_gelu"), of("s_split"), of("s_down")
    hi_done, tile_in = of("hi_done"), of("tile_in")
    y_free, id_ready, added = of("y_free"), of("id_ready"), of("added")
    stored = sem("stored")

    N_UP_R = RB * BATCH
    fold_before = {("fold", f, ch): n for n, (_, f, ch) in enumerate(i for i in misc_at if i[0] == "fold")}

    def tile_counts(eng):
        eng.wait_ge(tiles_ready, 1)
        last = {e: eng.value_load(last_i[0:1, e - 1:e], min_val=MIN_TILES - 1, max_val=TILES - 1) for e in range(1, E)}
        return last, {e: last[e] + 1 for e in last}

    def upto(tile, each, more=0):
        m, n = tile
        return m * each + (n * each + more)

    FIRST = (0, 0)

    with nc.Block() as block:

        @block.sync
        def _(sp):
            with nc.allow_non_contiguous_dma("token ids by tile; small vectors"):
                sp.dma_start(idx[:, :], x.rearrange("b (t p) -> p (b t)", p=P)).then_inc(idx_in, 16)
                for p0 in (0, 4 * HEADS):
                    sp.dma_start(raw_b[p0:p0 + NB, 0, :], base_w).then_inc(bases_in, 16)
                    sp.dma_start(raw_b[p0:p0 + NB, 1, :], lang_w).then_inc(bases_in, 16)
                    sp.dma_start(raw_b[p0:p0 + NB, 2, :],
                                 lang_w[LANG:LANG + 1, :].broadcast_to([NB, D])).then_inc(bases_in, 16)
                sp.dma_start(wqkv[:, :, :], w_qkv.rearrange("(k p) n -> p k n", p=P)).then_inc(wqkv_in, 16)
                sp.dma_start(wproj[:, :, :], w_proj.rearrange("(k p) n -> p k n", p=P)).then_inc(wproj_in, 16)
                sp.dma_start(rawr[:, :, :], rW1.rearrange("(k p) n -> p k n", p=P)).then_inc(rawr_in, 16)
                sp.dma_start(raw1[:, :, :], We1[TURN[0]].rearrange("(k p) n -> p k n", p=P)).then_inc(raw1_in, 16)
                sp.wait_ge(zeroed, 2)
                sp.dma_start(M2[ZF:ZF + E, :], be2).then_inc(be2_in, 16)
                sp.dma_start(rW2p[:, :, 0:E], rW2.rearrange("(p b) n -> p b n", b=RB)).then_inc(small_in, 16)
                sp.dma_start(b1r[:, :], rb1.rearrange("(p b) -> p b", b=RB)).then_inc(small_in, 16)
                sp.dma_start(b1e[:, :, :], be1.rearrange("e (p b) -> p e b", b=EB)).then_inc(small_in, 16)
                sp.dma_start(rb2b[:, :], rb2.rearrange("(o n) -> o n", o=1).broadcast_to([P, E])).then_inc(small_in, 16)
                sp.dma_start(raw2[0][:, :, :], We2[TURN[0]].rearrange("(p b) n -> p b n", b=EB)).then_inc(raw2_in, 16)
            def spread(f):
                dst = (WR if f == 0 else W1[(f - 1) % 2])
                chunks = 1 if f == 0 else 2
                done = 1 + 2 * (f - 1) if f else 0
                sp.wait_ge(lo_ready, done + chunks)
                d = dst[:, :, :, :].rearrange("p a b c -> p a (b c)").bitcast(F32)
                src = flo[:, 0:chunks * 512].bitcast(F32)
                sp.dma_start(d[0:ZF, 1, :], d[0:ZF, 0, :]).then_inc(w1_filled[f], 16)
                sp.dma_start(d[ZF:ZR, 0, :], src[0:ZF // 2, :]).then_inc(w1_filled[f], 16)
                sp.dma_start(d[ZF:ZR, 1, :], src[ZF // 2:ZF, :]).then_inc(w1_filled[f], 16)

            def load_raw1(e):
                sp.dma_start(raw1[:, :, :], We1[TURN[e]].rearrange("(k p) n -> p k n", p=P)).then_inc(raw1_in, 16)

            def load_raw2(e):
                sp.dma_start(raw2[e % 2][:, :, :], We2[TURN[e]].rearrange("(p b) n -> p b n", b=EB)).then_inc(raw2_in, 16)

            def load_rows(e):
                sp.dma_start(xe[e % 2][:, :, :], X[TOK * (e - 1):TOK * e, :].rearrange("(t p) c -> p t c", p=P)
                             ).then_inc(x_in[e], 16)

            spread(0)
            spread(1)
            load_raw1(1)
            spread(2)
            load_raw1(2)
            sp.wait_ge(consts, 6)
            for e in range(1, E):
                for k in range(2):
                    sp.dma_start(X[TOK * (e - 1):TOK * e, :].rearrange("(n s p) c -> p n s c", s=2, p=P)[:, :, k, :],
                                 pad[:, k:k + 1, :].broadcast_to([P, TILES, XR])).then_inc(pads_in, 16)
            sp.wait_ge(t_ready, 12 * UNITS)
            load_raw2(1)
            for c in range(BATCH):
                sp.wait_ge(comb_done, TB * (c + 1))
                sp.dma_start(stream[SEQ * c:SEQ * (c + 1), :].rearrange("(t p) d -> p t d", p=P),
                             acc[:, TB * c:TB * (c + 1), :]).then_inc(stream_in, 16)
                if c == 1:
                    sp.wait_ge(scattered, 16 * 2 * NT)
                    load_rows(1)
                    load_rows(2)
            last, tiles = tile_counts(sp)
            for e in range(1, E):
                sp.wait_ge(x_in[e], 16)
                sp.dma_start(tile_rows[e % 2][:, :, :], xe[e % 2][:, 0:2, 0:2 * ZR]).then_inc(tile_in[e], 16)
                with sp.Fori(0, last[e]) as m:
                    sp.wait_ge(xt_written[e], m + 1)
                    sp.dma_start(tile_rows[e % 2][:, :, :], xe[e % 2][:, bass.ds(2 * m + 2, 2), 0:2 * ZR]
                                 ).then_inc(tile_in[e], 16)
                if e < E - 1:
                    spread(e + 2)
                if e == 1:
                    load_raw1(3)
            sp.wait_ge(added[3], 16 + 32 * tiles[3])
            out_t = out.rearrange("b t d -> (b t) d")
            for c in range(BATCH):
                sp.dma_start(out_t[SEQ * c:SEQ * (c + 1), :], stream[SEQ * c:SEQ * (c + 1), :]).then_inc(stored, 16)
            sp.wait_ge(stored, 16 * BATCH)

        @block.gpsimd
        def _(pool):
            links = [0]

            def link(ins):
                links[0] += 1
                ins.then_inc(pool_link, 1)
                pool.wait_ge(pool_link, links[0])

            pool.wait_ge(idx_in, 16)
            for b in range(BATCH):
                for t in range(TB * b, TB * (b + 1)):
                    pool.indirect_dma_start(gathered[:, t, :], None, coeff_w,
                                            bass.IndirectOffsetOnAxis(ap=idx[:, t:t + 1], axis=0)
                                            ).then_inc(rows_in[b], 16)
                if b:
                    continue
                g = nc.gpsimd
                link(g.memset(ident[:, :], 0.0))
                g.affine_select(out=ident[:, :], in_=ident[:, :], compare_op=ALU.not_equal, fill=1.0, base=0,
                                pattern=[[-1, P]], channel_multiplier=1).then_inc(consts, 1)
                link(g.memset(head_mask[:, :], 1.0))
                link(g.affine_select(out=head_mask[:, :], in_=head_mask[:, :], compare_op=ALU.is_ge, fill=0.0, base=0,
                                     pattern=[[-ROWS, UH]], channel_multiplier=1))
                g.affine_select(out=head_mask[:, :], in_=head_mask[:, :], compare_op=ALU.is_ge, fill=0.0,
                                base=ROWS - 1, pattern=[[ROWS, UH]], channel_multiplier=-1).then_inc(consts, 1)
                link(g.memset(lo_rows8[:, :], 1.0))
                link(g.affine_select(out=lo_rows8[:, :], in_=lo_rows8[:, :], compare_op=ALU.is_ge, fill=0.0,
                                     base=-2 * NB, pattern=[[-ROWS, UH]], channel_multiplier=1))
                g.affine_select(out=lo_rows8[:, :], in_=lo_rows8[:, :], compare_op=ALU.is_ge, fill=0.0,
                                base=3 * NB - 1, pattern=[[ROWS, UH]], channel_multiplier=-1).then_inc(consts, 1)
                link(g.memset(minus_half[:, :], -0.5))
                link(g.memset(ident_b[:, :], 0.0))
                link(g.affine_select(out=ident_b[:, :], in_=ident_b[:, :], compare_op=ALU.not_equal, fill=1.0, base=0,
                                     pattern=[[-1, P]], channel_multiplier=1))
                link(g.memset(neg_mask[:, :], 0.0))
                g.affine_select(out=neg_mask[:, :], in_=neg_mask[:, :], compare_op=ALU.is_ge, fill=NEG, base=0,
                                pattern=[[0, 2], [-1, P]], channel_multiplier=1).then_inc(consts, 1)
                link(g.memset(tri[:, :, :, :], 1.0))
                g.affine_select(out=tri[:, :, :, :], in_=tri[:, :, :, :], compare_op=ALU.is_ge, fill=0.0, base=-1,
                                pattern=[[0, NT], [1, E], [-1, E]], channel_multiplier=0).then_inc(consts, 1)
                g.memset(ones[:, :], 1.0)
                link(g.memset(below[:, :], 1.0))
                g.affine_select(out=below[:, :], in_=below[:, :], compare_op=ALU.is_ge, fill=0.0, base=-1,
                                pattern=[[1, P]], channel_multiplier=-1)
                for e in range(1, E):
                    g.memset(region_far[:, :, e - 1:e], FAR + TOK * (e - 1))
                for m in range(MIN_TILES, TILES):
                    g.memset(limits[:, :, m - MIN_TILES:m - MIN_TILES + 1], float(TS * m))
                g.memset(no_id[:, :], 0)
                link(g.memset(pad[:, :, :], 0.0))
                g.iota(pad[:, :, 2 * ZR:2 * ZR + 1].bitcast(I32), pattern=[[P, 2], [0, 1]], base=TOK, channel_multiplier=1
                       ).then_inc(consts, 1)

            def inverse_root(pair, src, scale):
                link(nc.gpsimd.tensor_scalar(pair[:, 0, :], src, scale, EPS, ALU.mult, ALU.add))
                return nc.gpsimd.tensor_tensor(pair[:, 1, :], pair[:, 0, :], minus_half[:, :], ALU.pow)

            for item in order:
                kind = item[0]
                if kind == "rstd":
                    b = item[1]
                    pool.wait_ge(misc_read, misc_at[("H", b, 1)] + 1)
                    if b:
                        pool.wait_ge(ke_ready, b)
                    inverse_root(rstd, sq[:, :], 1.0 / D).then_inc(rstd_ready, 1)
                elif kind == "rstd2":
                    b = item[1]
                    pool.wait_ge(misc_read, misc_at[("H2", b, 1)] + 1)
                    if b:
                        pool.wait_ge(zab_ready, b)
                    inverse_root(rstd2, sq2[:, :], 1.0 / D).then_inc(rstd2_ready, 1)
                elif kind == "variants":
                    b = item[1]
                    pool.wait_ge(misc_read, misc_at[("KT", b)] + 1)
                    if b >= 2:
                        pool.wait_ge(t_ready, 12 * 2 * (b - 1))
                    for h in range(UH):
                        nc.gpsimd.tensor_scalar(UK[b % 2][:, h, :], KTs[:, :], head_mask[:, h:h + 1], 1.0,
                                                ALU.mult, ALU.mult).then_inc(keys_ready, 1)
                elif kind == "T" and item[2] % 3:
                    _, u, k = item
                    q, j = 2 * u + k // 6, 2 * ((k % 6) // 3)
                    pool.wait_ge(exp_done, 12 * u + k + 1)
                    for kb in PV_ORDER[:3] if k % 3 == 1 else PV_ORDER[3:]:
                        d = PQ[q % 2][:, j:j + 2, KB_AT[kb][0]:KB_AT[kb][0] + P]
                        nc.gpsimd.affine_select(out=d, in_=d, compare_op=ALU.is_ge, fill=0.0, base=0,
                                                pattern=[[0, 2], [1, P]], channel_multiplier=-1
                                                ).then_inc(mask_done, 1)
                elif kind == "places":
                    pool.wait_ge(w_ready, 1)
                    nc.gpsimd.iota(rows[:, :, 2 * ZR:2 * ZR + 1].bitcast(I32), pattern=[[P, NT], [0, 1]], base=0,
                                   channel_multiplier=1).then_inc(rows_ready, 1)
                    pool.wait_ge(rows_ready, 1)
                    pool.wait_ge(places_ready, 1)
                    pool.wait_ge(pads_in, 16 * 2 * (E - 1))
                    for t in range(NT):
                        for k in range(2):
                            pool.indirect_dma_start(X, bass.IndirectOffsetOnAxis(ap=dest_i[:, k, t:t + 1], axis=0),
                                                    rows[:, t, :], None, bounds_check=(E - 1) * TOK - 1,
                                                    oob_is_err=False).then_inc(scattered, 16)
                elif kind == "w2":
                    e = item[1]
                    pool.wait_ge(w2_hi, e + 1)
                    nc.gpsimd.tensor_tensor(W2[e % 2][:, 1, :, :], raw2[e % 2][:, :, :], W2[e % 2][:, 0, :, :].bitcast(F32),
                                            ALU.subtract).then_inc(w2_lo, 1)

            last, tiles = tile_counts(pool)
            for e, (c0, c1) in enumerate(((0, 64), (64, 128), (128, D)), 1):
                pool.dma_start(stream[TOK:TOK + TS, c0:c1].rearrange("(s p) c -> p s c", p=P), pad[:, :, 0:c1 - c0]
                               ).then_inc(added[e], 16)
            for e in range(1, E):
                pool.wait_ge(added[e], 16)
            pool.wait_ge(stream_in, 16 * BATCH)

            def add_tile(e, m):
                pool.wait_ge(y_free[e], m + 3)
                nc.gpsimd.tensor_tensor(ids[:, :], xe[e % 2][:, bass.ds(2 * m, 2), 2 * ZR].bitcast(I32), no_id[:, :],
                                        ALU.add).then_inc(id_ready[e], 1)
                pool.wait_ge(id_ready[e], m + 1)
                for k in range(2):
                    pool.indirect_dma_start(stream, bass.IndirectOffsetOnAxis(ap=ids[:, k:k + 1], axis=0), Yo[e % 2][:, k, :],
                                            None, bounds_check=m + (TOK + TS - 1), compute_op=ALU.add
                                            ).then_inc(added[e], 16)

            for e in range(1, E):
                if e > 1:
                    pool.wait_ge(added[e - 1], 16 + 32 * tiles[e - 1])
                    link(nc.gpsimd.tensor_tensor(ids[:, :], no_id[:, :], no_id[:, :], ALU.add))
                if e < E - 1:
                    if e == 1:
                        pool.wait_ge(down_done, BATCH * EB)
                    i = (e + 1) % 2
                    pool.dma_start(raw2[i][:, :, :], We2[TURN[e + 1]].rearrange("(p b) n -> p b n", b=EB)).then_inc(raw2_late, 16)
                    if e == 2:
                        pool.dma_start(xe[1][:, :, :], X[TOK * e:TOK * (e + 1), :].rearrange("(t p) c -> p t c", p=P)
                                       ).then_inc(x_in[3], 16)
                    pool.wait_ge(raw2_late, 16 * e)
                    nc.gpsimd.tensor_copy(W2[i][:, 0, :, :], raw2[i][:, :, :]).then_inc(w2_hi, 1)
                    pool.wait_ge(w2_hi, e + 2)
                    nc.gpsimd.tensor_tensor(W2[i][:, 1, :, :], raw2[i][:, :, :], W2[i][:, 0, :, :].bitcast(F32),
                                            ALU.subtract).then_inc(w2_lo, 1)
                with pool.Fori(0, tiles[e]) as m:
                    add_tile(e, m)

        @block.tensor
        def _(pe):
            mm = nc.tensor.matmul

            def misc_begin(item):
                if misc_at[item]:
                    pe.wait_ge(misc_read, misc_at[item])

            def turn(src, rows, cols, n=TB):
                for t in range(n):
                    last = nc.tensor.transpose(psM[0:cols, P * t:P * t + rows], src(t), ident[0:rows, 0:rows])
                return last

            def fold(item):
                _, f, ch = item
                if f == 0:
                    pe.wait_ge(rawr_in, 16)
                    src = rawr
                else:
                    pe.wait_ge(raw1_in, 16 * f)
                    src = raw1
                for k in range(KD):
                    last = mm(psM[0:ZF, :], McT[:, k, :], src[:, k, 512 * ch:512 * (ch + 1)],
                              start=(k == 0), stop=(k == KD - 1))
                last.then_inc(misc_written, 1)

            pe.wait_ge(consts, 1)
            for item in order:
                kind = item[0]
                if kind in MISC:
                    misc_begin(item)
                if kind == "BcT":
                    pe.wait_ge(bases_ready, 2)
                    for k in range(KD):
                        last = nc.tensor.transpose(psM[:, P * k:P * k + NB], Bcr[0:NB, P * k:P * (k + 1)],
                                                   ident[0:NB, 0:NB])
                    last.then_inc(misc_written, 1)
                elif kind == "QKV":
                    pe.wait_ge(wqkv_in, 16)
                    for j in range(6):
                        for k in range(KD):
                            last = mm(psM[:, NB * j:NB * j + NB], wqkv[:, k, P * j:P * (j + 1)], BcT[:, k, :],
                                      start=(k == 0), stop=(k == KD - 1))
                    last.then_inc(misc_written, 1)
                elif kind == "Arep":
                    pe.wait_ge(bases_ready, 3)
                    for g in range(2):
                        last = mm(psM4[:, g, :], QBpad[:, g, :], KBexp[:, g, :, :].rearrange("p h r -> p (h r)"),
                                  start=True, stop=True)
                    last.then_inc(misc_written, 1)
                elif kind == "M":
                    pe.wait_ge(wproj_in, 16)
                    pe.wait_ge(bases_ready, 4)
                    for g in range(2):
                        last = mm(psM[0:4 * HEADS, 0:D], VBexp[:, g, :], wproj[:, g, :], start=(g == 0), stop=(g == 1))
                    last.then_inc(misc_written, 1)
                elif kind == "McT":
                    pe.wait_ge(bases_ready, 5)
                    turn(lambda k: M2c[0:ZF, P * k:P * (k + 1)], ZF, P, KD).then_inc(misc_written, 1)
                elif kind == "fold":
                    fold(item)
                elif kind == "places":
                    pe.wait_ge(w_ready, 1)
                    pe.wait_ge(consts, 6)
                    mm(psM[:, 0:NT * E], below[:, :], rank[:, :, :].rearrange("p t e -> p (t e)"), start=True, stop=False,
                       skip_group_check=True)
                    for t in range(NT):
                        last = mm(psM[:, E * (t + 1):E * (NT + 1)].rearrange("p (t e) -> p t e", e=E), ones[:, :],
                                  rank[:, t:t + 1, :].broadcast_to([P, NT - t, E]), start=False, stop=(t == NT - 1),
                                  skip_group_check=True)
                    last.then_inc(misc_written, 1)
                elif kind == "CT":
                    pe.wait_ge(coeff_ready, item[1] + 1)
                    turn(lambda t: CP[:, t, :], P, P).then_inc(misc_written, 1)
                elif kind == "H":
                    for t in range(2):
                        c0 = P * (2 * item[2] + t)
                        last = mm(psM2[:, t, :], CTs[:, c0:c0 + P], Bcr[:, :], start=True, stop=True)
                    last.then_inc(misc_written, 1)
                elif kind == "KT":
                    pe.wait_ge(ke_ready, item[1] + 1)
                    turn(lambda t: KE8[:, t, :, :].rearrange("p h r -> p (h r)"), P, P).then_inc(misc_written, 1)
                elif kind == "QA":
                    mm(psM[:, :], Arep[:, item[2], :], KTs[:, :], start=True, stop=True).then_inc(misc_written, 1)
                elif kind == "shift":
                    pe.wait_ge(mexp_ready, item[1] + 1)
                    turn(lambda t: mexp[:, t, :, :].rearrange("p h r -> p (h r)"), P, P).then_inc(misc_written, 1)
                elif kind == "ZT":
                    pe.wait_ge(zs_done, item[1] + 1)
                    turn(lambda t: Zs[:, P * t:P * (t + 1)], P, P).then_inc(misc_written, 1)
                elif kind == "ZF":
                    turn(lambda t: Z[:, TB * item[1] + t, :], P, P).then_inc(misc_written, 1)
                elif kind in ("H2", "FH"):
                    pe.wait_ge(be2_in, 16)
                    for t in range(2):
                        c0 = P * (2 * item[2] + t)
                        last = mm(psM2[:, t, :], ZTs[:, c0:c0 + P], (M2c if kind == "H2" else M2)[:, :], start=True, stop=True)
                    last.then_inc(misc_written, 1)
                elif kind == "ZA":
                    if item[2] == 0:
                        pe.wait_ge(zab_ready, item[1] + 1)
                    turn(lambda t: rows[:, TB * item[1] + t, ZR * item[2]:ZR * (item[2] + 1)], P, ZR).then_inc(misc_written, 1)
                elif kind == "S":
                    _, u, k = item
                    b, g = u // 2, u % 2
                    n = 20 * u + k
                    if k == 0:
                        pe.wait_ge(misc_read, misc_at[("QA", b, g)] + 1)
                        if u == 0:
                            pe.wait_ge(consts, 4)
                    if n >= 2:
                        pe.wait_ge(max_done, n - 1)
                    ps = psS[:, n % 2, :]
                    h = 4 * (k // 10) + 2 * ((k % 10) // 5)
                    kk = k % 5
                    if g == 0:
                        pe.wait_ge(keys_ready, UH * b + min(h + 1 + kk // 2, h + 2))

                    def score(cols, head, qb, width, start):
                        mm(cols, RQ1[g][:, P * qb:P * (qb + 1)], UK[b % 2][:, head, 0:width], start=start, stop=False,
                           skip_group_check=True)
                    def diagonal(cols):
                        return mm(cols, ident_b[:, :], neg_mask[:, 0:P], start=False, stop=True, skip_group_check=True)

                    if kk in (0, 2):
                        score(ps, h + kk // 2, 3, 512, True)
                        last = diagonal(ps[:, 384:512])
                    elif kk in (1, 3):
                        score(ps[:, 0:256], h + kk // 2, 0, 256, True)
                        diagonal(ps[:, 0:128])
                        score(ps[:, 128:512], h + kk // 2, 2, 384, True)
                        last = diagonal(ps[:, 384:512])
                    else:
                        score(ps[:, 0:256], h, 1, 256, True)
                        score(ps[:, 256:512], h + 1, 1, 256, False)
                        ends = ps.rearrange("p (n c) -> p n c", c=P)[:, 1:4:2, :]
                        last = mm(ends, ident_b[:, :], neg_mask[:, :].rearrange("p (n c) -> p n c", c=P),
                                  start=False, stop=True, skip_group_check=True)
                    last.then_inc(s_ready, 1)
                elif kind == "T":
                    _, u, k = item
                    b, g = u // 2, u % 2
                    n = 12 * u + k
                    if k == 0:
                        pe.wait_ge(misc_read, misc_at[("shift", u)] + 1)
                    if n >= 2:
                        pe.wait_ge(exp_done, n - 1)
                    ps = psT[:, 2 * (n % 2):2 * (n % 2) + 2, :]
                    h = 4 * (k // 6) + 2 * ((k % 6) // 3)

                    def score(cols, head, kb, q0):
                        return mm(cols, UK[b % 2][:, head, P * kb:P * (kb + 1)], RQ2[g][:, q0:SEQ], start=True,
                                  stop=True, skip_group_check=True)
                    if k % 3 < 2:
                        h += k % 3
                        score(ps[:, 0, :], h, 0, 0)
                        score(ps[:, 1, 256:512], h, 3, 256)
                        last = score(ps[:, 1, 0:384], h, 1, 128)
                    else:
                        score(ps[:, 0, 0:256], h, 2, 256)
                        last = score(ps[:, 0, 256:512], h + 1, 2, 256)
                    last.then_inc(t_ready, 1)
                elif kind == "PV":
                    _, q, kb = item
                    b, r = q // 4, q % 4
                    n = PV_ORDER.index(kb)
                    pe.wait_ge(mask_done, 8 * q + 4 + n + 1)
                    if kb == 0:
                        pe.wait_ge(vst_ready, b + 1)
                        if r == 0 and b:
                            pe.wait_ge(zs_done, b)
                    c0, c1 = KB_AT[kb]
                    for j in range(4):
                        last = mm(psV[32 * j:32 * j + 32, P * kb:SEQ], Vst[b % 2][:, kb, 32 * r:32 * r + 32],
                                  PQ[q % 2][:, j, c0:c1], start=(r == 0 and kb == 0), stop=(r == 3 and n == 3),
                                  skip_group_check=True)
                    if n == 3:
                        last.then_inc(pv_done, 1)
                elif kind == "up":
                    i = item[1]
                    if i == 0:
                        pe.wait_ge(max_done, 20 * UNITS)
                    if i < N_UP_R:
                        c, b, w = i // RB, i % RB, WR
                        if b == 0:
                            pe.wait_ge(misc_read, misc_at[("ZA", c, 1)] + 1)
                        if i == 0:
                            pe.wait_ge(w1_filled[0], 48)
                    else:
                        j = i - N_UP_R
                        e, c, b = j // (BATCH * EB), j // EB % BATCH, j % EB
                        w = W1[e % 2]
                        if c == 0 and b == 0:
                            pe.wait_ge(w1_filled[e + 1], 48)
                    if i >= 2:
                        pe.wait_ge(gelu_done, i - 1)
                    for a in range(2):
                        last = mm(psS[:, i % 2, :], w[0:ZR, a, b, :], ZAB[0:ZR, a, SEQ * c:SEQ * (c + 1)],
                                  start=(a == 0), stop=(a == 1))
                    last.then_inc(up_ready, 1)
                elif kind == "logits":
                    c = item[1]
                    pe.wait_ge(gelu_done, RB * (c + 1))
                    if c == 0:
                        pe.wait_ge(small_in, 64)
                        pe.wait_ge(exp_done, 12 * UNITS)
                    for b in range(RB):
                        last = mm(psT[32 * b:32 * b + 32, c, :], rW2p[:, b, :], rh[c % 2][:, b, :], start=True, stop=True)
                    last.then_inc(logits_ready, 1)
                elif kind == "LT":
                    pe.wait_ge(lg_done, item[1] + 1)
                    turn(lambda t: LG[:, P * t:P * (t + 1)], P, P).then_inc(misc_written, 1)
                elif kind == "FZ":
                    pe.wait_ge(w_ready, 1)
                    turn(lambda t: Z[:, TB * item[1] + t, :], P, P).then_inc(misc_written, 1)
                elif kind == "down":
                    j = item[1]
                    e, ec, b = j // (BATCH * EB), j // EB, j % EB
                    pe.wait_ge(split_done, j + 1)
                    if b == 0:
                        if ec % BATCH == 0:
                            pe.wait_ge(w2_lo, e + 1)
                        if ec == 0:
                            pe.wait_ge(lg_done, BATCH)
                        if ec >= 2:
                            pe.wait_ge(comb_done, TB * (ec - 1))
                    hi, lo = hl[j % 3][:, 0, :], hl[j % 3][:, 1, :]
                    w = W2[e % 2]
                    for t in range(TB):
                        o = psT[:, 2 * (ec % 2) + t // 2, D * (t % 2):D * (t % 2 + 1)]
                        c0 = P * t
                        mm(o, hi[:, c0:c0 + P], w[:, 0, b, :], start=(b == 0 and t % 2 == 0), stop=False,
                           skip_group_check=True)
                        mm(o, hi[:, c0:c0 + P], w[:, 1, b, :], start=False, stop=False, skip_group_check=True)
                        last = mm(o, lo[:, c0:c0 + P], w[:, 0, b, :], start=False, stop=(b == EB - 1),
                                  skip_group_check=True)
                    last.then_inc(down_done, 1)

            last, tiles = tile_counts(pe)
            pe.wait_ge(gelu_done, N_UP_R + BATCH * EB)
            pe.wait_ge(comb_done, TB * BATCH)

            def turn_rows(e, i):
                if i is FIRST:
                    pe.wait_ge(misc_read, len(misc_at) - len(LATE) + (0 if e == 1 else 2 * (e - 1)))
                    if e > 1:
                        pe.wait_ge(xt_read[e - 1], tiles[e - 1])
                else:
                    pe.wait_ge(xt_read[e], upto(i, 1))
                pe.wait_ge(tile_in[e], upto(i, 16, 16))
                for a in range(2):
                    for k in range(2):
                        done = nc.tensor.transpose(psM[0:ZR, TS * a + P * k:TS * a + P * (k + 1)],
                                                   tile_rows[e % 2][:, k, ZR * a:ZR * (a + 1)], ident[:, :])
                done.then_inc(xt_written[e], 1)

            def up(e, i, b):
                if b == 0:
                    pe.wait_ge(xt_read[e], upto(i, 1, 1))
                if i is not FIRST:
                    pe.wait_ge(s_gelu[e], upto(i, EB, b - 1))
                elif b >= 2:
                    pe.wait_ge(s_gelu[e], b - 1)
                elif e > 1:
                    pe.wait_ge(s_gelu[e - 1], EB * tiles[e - 1])
                for a in range(2):
                    done = mm(psS[:, b % 2, 0:TS], W1[e % 2][0:ZR, a, b, :], Xt[0:ZR, a, :], start=(a == 0), stop=(a == 1))
                done.then_inc(s_up[e], 1)

            def down(e, m, b):
                pe.wait_ge(s_split[e], upto(m, EB, b + 1))
                if b == 0:
                    pe.wait_ge(y_free[e], upto(m, 1, 1))
                for k in range(2):
                    o = psT[:, bass.ds(upto(m, 1) % 2 + 2 * (e % 2), 1), D * k:D * (k + 1)].rearrange("p o c -> p (o c)")
                    for n, (x, w) in enumerate(((0, 0), (0, 1), (1, 0))):
                        done = mm(o, hs[:, b, x, P * k:P * (k + 1)], W2[e % 2][:, w, b, :],
                                  start=(b == 0 and k == 0 and n == 0), stop=(b == EB - 1 and n == 2), skip_group_check=True)
                done.then_inc(s_down[e], 1)

            def step(new, old):
                if new:
                    turn_rows(*new)
                if old:
                    down(*old, 0), down(*old, 1)
                for b in range(EB):
                    if new:
                        up(*new, b)
                    if old and b + 2 < EB:
                        down(*old, b + 2)

            for e in range(1, E):
                if e > 1:
                    pe.wait_ge(w1_filled[e + 1], 48)
                step((e, FIRST), (e - 1, (last[e - 1], 0)) if e > 1 else None)
                if e < E - 1:
                    pe.wait_ge(w1_filled[e + 1], 48)
                    for ch in range(2):
                        pe.wait_ge(misc_read, misc_at[("fold", e + 2, ch)])
                        fold(("fold", e + 2, ch))
                    pe.wait_ge(misc_read, misc_at[("fold", e + 2, 1)] + 1)
                pe.wait_ge(w2_lo, e + 1)
                with pe.Fori(0, last[e]) as m:
                    step((e, (m, 1)), (e, (m, 0)))
            step(None, (E - 1, (last[E - 1], 0)))

        @block.scalar
        def _(act):
            A = nc.scalar.activation

            def out_of_misc(item, dst, src):
                act.wait_ge(misc_written, misc_at[item] + 1)
                A(dst, src, ACT.Copy).then_inc(misc_read, 1)

            def fold_hi(item):
                _, f, ch = item
                act.wait_ge(misc_written, misc_at[item] + 1)
                nb = RB if f == 0 else EB
                dst = WR if f == 0 else W1[(f - 1) % 2]
                np_ = 512 // nb
                A(dst[0:ZF, 0, :, np_ * ch:np_ * (ch + 1)],
                  psM[0:ZF, :].rearrange("z (p b) -> z b p", b=nb), ACT.Copy).then_inc(hi_ready, 1)

            for item in order:
                kind = item[0]
                if kind == "soft":
                    act.wait_ge(logit_shift, item[1] + 1)
                    A(soft_x[:, :, :], soft_e[:, :, :], ACT.Exp).then_inc(base_exp, 1)
                elif kind == "CT":
                    out_of_misc(item, CTs[:, :], psM[:, :])
                elif kind == "H":
                    act.wait_ge(misc_written, misc_at[item] + 1)
                    if item[1] and item[2] == 0:
                        act.wait_ge(rstd_ready, item[1])
                    for t in range(2):
                        last = A(psM2[:, t, :], psM2[:, t, :], ACT.Square,
                                 accum_out=sq[:, 2 * item[2] + t:2 * item[2] + t + 1])
                    last.then_inc(misc_read, 1)
                elif kind == "KT":
                    if item[1]:
                        act.wait_ge(keys_ready, UH * item[1])
                    out_of_misc(item, KTs[:, :], psM[:, :])
                elif kind == "QA":
                    act.wait_ge(misc_written, misc_at[item] + 1)
                    A(RQh[:, :], psM[:, :], ACT.Copy).then_inc(qh_ready, 1)
                elif kind == "fold":
                    fold_hi(item)
                elif kind == "T":
                    _, u, k = item
                    n, q = 12 * u + k, 2 * u + k // 6
                    act.wait_ge(t_ready, n + 1)
                    if k % 6 == 0 and q >= 2:
                        act.wait_ge(pv_done, q - 1)
                    j = 2 * ((k % 6) // 3)
                    ps = psT[:, 2 * (n % 2):2 * (n % 2) + 2, :]
                    if k % 3 < 2:
                        A(PQ[q % 2][:, j + k % 3, 0:1024], ps.rearrange("p n c -> p (n c)"), ACT.Exp
                          ).then_inc(exp_done, 1)
                    else:
                        A(PQ[q % 2][:, j:j + 2, 1024:PT], ps[:, 0, :].rearrange("p (n c) -> p n c", c=256), ACT.Exp
                          ).then_inc(exp_done, 1)
                elif kind == "Zs":
                    b = item[1]
                    act.wait_ge(pv_done, 4 * (b + 1))
                    if b:
                        act.wait_ge(misc_written, misc_at[("ZT", b - 1)] + 1)
                    A(Zs[:, :], psV[:, :], ACT.Copy).then_inc(zs_done, 1)
                elif kind == "H2":
                    act.wait_ge(misc_written, misc_at[item] + 1)
                    if item[1] and item[2] == 0:
                        act.wait_ge(rstd2_ready, item[1])
                    for t in range(2):
                        last = A(psM2[:, t, :], psM2[:, t, :], ACT.Square,
                                 accum_out=sq2[:, 2 * item[2] + t:2 * item[2] + t + 1])
                    last.then_inc(misc_read, 1)
                elif kind in ("ZF", "FZ"):
                    out_of_misc(item, ZTs[:, :], psM[:, :])
                elif kind == "ZA":
                    out_of_misc(item, ZAB[0:ZR, item[2], SEQ * item[1]:SEQ * (item[1] + 1)], psM[0:ZR, :])
                elif kind == "FH":
                    t0 = TB * item[1] + 2 * item[2]
                    if item[1] == 0 and item[2] == 0:
                        act.wait_ge(t_ready, 12 * UNITS)
                    out_of_misc(item, acc[:, t0:t0 + 2, :], psM2[:, :, :])
                elif kind == "up":
                    i = item[1]
                    act.wait_ge(up_ready, i + 1)
                    if i == 0:
                        act.wait_ge(pv_done, 2 * UNITS)
                        act.wait_ge(small_in, 64)
                    if i < N_UP_R:
                        c, b = i // RB, i % RB
                        if c >= 2 and b == 0:
                            act.wait_ge(logits_ready, c - 1)
                        A(rh[c % 2][:, b, :], psS[:, i % 2, :], ACT.Gelu, bias=b1r[:, b:b + 1]).then_inc(gelu_done, 1)
                    else:
                        j = i - N_UP_R
                        e, b = j // (BATCH * EB), j % EB
                        if j >= 2:
                            act.wait_ge(split_done, j - 1)
                        A(hbuf[j % 2][:, :], psS[:, i % 2, :], ACT.Gelu, bias=b1e[:, TURN[e], b:b + 1]).then_inc(gelu_done, 1)
                elif kind == "route":
                    act.wait_ge(rl_ready, 1)
                    A(Lx[:, :, :], L[:, :, :], ACT.Exp).then_inc(rexp_done, 1)

            last, tiles = tile_counts(act)

            def copy_rows(e, i):
                act.wait_ge(xt_written[e], upto(i, 1, 1))
                if i is not FIRST:
                    act.wait_ge(s_up[e], upto(i, EB))
                elif e > 1:
                    act.wait_ge(s_up[e - 1], EB * tiles[e - 1])
                A(Xt[0:ZR, :, :], psM[0:ZR, :].rearrange("p (a c) -> p a c", a=2), ACT.Copy).then_inc(xt_read[e], 1)

            def gelu(e, i, b):
                act.wait_ge(s_up[e], upto(i, EB, b + 1))
                if i is not FIRST or b >= 2:
                    act.wait_ge(s_split[e], upto(i, EB, b - 1))
                elif e > 1:
                    act.wait_ge(s_split[e - 1], EB * tiles[e - 1])
                A(hbuf[b % 2][:, 0:TS], psS[:, b % 2, 0:TS], ACT.Gelu, bias=b1e[:, TURN[e], b:b + 1]).then_inc(s_gelu[e], 1)

            def outputs(e, m):
                act.wait_ge(s_down[e], upto(m, EB, EB))
                act.wait_ge(added[e], upto(m, 32, 16))
                for k in range(2):
                    done = A(Yo[e % 2][:, k, :],
                             psT[:, bass.ds(upto(m, 1) % 2 + 2 * (e % 2), 1), D * k:D * (k + 1)].rearrange("p o c -> p (o c)"),
                             ACT.Copy, scale=xe[e % 2][:, bass.ds(upto(m, 2, k), 1), 2 * ZR + e])
                done.then_inc(y_free[e], 1)

            def step(new, old):
                if new:
                    copy_rows(*new)
                for b in range(EB):
                    if new:
                        gelu(*new, b)
                    if b == EB - 2 and old:
                        outputs(*old)

            for e in range(1, E):
                for k in range(2):
                    A(scrap[:, k:k + 1], ident[:, 0:1], ACT.Copy).then_inc(y_free[e], 1)
                step((e, FIRST), (e - 1, (last[e - 1], 0)) if e > 1 else None)
                if e < E - 1:
                    for ch in range(2):
                        fold_hi(("fold", e + 2, ch))
                if e > 2:
                    act.wait_ge(added[e - 2], 16 + 32 * tiles[e - 2])
                with act.Fori(0, last[e]) as m:
                    step((e, (m, 1)), (e, (m, 0)))
            step(None, (E - 1, (last[E - 1], 0)))

        @block.vector
        def _(dve):
            v = nc.vector
            links = [0]

            def link(ins):
                links[0] += 1
                ins.then_inc(dve_link, 1)
                dve.wait_ge(dve_link, links[0])

            def bc(ap, shape):
                return ap.broadcast_to(shape)

            v.memset(M2[:, :], 0.0).then_inc(zeroed, 1)
            v.memset(rW2p[:, :, :], 0.0).then_inc(zeroed, 1)
            v.memset(Bcr[:, :], 0.0).then_inc(zeroed, 1)
            v.memset(CP[:, :, :], 0.0).then_inc(zeroed, 1)
            v.memset(KE[:, :, :], 0.0).then_inc(zeroed, 1)
            dve.wait_ge(zeroed, 5)
            dve.wait_ge(bases_in, 96)
            for p0 in (0, 4 * HEADS):
                r = slice(p0, p0 + NB)
                v.tensor_tensor(rows_b[r, 0, :], raw_b[r, 0, :], raw_b[r, 1, :], ALU.add)
                link(v.tensor_scalar(rows_b[r, 1, :], raw_b[r, 2, :], 0.1, None, ALU.mult))
                dst = M2[r, :] if p0 else Bcr[r, :]
                link(v.scalar_tensor_tensor(dst, rows_b[r, 0, :], SCALE_D, rows_b[r, 1, :], ALU.mult, ALU.add))

            def centre(dst, src, rows):
                link(v.tensor_reduce(stat[0:rows, 0:1], src, AX.X, ALU.add))
                link(v.tensor_scalar(stat[0:rows, 1:2], stat[0:rows, 0:1], 1.0 / D, None, ALU.mult))
                return v.tensor_scalar(dst, src, stat[0:rows, 1:2], None, ALU.subtract)

            centre(Bcr[0:NB, :], Bcr[0:NB, :], NB).then_inc(bases_ready, 1)
            dve.wait_ge(bases_ready, 1)
            v.memset(QBpad[:, :, :], 0.0).then_inc(bases_ready, 1)
            v.memset(M2c[:, :], 0.0)
            v.memset(KBexp[:, :, :, :], 0.0)
            v.memset(mexp[:, :, :, :], 0.0)
            v.memset(Z[:, :, :], 0.0)
            v.memset(Vst[0][:, :, :], 0.0)
            v.memset(Vst[1][:, :, :], 0.0)
            link(v.memset(KE[:, :, 3 * NB:3 * NB + 2], 1.0))
            for i in range(2):
                link(v.memset(Vst[i][:, :, :].rearrange("p t (r s) -> p t r s", s=40)[:, :, :, NB:NB + 1], 1.0))
            dve.wait_ge(consts, 3)
            link(v.tensor_scalar(head_mask_q[:, :], head_mask[:, :], DH ** -0.5, None, ALU.mult))
            link(v.tensor_reduce(neg_lo_rows[:, :], lo_rows8[:, :], AX.X, ALU.add, negate=True))

            def misc_wait(item):
                dve.wait_ge(misc_written, misc_at[item] + 1)

            def fold_lo(item):
                _, f, ch = item
                nb = RB if f == 0 else EB
                np_ = 512 // nb
                dst = WR if f == 0 else W1[(f - 1) % 2]
                dve.wait_ge(hi_ready, fold_before[item] + 1)
                if f >= 1 and ch == 0:
                    dve.wait_ge(w1_filled[f - 1], 48)
                lo = flo[:, 0:512 * (1 if f == 0 else 2)].rearrange("z (b p) -> z b p", b=nb)
                v.tensor_tensor(lo[:, :, np_ * ch:np_ * (ch + 1)],
                                psM[0:ZF, :].rearrange("z (p b) -> z b p", b=nb),
                                dst[0:ZF, 0, :, np_ * ch:np_ * (ch + 1)].bitcast(F32), ALU.subtract
                                ).then_inc(misc_read, 1)
                dve.wait_ge(misc_read, misc_at[item] + 1)
                v.memset(stat[:, 4:5], 0.0).then_inc(lo_ready, 1)

            for item in order:
                kind = item[0]
                if kind == "BcT":
                    misc_wait(item)
                    v.tensor_copy(BcT[:, :, :], psM[:, 0:2 * P].rearrange("p (k c) -> p k c", c=P)[:, :, 0:NB]
                                  ).then_inc(misc_read, 1)
                elif kind == "QKV":
                    misc_wait(item)
                    v.tensor_copy(qkvb[:, :, :], psM[:, 0:6 * NB].rearrange("p (j n) -> p j n", n=NB)
                                  ).then_inc(misc_read, 1)
                    dve.wait_ge(misc_read, misc_at[item] + 1)
                    for g in range(2):
                        v.tensor_copy(QBpad[:, g, 0:NB], qkvb[:, g, :])
                        v.tensor_copy(QBpad[:, g, NB:2 * NB], qkvb[:, g, :])
                        for part in range(3):
                            v.tensor_tensor(KBexp[:, g, :, NB * part:NB * (part + 1)],
                                            bc(qkvb[:, 2 + g, :].rearrange("p (o n) -> p o n", o=1), [P, UH, NB]),
                                            bc(head_mask_q[:, :].rearrange("p (h o) -> p h o", o=1), [P, UH, NB]),
                                            ALU.mult)
                    v.memset(VBexp[:, :, :], 0.0).then_inc(bases_ready, 1)
                    dve.wait_ge(bases_ready, 3)
                    for g in range(2):
                        last = v.tensor_tensor(
                            VBexp[:, g, 32 * g:32 * g + 32].rearrange("p (h n) -> p h n", n=NB),
                            bc(qkvb[:, 4 + g, :].rearrange("p (o n) -> p o n", o=1), [P, UH, NB]),
                            bc(head_mask[:, :].rearrange("p (h o) -> p h o", o=1), [P, UH, NB]), ALU.mult)
                    last.then_inc(bases_ready, 1)
                elif kind == "Arep":
                    misc_wait(item)
                    v.tensor_copy(Arep[:, :, :], psM4[:, 0:2, :]).then_inc(misc_read, 1)
                elif kind == "M":
                    misc_wait(item)
                    v.tensor_copy(M2[0:4 * HEADS, :], psM[0:4 * HEADS, 0:D]).then_inc(misc_read, 1)
                    dve.wait_ge(misc_read, misc_at[item] + 1)
                    centre(M2c[0:ZF, :], M2[0:ZF, :], ZF).then_inc(bases_ready, 1)
                elif kind == "McT":
                    misc_wait(item)
                    v.tensor_copy(McT[:, :, :], psM4[:, 0:KD, 0:ZF]).then_inc(misc_read, 1)
                elif kind == "fold":
                    fold_lo(item)
                elif kind == "soft":
                    b = item[1]
                    g = gathered[:, TB * b:TB * (b + 1), :]
                    dve.wait_ge(rows_in[b], 16 * TB)
                    if b:
                        dve.wait_ge(base_exp, b)
                    link(v.tensor_reduce(soft_s[:, 0, :], g, AX.X, ALU.max))
                    v.tensor_tensor(soft_e[:, :, :], g, bc(soft_s[:, 0, :].rearrange("p (t o) -> p t o", o=1),
                                                          [P, TB, NB]), ALU.subtract).then_inc(logit_shift, 1)
                elif kind == "mix":
                    b = item[1]
                    dve.wait_ge(base_exp, b + 1)
                    link(v.tensor_reduce(soft_s[:, 1, :], soft_x[:, :, :], AX.X, ALU.add))
                    link(v.reciprocal(soft_s[:, 2, :], soft_s[:, 1, :]))
                    inv = bc(soft_s[:, 2, :].rearrange("p (t o) -> p t o", o=1), [P, TB, NB])
                    v.tensor_tensor(Z[:, TB * b:TB * (b + 1), 4 * HEADS:ZF], soft_x[:, :, :], inv, ALU.mult)
                    if b:
                        dve.wait_ge(misc_written, misc_at[("CT", b - 1)] + 1)
                    v.tensor_tensor(CP[:, :, 0:NB], soft_x[:, :, :], inv, ALU.mult).then_inc(coeff_ready, 1)
                elif kind == "keys":
                    b = item[1]
                    dve.wait_ge(rstd_ready, b + 1)
                    dve.wait_ge(coeff_ready, b + 1)
                    if b:
                        dve.wait_ge(vst_ready, b)
                    link(v.tensor_tensor(U[:, :, :], Z[:, TB * b:TB * (b + 1), 4 * HEADS:ZF],
                                         bc(rstd[:, 1, :].rearrange("p (t o) -> p t o", o=1), [P, TB, NB]), ALU.mult))
                    link(v.tensor_copy(KE[:, :, 0:NB].bitcast(F32R), U[:, :, :]))
                    v.tensor_tensor(KE[:, :, NB:2 * NB], U[:, :, :], KE[:, :, 0:NB], ALU.subtract)
                    link(v.tensor_copy(KE[:, :, 2 * NB:3 * NB], KE[:, :, 0:NB]))
                    if b:
                        dve.wait_ge(misc_written, misc_at[("KT", b - 1)] + 1)
                    v.tensor_copy(KE8[:, :, :, :],
                                  bc(KE[:, :, :].rearrange("p t (o r) -> p t o r", o=1), [P, TB, UH, ROWS])
                                  ).then_inc(ke_ready, 1)
                elif kind == "values":
                    b = item[1]
                    if b >= 2:
                        dve.wait_ge(pv_done, 4 * (b - 1))
                    v.tensor_copy(Vst[b % 2][:, :, :].rearrange("p t (r s) -> p t r s", s=40)[:, :, :, 0:NB],
                                  bc(U[:, :, :].rearrange("p t (o n) -> p t o n", o=1), [P, TB, 4, NB])
                                  ).then_inc(vst_ready, 1)
                elif kind == "QA":
                    b, g = item[1:]
                    u = 2 * b + g
                    dve.wait_ge(qh_ready, u + 1)
                    if u >= 2:
                        dve.wait_ge(s_ready, 20 * (u - 1))
                    v.scalar_tensor_tensor(RQ1[g][:, :], RQh[:, :].bitcast(F32), neg_lo_rows[:, :], psM[:, :],
                                           ALU.mult, ALU.add).then_inc(misc_read, 1)
                elif kind == "S":
                    _, u, k = item
                    n = 20 * u + k
                    h = 4 * (k // 10) + 2 * ((k % 10) // 5)
                    kk = k % 5
                    dve.wait_ge(s_ready, n + 1)
                    m = maxp[u % 2]
                    src = psS[:, n % 2, :].rearrange("p (n c) -> p n c", c=P)
                    if kk < 4:
                        dst = m[:, h + kk // 2, 4 * (kk % 2):4 * (kk % 2) + 4]
                    else:
                        dst = m[:, h:h + 2, 8:10]
                        src = psS[:, n % 2, :].rearrange("p (a n c) -> p a n c", a=2, c=P)
                    v.tensor_reduce(dst, src, AX.X, ALU.max).then_inc(max_done, 1)
                elif kind == "max":
                    u = item[1]
                    m = maxp[u % 2]
                    dve.wait_ge(max_done, 20 * (u + 1))
                    if u:
                        dve.wait_ge(mexp_ready, u)
                    for qb, (a, z) in enumerate([(4, 5), (8, 10), (5, 8), (0, 4)]):
                        last = v.tensor_reduce(nm[:, qb, :], m[:, :, a:z], AX.X, ALU.max, negate=True)
                    link(last)
                    if u:
                        dve.wait_ge(misc_written, misc_at[("shift", u - 1)] + 1)
                    hi = mexp[:, :, :, 3 * NB]
                    link(v.tensor_copy(hi.bitcast(F32R), nm[:, :, :]))
                    v.tensor_tensor(mexp[:, :, :, 3 * NB + 1], nm[:, :, :], hi, ALU.subtract).then_inc(mexp_ready, 1)
                elif kind == "shift":
                    u = item[1]
                    g = u % 2
                    misc_wait(item)
                    if u >= 2:
                        dve.wait_ge(t_ready, 12 * (u - 1))
                    v.tensor_tensor(RQ2[g][:, :], RQ1[g][:, :].bitcast(F32), psM[:, :], ALU.add
                                    ).then_inc(misc_read, 1)
                elif kind == "ZT":
                    b = item[1]
                    misc_wait(item)
                    link(v.reciprocal(rec[:, :, :], psM[:, :].rearrange("p (t h e) -> p t h e", t=TB, e=8)[:, :, :, NB]))
                    for t in range(TB):
                        last = v.tensor_tensor(
                            Z[:, TB * b + t, 0:4 * HEADS].rearrange("p (r j n) -> p j r n", j=4, n=NB),
                            psM4[:, t, :].rearrange("p (j r e) -> p j r e", j=4, e=8)[:, :, :, 0:NB],
                            bc(rec[:, t, :].rearrange("p (j r o) -> p j r o", j=4, o=1), [P, 4, 4, NB]), ALU.mult)
                    last.then_inc(misc_read, 1)
                elif kind == "zab":
                    b = item[1]
                    dve.wait_ge(rstd2_ready, b + 1)
                    link(v.tensor_tensor(Zr[:, :, :], Z[:, TB * b:TB * (b + 1), 0:ZF],
                                         bc(rstd2[:, 1, :].rearrange("p (t o) -> p t o", o=1), [P, TB, ZF]), ALU.mult))
                    half = ZF // 2
                    r = rows[:, TB * b:TB * (b + 1), :]
                    link(v.tensor_copy(r[:, :, 0:ZF].bitcast(F32R), Zr[:, :, :]))
                    v.tensor_copy(r[:, :, ZF:ZR], r[:, :, 0:half])
                    v.tensor_copy(r[:, :, ZR + ZF:2 * ZR], r[:, :, half:ZF])
                    v.tensor_tensor(r[:, :, ZR:ZR + ZF], Zr[:, :, :], r[:, :, 0:ZF], ALU.subtract
                                    ).then_inc(zab_ready, 1)
                elif kind == "w2":
                    e = item[1]
                    dve.wait_ge(raw2_in, 16 * (e + 1))
                    if e == 1:
                        dve.wait_ge(t_ready, 12 * UNITS)
                    v.tensor_copy(W2[e % 2][:, 0, :, :], raw2[e % 2][:, :, :]).then_inc(w2_hi, 1)
                elif kind == "logits":
                    c = item[1]
                    dve.wait_ge(logits_ready, c + 1)
                    if c:
                        dve.wait_ge(misc_written, misc_at[("LT", c - 1)] + 1)
                    v.tensor_copy(LG[:, :], psT[:, c, :]).then_inc(lg_done, 1)
                elif kind == "LT":
                    c = item[1]
                    misc_wait(item)
                    v.tensor_reduce(L[:, TB * c:TB * (c + 1), :],
                                    psM[:, :].rearrange("p (t b r) -> p t r b", t=TB, r=32)[:, :, 0:E, :],
                                    AX.X, ALU.add).then_inc(misc_read, 1)
                elif kind == "route":
                    dve.wait_ge(misc_read, misc_at[("LT", BATCH - 1)] + 1)
                    link(v.tensor_tensor(L[:, :, :], L[:, :, :],
                                         bc(rb2b[:, :].rearrange("p (o n) -> p o n", o=1), [P, NT, E]), ALU.add))
                    link(v.tensor_reduce(Ls[:, 0, :], L[:, :, :], AX.X, ALU.max))
                    v.tensor_tensor(L[:, :, :], L[:, :, :],
                                    bc(Ls[:, 0, :].rearrange("p (t o) -> p t o", o=1), [P, NT, E]), ALU.subtract
                                    ).then_inc(rl_ready, 1)
                    dve.wait_ge(rexp_done, 1)
                    link(v.tensor_reduce(Ls[:, 0, :], Lx[:, :, :], AX.X, ALU.add))
                    link(v.reciprocal(Ls[:, 1, :], Ls[:, 0, :]))
                    link(v.tensor_tensor(prob[:, :, :], Lx[:, :, :],
                                         bc(Ls[:, 1, :].rearrange("p (t o) -> p t o", o=1), [P, NT, E]), ALU.mult))
                    other = bc(prob[:, :, :].rearrange("p t (o j) -> p t o j", o=1), [P, NT, E, E])
                    own = bc(prob[:, :, :].rearrange("p t (e o) -> p t e o", o=1), [P, NT, E, E])
                    v.tensor_tensor(cmp_a[:, :, :, :], other, own, ALU.is_gt)
                    link(v.tensor_tensor(cmp_b[:, :, :, :], other, own, ALU.is_equal))
                    dve.wait_ge(consts, 5)
                    link(v.tensor_tensor(cmp_b[:, :, :, :], cmp_b[:, :, :, :], tri[:, :, :, :], ALU.mult))
                    link(v.tensor_tensor(cmp_a[:, :, :, :], cmp_a[:, :, :, :], cmp_b[:, :, :, :], ALU.add))
                    link(v.tensor_reduce(rank[:, :, :], cmp_a[:, :, :, :], AX.X, ALU.add))
                    link(v.tensor_scalar(rank[:, :, :], rank[:, :, :], 1.5, None, ALU.is_lt))
                    v.tensor_tensor(wgt[:, :, :], rank[:, :, :], prob[:, :, :], ALU.mult)
                    v.tensor_tensor(rows[:, :, 2 * ZR + 1:XR], rank[:, :, 0:E - 1], prob[:, :, 0:E - 1], ALU.mult)
                    v.tensor_tensor(Z[:, :, ZF:ZF + E], rank[:, :, :], prob[:, :, :], ALU.mult).then_inc(w_ready, 1)
                elif kind == "places":
                    misc_wait(item)
                    before = psM[:, 0:(NT + 1) * E].rearrange("p (t e) -> p t e", e=E)
                    v.tensor_tensor(more[:, :, :], bc(before[0:1, NT, 0:E - 1].rearrange("p (e o) -> p e o", o=1),
                                                      [1, E - 1, TILES - MIN_TILES]), limits[:, :, :], ALU.is_gt)
                    link(v.scalar_tensor_tensor(dest[:, :, :], rank[:, :, 0:E - 1], -FAR, region_far[:, :, :],
                                                ALU.mult, ALU.add))
                    link(v.tensor_reduce(tiles_f[:, :], more[:, :, :], AX.X, ALU.add))
                    v.tensor_scalar(last_i[:, :], tiles_f[:, :], float(MIN_TILES - 1), None, ALU.add).then_inc(tiles_ready, 1)
                    v.tensor_tensor(dest[:, :, :], dest[:, :, :], before[:, 0:NT, 0:E - 1], ALU.add).then_inc(misc_read, 1)
                    dve.wait_ge(misc_read, misc_at[item] + 1)
                    v.tensor_reduce(dest_s[:, 0, :], dest[:, :, :], AX.X, ALU.min)
                    v.tensor_reduce(dest_s[:, 1, :], dest[:, :, :], AX.X, ALU.max)
                    link(v.tensor_reduce(dest_s[:, 2, :], dest[:, :, :], AX.X, ALU.add))
                    link(v.tensor_tensor(dest_s[:, 2, :], dest_s[:, 2, :], dest_s[:, 0, :], ALU.subtract))
                    link(v.tensor_tensor(dest_s[:, 1, :], dest_s[:, 2, :], dest_s[:, 1, :], ALU.subtract))
                    v.tensor_copy(dest_i[:, :, :], dest_s[:, 0:2, :]).then_inc(places_ready, 1)
                elif kind == "split":
                    j = item[1]
                    dve.wait_ge(gelu_done, N_UP_R + j + 1)
                    if j >= 3:
                        dve.wait_ge(down_done, j - 2)
                    link(v.tensor_copy(hl[j % 3][:, 0, :], hbuf[j % 2][:, :]))
                    v.tensor_tensor(hl[j % 3][:, 1, :], hbuf[j % 2][:, :], hl[j % 3][:, 0, :].bitcast(F32), ALU.subtract
                                    ).then_inc(split_done, 1)
                elif kind == "combine":
                    ec = item[1]
                    e, c = ec // BATCH, ec % BATCH
                    dve.wait_ge(down_done, EB * (ec + 1))
                    if e == 0:
                        dve.wait_ge(misc_read, misc_at[("FH", c, 1)] + 1)
                        dve.wait_ge(w_ready, 1)
                    else:
                        dve.wait_ge(comb_done, TB * (ec - BATCH + 1))
                    for t in range(TB):
                        a = acc[:, TB * c + t, :]
                        o = psT[:, 2 * (ec % 2) + t // 2, D * (t % 2):D * (t % 2 + 1)]
                        v.scalar_tensor_tensor(a, o, wgt[:, TB * c + t, TURN[e]:TURN[e] + 1], a, ALU.mult, ALU.add
                                               ).then_inc(comb_done, 1)

            last, tiles = tile_counts(dve)

            def split_tile(e, i):
                for b in range(EB):
                    dve.wait_ge(s_gelu[e], upto(i, EB, b + 1))
                    if i is FIRST:
                        if e > 1:
                            dve.wait_ge(s_down[e - 1], upto((last[e - 1], 0), EB, b + 1))
                    else:
                        dve.wait_ge(s_down[e], upto((i[0], 0), EB, b + 1))
                    v.tensor_copy(hs[:, b, 0, :], hbuf[b % 2][:, 0:TS]).then_inc(hi_done[e], 1)
                    dve.wait_ge(hi_done[e], upto(i, EB, b + 1))
                    v.tensor_tensor(hs[:, b, 1, :], hbuf[b % 2][:, 0:TS], hs[:, b, 0, :].bitcast(F32), ALU.subtract
                                    ).then_inc(s_split[e], 1)

            for e in range(1, E):
                split_tile(e, FIRST)
                if e < E - 1:
                    for ch in range(2):
                        fold_lo(("fold", e + 2, ch))
                with dve.Fori(0, last[e]) as m:
                    split_tile(e, (m, 1))


_INS = ["x", "L0_tok_coeff_weight", "L0_tok_base_embed_weight", "L0_tok_lang_bias", "L0_attn_w_qkv", "L0_attn_w_proj",
        "L0_ffn_rW1", "L0_ffn_rb1", "L0_ffn_rW2", "L0_ffn_rb2", "L0_ffn_We1", "L0_ffn_be1", "L0_ffn_We2", "L0_ffn_be2"]


def kernel(**inputs):
    import concourse.bacc as bacc
    from concourse.bass_utils import run_bass_kernel_spmd

    nc = bacc.Bacc("TRN2", target_bir_lowering=False, num_devices=1)
    arrays, args = {}, []
    for name in _INS:
        a = np.ascontiguousarray(inputs[name])
        arrays[f"in_{name}"] = a
        args.append(nc.dram_tensor(f"in_{name}", a.shape, mybir.dt.from_np(a.dtype), kind="ExternalInput").ap())
    out = nc.dram_tensor("out", (BATCH, SEQ, D), F32, kind="ExternalOutput").ap()
    tower_kernel(nc, *args, out)
    r = run_bass_kernel_spmd(nc, [arrays], core_ids=[0])
    return r.results[0]["out"]
```

```python
import numpy as np
import concourse.bass as bass
from concourse import mybir

F32, F32R, BF16, I32 = mybir.dt.float32, mybir.dt.float32r, mybir.dt.bfloat16, mybir.dt.int32
ALU, ACT, AX = mybir.AluOpType, mybir.ActivationFunctionType, mybir.AxisListType

P = 128
BATCH, SEQ, D = 4, 512, 256
NB = 4
HEADS, DH = 16, 16
E, HID, RHID = 4, 1024, 512
TB = SEQ // P
NT = BATCH * TB
KD = D // P
UNITS = 2 * BATCH
UH = 8
ROWS = P // UH
ZF = 4 * HEADS + NB
ZR = ZF + ZF // 2
EB, RB = HID // P, RHID // P
PT = 1280
TURN = tuple(reversed(range(E)))
W2_OF = (0, 1, 0, 2)
XR = 2 * ZR + E
TS = 2 * P
TOK = NT * P
TILES = TOK // TS
MIN_TILES = 1
FAR = float(1 << 20)
EPS = 1e-5
SCALE_D, LANG = 16.0, 2
NEG = -1e30
PV_ORDER = (0, 1, 3, 2)

KB_AT = {0: (0, 512), 1: (512, 896), 2: (1024, 1280), 3: (896, 1024)}


AT = dict(BcT=-65.57, QKV=-57.44, Arep=-54.83, gather1=-50.1, gather2=-3.33, gather3=-30.51,
          more_consts=-13.42, M=-11.95, McT=2.43, fold00=3.57, fold10=5.29, fold11=7.19, fold20=15.09,
          fold21=17.86, w20=30.3, soft=-45.98, mix=-44.11, CT=-35.99, H0=-17.56, H1=-28.45, rstd=-29.94,
          keys=-25.37, KT=-19.16, variants=3.77, QA0=-3.74, QA1=8.11, values=12.83, max=20.38, shift=23.1,
          T=26.0, PV=38.03, PVstep=2.1, Zs=88.2, ZT=61.52, ZF=68.86, H20=61.87, H21=77.74, rstd2=68.8,
          zab=93.01, ZA0=116.38, ZA1=100.48, up=199.37, upc=9.03, ups=2.17, logits=10.14, LT=13.52, ex=236.31,
          down=2.06, comb=3.37, route=3.91, FZ=5.45, w21=5.84, places=8.55)
AT1 = {('ZA1', 3): 102.83, ('rstd2', 0): 92.29, ('zab', 0): 93.06, ('ZA0', 0): 96.25, ('ZA1', 0): 98.55,
       ('QA1', 2): 7.76, ('CT', 3): -27.51, ('QA0', 2): -12.62, ('values', 2): -1.63, ('H0', 0): -57.04,
       ('H1', 0): -56.97, ('rstd', 0): -56.44, ('QA0', 3): -12.72, ('ZF', 0): 79.9, ('QA1', 0): 1.15,
       ('ZF', 1): 79.95, ('values', 1): 16.2, ('zab', 3): 93.8, ('H21', 1): 88.7, ('ZT', 2): 77.63,
       ('mix', 2): -35.16, ('H21', 3): 90.17, ('ZA0', 2): 107.37, ('mix', 0): -58.26, ('CT', 0): -57.16,
       ('ZA0', 3): 99.24, ('mix', 1): -32.86, ('QA1', 3): 6.11, ('ZT', 1): 77.35, ('H20', 2): 87.28,
       ('H21', 2): 95.62, ('rstd2', 2): 97.48, ('zab', 2): 106.85, ('keys', 2): -21.16, ('values', 3): 9.57,
       ('variants', 0): -51.45, ('H20', 1): 81.79, ('KT', 0): -54.04, ('rstd2', 3): 91.05, ('soft', 1): -35.78,
       ('H20', 3): 87.5, ('H1', 1): -27.18, ('mix', 3): -32.3, ('H0', 2): -25.86, ('rstd2', 1): 89.48,
       ('zab', 1): 94.93, ('ZA0', 1): 96.64, ('ZA1', 2): 110.38, ('soft', 0): -58.45, ('soft', 2): -41.95,
       ('keys', 0): -54.99, ('QA0', 0): -47.2, ('ZF', 3): 83.59, ('ZT', 0): 77.15, ('rstd', 2): -23.78,
       ('variants', 2): -14.16, ('variants', 3): -15.02, ('Zs', 3): 77.02, ('ZT', 3): 83.52, ('H0', 3): -26.16,
       ('H1', 3): -25.36, ('rstd', 3): -23.45, ('H20', 0): 85.16, ('CT', 2): -32.14, ('H21', 0): 89.87,
       ('soft', 3): -39.28, ('H0', 1): -29.71, ('rstd', 1): -25.66, ('keys', 1): -25.31, ('KT', 1): -19.14,
       ('variants', 1): -12.64, ('QA0', 1): -7.39, ('QA1', 1): 5.74, ('values', 0): 8.13, ('KT', 2): -19.22,
       ('Zs', 0): 74.86, ('keys', 3): -21.86, ('ZA1', 1): 98.69, ('H1', 2): -23.99, ('ZF', 2): 80.84,
       ('Zs', 1): 75.95, ('Zs', 2): 75.97, ('KT', 3): -19.79, ('CT', 1): -32.63}


def step_order():
    at = []

    def put(when, *item):
        at.append((when, len(at), item))

    A = AT
    put(A["BcT"], "BcT"), put(A["QKV"], "QKV"), put(A["Arep"], "Arep"), put(A["more_consts"], "consts")
    for b in range(1, BATCH):
        put(A[f"gather{b}"], "gather", b)
    put(A["M"], "M"), put(A["McT"], "McT")
    for f, ch in ((0, 0), (1, 0), (1, 1), (2, 0), (2, 1)):
        put(A[f"fold{f}{ch}"], "fold", f, ch)
    put(A["w20"], "w2", 0)
    for b in range(BATCH):
        def a(name):
            return 40 * b + AT1.get((name, b), A[name])
        put(a("soft"), "soft", b), put(a("mix"), "mix", b), put(a("CT"), "CT", b)
        put(a("H0"), "H", b, 0), put(a("H1"), "H", b, 1), put(a("rstd"), "rstd", b)
        put(a("keys"), "keys", b), put(a("KT"), "KT", b)
        put(a("variants"), "variants", b)
        put(a("QA0"), "QA", b, 0)
        put(a("QA1"), "QA", b, 1)
        put(a("values"), "values", b)
        put(a("Zs"), "Zs", b), put(a("ZT"), "ZT", b), put(a("ZF"), "ZF", b), put(a("H20"), "H2", b, 0)
        put(a("H21"), "H2", b, 1), put(a("rstd2"), "rstd2", b), put(a("zab"), "zab", b)
        put(a("ZA0"), "ZA", b, 0), put(a("ZA1"), "ZA", b, 1)
    for u in range(UNITS):
        for k in range(20):
            put(20 * u + k, "S", u, k)
        put(20 * u + A["max"], "max", u)
        put(20 * u + A["shift"], "shift", u)
        for k in range(12):
            put(20 * u + A["T"] + k * 20 / 12, "T", u, k)
    for q in range(2 * UNITS):
        for n, kb in enumerate(PV_ORDER):
            put(10 * q + A["PV"] + A["PVstep"] * n, "PV", q, kb)

    for c in range(BATCH):
        for b in range(RB):
            put(A["up"] + A["upc"] * c + A["ups"] * b, "up", RB * c + b)
        put(A["up"] + A["upc"] * c + A["logits"], "logits", c), put(A["up"] + A["upc"] * c + A["LT"], "LT", c)
    t0, n = A["ex"], BATCH * EB
    for j in range(n):
        put(t0 + j, "up", RB * BATCH + j), put(t0 + j + 0.1, "split", j), put(t0 + j + A["down"], "down", j)
        if j % EB == EB - 1:
            put(t0 + j + A["comb"], "combine", j // EB)
    put(t0 + A["route"], "route"), put(t0 + A["places"], "places")
    for c in range(BATCH):
        for k, what in enumerate((("FZ", c), ("FH", c, 0), ("FH", c, 1))):
            put(t0 + 8 * c + A["FZ"] + k, *what)
    put(t0 + A["w21"], "w2", 1)
    return [item for _, _, item in sorted(at)]


MISC = ("BcT", "QKV", "Arep", "CT", "H", "KT", "QA", "M", "McT", "fold", "shift", "ZT", "ZF", "H2", "ZA",
        "LT", "FZ", "FH", "places")
FOLD_AT = {(e, b): ("fold", e + 2, ch) for e in (1, 2) for b, ch in ((1, 0), (3, 1))}
LATE = (("fold", 3, 0), ("fold", 3, 1), ("fold", 4, 0), ("fold", 4, 1))


def tower_kernel(nc, x, coeff_w, base_w, lang_w, w_qkv, w_proj, rW1, rb1, rW2, rb2, We1, be1, We2, be2, out):
    order = step_order()
    misc_at = {item: n for n, item in enumerate([i for i in order if i[0] in MISC] + list(LATE))}

    at = [(nc.sbuf_base + 31) // 32 * 32]

    def place(name, shape, dt=F32, over=None):
        size = int(np.prod(shape[1:])) * (2 if dt == BF16 else 4)
        size = (size + 31) // 32 * 32
        here = at if over is None else over
        t = nc.alloc_sbuf_tensor_at(name, shape, dt, offset=here[0])
        here[0] += size
        return t

    ident = place("ident", [P, P])
    ident_b = place("ident_b", [P, P], BF16)
    neg_mask = place("neg_mask", [P, 2 * P], BF16)
    head_mask = place("head_mask", [P, UH])
    head_mask_q = place("head_mask_q", [P, UH])
    lo_rows8 = place("lo_rows8", [P, UH])
    neg_lo_rows = place("neg_lo_rows", [P, 1])
    tri = place("tri", [P, NT, E, E])
    below = place("below", [P, P])
    ones = place("ones", [P, P])
    region_far = place("region_far", [P, NT, E - 1])
    limits = place("limits", [1, E - 1, TILES - MIN_TILES])
    pad = place("pad", [P, 2, XR])
    no_id = place("no_id", [P, 2], I32)
    minus_half = place("minus_half", [P, TB])
    idx = place("idx", [P, NT], I32)
    gathered = place("gathered", [P, NT, NB])
    Bcr = place("Bcr", [P, D])
    rows_at, rows_at0 = list(at), at[0]
    raw_b = place("raw_b", [P, 3, D])
    rows_b = place("rows_b", [P, 2, D])
    wqkv = place("wqkv", [P, KD, 3 * D])
    wproj = place("wproj", [P, KD, D])
    rows_end = at[0]
    rows = place("rows", [P, NT, XR], over=rows_at)
    assert rows_at[0] <= rows_end
    BcT = place("BcT", [P, KD, NB])
    qkvb = place("qkvb", [P, 6, NB])
    KBexp = place("KBexp", [P, 2, UH, ROWS])
    QBpad = place("QBpad", [P, 2, P])
    Arep = place("Arep", [P, 2, P])
    VBexp = place("VBexp", [P, 2, 2 * UH * NB])
    M2 = place("M2", [P, D])
    M2c = place("M2c", [P, D])
    McT = place("McT", [P, KD, ZF])
    stat = place("stat", [P, 8])
    soft_e = place("soft_e", [P, TB, NB])
    soft_x = place("soft_x", [P, TB, NB])
    soft_s = place("soft_s", [P, 3, TB])
    dead_at = list(at)
    CP = place("CP", [P, TB, P])
    cts_at = list(at)
    CTs = place("CTs", [P, SEQ])
    RQh = place("RQh", [P, SEQ], F32R, over=cts_at)
    sq = place("sq", [P, TB])
    rstd = place("rstd", [P, 2, TB])
    U = place("U", [P, TB, NB])
    KE = place("KE", [P, TB, ROWS])
    KE8 = place("KE8", [P, TB, UH, ROWS])
    KTs = place("KTs", [P, SEQ])
    Vst = [place(f"Vst{i}", [P, TB, 160]) for i in range(2)]
    RQ1 = [place(f"RQ1_{i}", [P, SEQ], F32R) for i in range(2)]
    RQ2 = [place(f"RQ2_{i}", [P, SEQ], F32R) for i in range(2)]
    maxp = [place(f"maxp{i}", [P, UH, 10]) for i in range(2)]
    nm = place("nm", [P, TB, UH])
    mexp = place("mexp", [P, TB, UH, ROWS])
    Zs = place("Zs", [P, SEQ])
    rec = place("rec", [P, TB, HEADS])
    dead_end = at[0]
    Z = place("Z", [P, NT, P])
    ZTs = place("ZTs", [P, SEQ])
    sq2 = place("sq2", [P, TB])
    rstd2 = place("rstd2", [P, 2, TB])
    Zr = place("Zr", [P, TB, ZF])
    ZAB = place("ZAB", [P, 2, NT * P], F32R)
    raw1 = place("raw1", [P, KD, HID])
    rawr = place("rawr", [P, KD, RHID])
    flo = place("flo", [ZF, HID], F32R)
    W1 = [place(f"W1_{i}", [P, 2, EB, P], F32R) for i in range(2)]
    WR = place("WR", [P, 2, RB, P], F32R)
    rW2p = place("rW2p", [P, RB, 32])
    b1r = place("b1r", [P, RB])
    b1e = place("b1e", [P, E, EB])
    rb2b = place("rb2b", [P, E])
    lo_at = [at[0] + EB * D * 4]
    W2 = [place("W2_0", [P, 2, EB, D], F32R)]
    raw2 = [place("raw2_0", [P, EB, D], over=lo_at)]
    L = place("L", [P, NT, E])
    Lx = place("Lx", [P, NT, E])
    Ls = place("Ls", [P, 2, NT])
    prob = place("prob", [P, NT, E])
    rank = place("rank", [P, NT, E])
    wgt = place("wgt", [P, NT, E])
    over_k, over_p = [at[0]], [at[0] + 2 * UH * SEQ * 4]
    UK = [place(f"UK{i}", [P, UH, SEQ], F32R) for i in range(2)]
    PQ = [place(f"PQ{i}", [P, 4, PT]) for i in range(2)]
    acc_at = list(over_k)
    acc = place("acc", [P, NT, D], over=over_k)
    lo_at = [over_k[0] + EB * D * 4]
    W2.append(place("W2_1", [P, 2, EB, D], F32R, over=over_k))
    raw2.append(place("raw2_1", [P, EB, D], over=lo_at))
    rh_at = list(over_p)
    rh = [place(f"rh{i}", [P, RB, SEQ], over=over_p) for i in range(2)]
    hbuf = [place(f"h{i}", [P, SEQ], over=over_p) for i in range(2)]
    hl_at = list(over_p)
    hl = [place(f"hl{i}", [P, 2, SEQ], F32R, over=over_p) for i in range(3)]
    LG = place("LG", [P, SEQ], over=over_p)
    assert hl_at[0] + NT * XR * 4 <= over_p[0]
    cmp_a = place("cmp_a", [P, NT, E, E], over=over_p)
    cmp_b = place("cmp_b", [P, NT, E, E], over=over_p)
    assert over_k[0] <= at[0] - 2 * 4 * PT * 4 and over_p[0] <= at[0]
    lo_at = [acc_at[0] + EB * D * 4]
    W2.append(place("W2_2", [P, 2, EB, D], F32R, over=acc_at))
    raw2.append(place("raw2_2", [P, EB, D], over=lo_at))
    hs = place("hs", [P, EB, 2, TS], F32R, over=rh_at)
    xe = [place("xe1", [P, NT, XR], over=dead_at),
          nc.alloc_sbuf_tensor_at("xe2", [P, NT, XR], F32, offset=rows_at0),
          nc.alloc_sbuf_tensor_at("xe3", [P, NT, XR], F32, offset=hl_at[0])]
    tile_rows = [place(f"tile_rows{i}", [P, 2, 2 * ZR], over=dead_at) for i in range(2)]
    Xt = place("Xt", [P, 2, TS], F32R, over=dead_at)
    Yo = [place(f"Yo{i}", [P, 2, D], over=dead_at) for i in range(2)]
    scrap = place("scrap", [P, 2], over=dead_at)
    ids = place("ids", [P, 2], I32, over=dead_at)
    dest = place("dest", [P, NT, E - 1], over=dead_at)
    dest_s = place("dest_s", [P, 3, NT], over=dead_at)
    dest_i = place("dest_i", [P, 2, NT], I32, over=dead_at)
    more = place("more", [1, E - 1, TILES - MIN_TILES], over=dead_at)
    tiles_f = place("tiles_f", [1, E - 1], over=dead_at)
    last_i = place("last_i", [1, E - 1], I32, over=dead_at)
    assert dead_at[0] <= dead_end
    X = nc.dram_tensor("expert_rows", ((E - 1) * TOK, XR), F32, kind="Internal").ap()
    stream = nc.dram_tensor("stream", (TOK + TS, D), F32, kind="Internal").ap()

    psS = nc.alloc_psum_tensor("psS", [P, 2, 512], F32)
    psT = nc.alloc_psum_tensor("psT", [P, 4, 512], F32)
    psV = nc.alloc_psum_tensor("psV", [P, 512], F32)
    psM = nc.alloc_psum_tensor("psM", [P, 512], F32)
    psM4 = psM[:, :].rearrange("p (t c) -> p t c", c=P)
    psM2 = psM[:, :].rearrange("p (t c) -> p t c", c=D)

    sem = lambda name: nc.alloc_semaphore(name)
    idx_in, bases_in, wqkv_in, wproj_in = sem("idx_in"), sem("bases_in"), sem("wqkv_in"), sem("wproj_in")
    rawr_in, raw1_in, raw2_in, small_in = sem("rawr_in"), sem("raw1_in"), sem("raw2_in"), sem("small_in")
    be2_in, last_in, raw2_late = sem("be2_in"), sem("last_in"), sem("raw2_late")
    rows_in = [sem(f"rows_in{b}") for b in range(BATCH)]
    consts = sem("consts")
    zeroed = sem("zeroed")
    dve_link = sem("dve_link")
    pool_link = sem("pool_link")
    bases_ready = sem("bases_ready")
    misc_written, misc_read = sem("misc_written"), sem("misc_read")
    logit_shift, base_exp, coeff_ready = sem("logit_shift"), sem("base_exp"), sem("coeff_ready")
    rstd_ready, ke_ready, vst_ready = sem("rstd_ready"), sem("ke_ready"), sem("vst_ready")
    keys_ready, qh_ready = sem("keys_ready"), sem("qh_ready")
    s_ready, max_done, mexp_ready = sem("s_ready"), sem("max_done"), sem("mexp_ready")
    t_ready, exp_done, mask_done, pv_done = sem("t_ready"), sem("exp_done"), sem("mask_done"), sem("pv_done")
    zs_done, rstd2_ready, zab_ready = sem("zs_done"), sem("rstd2_ready"), sem("zab_ready")
    hi_ready, lo_ready = sem("hi_ready"), sem("lo_ready")
    w1_filled = [sem(f"w1_filled{f}") for f in range(E + 1)]
    w2_hi, w2_lo = sem("w2_hi"), sem("w2_lo")
    up_ready, gelu_done, logits_ready, lg_done = sem("up_ready"), sem("gelu_done"), sem("logits_ready"), sem("lg_done")
    rl_ready, rexp_done, w_ready = sem("rl_ready"), sem("rexp_done"), sem("w_ready")
    split_done, down_done, comb_done = sem("split_done"), sem("down_done"), sem("comb_done")
    places_ready, rows_ready, tiles_ready = sem("places_ready"), sem("rows_ready"), sem("tiles_ready")
    pads_in, scattered, stream_in = sem("pads_in"), sem("scattered"), sem("stream_in")
    of = lambda name: {e: sem(f"{name}{e}") for e in range(1, E)}
    x_in, xt_written, xt_read = of("x_in"), of("xt_written"), of("xt_read")
    s_up, s_gelu, s_split, s_down = of("s_up"), of("s_gelu"), of("s_split"), of("s_down")
    hi_done, tile_in = of("hi_done"), of("tile_in")
    y_free, id_ready, added = of("y_free"), of("id_ready"), of("added")
    stored = sem("stored")

    N_UP_R = RB * BATCH
    fold_before = {("fold", f, ch): n for n, (_, f, ch) in enumerate(i for i in misc_at if i[0] == "fold")}

    def tile_counts(eng):
        eng.wait_ge(tiles_ready, 1)
        last = {e: eng.value_load(last_i[0:1, TURN[e]:TURN[e] + 1], min_val=MIN_TILES - 1, max_val=TILES - 1) for e in range(1, E)}
        return last, {e: last[e] + 1 for e in last}

    def upto(tile, each, more=0):
        m, n = tile
        return m * each + (n * each + more)

    FIRST = (0, 0)

    with nc.Block() as block:

        @block.sync
        def _(sp):
            with nc.allow_non_contiguous_dma("token ids by tile; small vectors"):
                sp.dma_start(idx[:, :], x.rearrange("b (t p) -> p (b t)", p=P)).then_inc(idx_in, 16)
                for p0 in (0, 4 * HEADS):
                    sp.dma_start(raw_b[p0:p0 + NB, 0, :], base_w).then_inc(bases_in, 16)
                    sp.dma_start(raw_b[p0:p0 + NB, 1, :], lang_w).then_inc(bases_in, 16)
                    sp.dma_start(raw_b[p0:p0 + NB, 2, :],
                                 lang_w[LANG:LANG + 1, :].broadcast_to([NB, D])).then_inc(bases_in, 16)
                sp.wait_ge(rows_in[0], 16 * TB)
                sp.dma_start(wproj[:, :, :], w_proj.rearrange("(k p) n -> p k n", p=P)).then_inc(wproj_in, 16)
                sp.dma_start(rawr[:, :, :], rW1.rearrange("(k p) n -> p k n", p=P)).then_inc(rawr_in, 16)
                sp.dma_start(raw1[:, :, :], We1[TURN[0]].rearrange("(k p) n -> p k n", p=P)).then_inc(raw1_in, 16)
                sp.wait_ge(zeroed, 2)
                sp.dma_start(M2[ZF:ZF + E, :], be2).then_inc(be2_in, 16)
                sp.dma_start(rW2p[:, :, 0:E], rW2.rearrange("(p b) n -> p b n", b=RB)).then_inc(small_in, 16)
                sp.dma_start(b1r[:, :], rb1.rearrange("(p b) -> p b", b=RB)).then_inc(small_in, 16)
                sp.dma_start(b1e[:, :, :], be1.rearrange("e (p b) -> p e b", b=EB)).then_inc(small_in, 16)
                sp.dma_start(rb2b[:, :], rb2.rearrange("(o n) -> o n", o=1).broadcast_to([P, E])).then_inc(small_in, 16)
                sp.dma_start(raw2[0][:, :, :], We2[TURN[0]].rearrange("(p b) n -> p b n", b=EB)).then_inc(raw2_in, 16)
            def spread(f):
                dst = (WR if f == 0 else W1[(f - 1) % 2])
                chunks = 1 if f == 0 else 2
                done = 1 + 2 * (f - 1) if f else 0
                sp.wait_ge(lo_ready, done + chunks)
                d = dst[:, :, :, :].rearrange("p a b c -> p a (b c)").bitcast(F32)
                src = flo[:, 0:chunks * 512].bitcast(F32)
                sp.dma_start(d[0:ZF, 1, :], d[0:ZF, 0, :]).then_inc(w1_filled[f], 16)
                sp.dma_start(d[ZF:ZR, 0, :], src[0:ZF // 2, :]).then_inc(w1_filled[f], 16)
                sp.dma_start(d[ZF:ZR, 1, :], src[ZF // 2:ZF, :]).then_inc(w1_filled[f], 16)

            def load_raw1(e):
                sp.dma_start(raw1[:, :, :], We1[TURN[e]].rearrange("(k p) n -> p k n", p=P)).then_inc(raw1_in, 16)

            def load_raw2(e):
                sp.dma_start(raw2[W2_OF[e]][:, :, :], We2[TURN[e]].rearrange("(p b) n -> p b n", b=EB)).then_inc(raw2_in, 16)

            spread(0)
            spread(1)
            load_raw1(1)
            spread(2)
            load_raw1(2)
            sp.wait_ge(consts, 6)
            for e in range(1, E):
                for k in range(2):
                    sp.dma_start(X[TOK * (e - 1):TOK * e, :].rearrange("(n s p) c -> p n s c", s=2, p=P)[:, :, k, :],
                                 pad[:, k:k + 1, :].broadcast_to([P, TILES, XR])).then_inc(pads_in, 16)
            sp.wait_ge(t_ready, 12 * UNITS)
            load_raw2(1)

            def store_stream(c):
                sp.wait_ge(comb_done, TB * (c + 1))
                sp.dma_start(stream[SEQ * c:SEQ * (c + 1), :].rearrange("(t p) d -> p t d", p=P),
                             acc[:, TB * c:TB * (c + 1), :]).then_inc(stream_in, 16)

            def load_tile(e, row):
                sp.dma_start(tile_rows[e % 2][:, :, :], X[bass.ds(row + TOK * TURN[e], TS), 0:2 * ZR].rearrange(
                    "(k p) c -> p k c", p=P)).then_inc(tile_in[e], 16)

            store_stream(0), store_stream(1)
            sp.wait_ge(scattered, 16 * 2 * NT)
            load_tile(1, 0), load_tile(2, 0)
            store_stream(2)
            last, tiles = tile_counts(sp)
            for e in range(1, E):
                if e == 3:
                    sp.wait_ge(xt_written[1], tiles[1])
                    load_tile(3, 0)
                with sp.If(last[e] > 0):
                    with sp.Fori(0, last[e]) as m:
                        sp.wait_ge(xt_written[e], m + 1)
                        load_tile(e, m * TS + TS)
                if e < E - 1:
                    spread(e + 2)
                if e == 1:
                    load_raw1(3)
            sp.wait_ge(added[3], 16 + 32 * tiles[3])
            out_t = out.rearrange("b t d -> (b t) d")
            for c in range(BATCH):
                sp.dma_start(out_t[SEQ * c:SEQ * (c + 1), :], stream[SEQ * c:SEQ * (c + 1), :]).then_inc(stored, 16)
            sp.wait_ge(stored, 16 * BATCH)

        @block.gpsimd
        def _(pool):
            links = [0]

            def link(ins):
                links[0] += 1
                ins.then_inc(pool_link, 1)
                pool.wait_ge(pool_link, links[0])

            g = nc.gpsimd

            def gather(b):
                for t in range(TB * b, TB * (b + 1)):
                    pool.indirect_dma_start(gathered[:, t, :], None, coeff_w,
                                            bass.IndirectOffsetOnAxis(ap=idx[:, t:t + 1], axis=0)
                                            ).then_inc(rows_in[b], 16)

            g.memset(minus_half[:, :], -0.5)
            g.memset(head_mask[:, :], 1.0)
            g.memset(lo_rows8[:, :], 1.0)
            link(g.memset(ident[:, :], 0.0))
            g.affine_select(out=ident[:, :], in_=ident[:, :], compare_op=ALU.not_equal, fill=1.0, base=0,
                            pattern=[[-1, P]], channel_multiplier=1).then_inc(consts, 1)
            g.affine_select(out=lo_rows8[:, :], in_=lo_rows8[:, :], compare_op=ALU.is_ge, fill=0.0,
                            base=-2 * NB, pattern=[[-ROWS, UH]], channel_multiplier=1)
            link(g.affine_select(out=head_mask[:, :], in_=head_mask[:, :], compare_op=ALU.is_ge, fill=0.0, base=0,
                                 pattern=[[-ROWS, UH]], channel_multiplier=1))
            g.affine_select(out=head_mask[:, :], in_=head_mask[:, :], compare_op=ALU.is_ge, fill=0.0,
                            base=ROWS - 1, pattern=[[ROWS, UH]], channel_multiplier=-1).then_inc(consts, 1)
            g.affine_select(out=lo_rows8[:, :], in_=lo_rows8[:, :], compare_op=ALU.is_ge, fill=0.0,
                            base=3 * NB - 1, pattern=[[ROWS, UH]], channel_multiplier=-1).then_inc(consts, 1)
            pool.wait_ge(idx_in, 16)
            gather(0)
            g.memset(ident_b[:, :], 0.0)
            link(g.memset(neg_mask[:, :], 0.0))
            g.affine_select(out=ident_b[:, :], in_=ident_b[:, :], compare_op=ALU.not_equal, fill=1.0, base=0,
                            pattern=[[-1, P]], channel_multiplier=1)
            g.affine_select(out=neg_mask[:, :], in_=neg_mask[:, :], compare_op=ALU.is_ge, fill=NEG, base=0,
                            pattern=[[0, 2], [-1, P]], channel_multiplier=1).then_inc(consts, 1)

            def more_consts():
                g.memset(mexp[:, :, :, :], 0.0)
                g.memset(Vst[0][:, :, :], 0.0)
                link(g.memset(Vst[1][:, :, :], 0.0))
                for i in range(2):
                    last = g.memset(Vst[i][:, :, :].rearrange("p t (r s) -> p t r s", s=40)[:, :, :, NB:NB + 1], 1.0)
                last.then_inc(consts, 1)
                g.memset(ones[:, :], 1.0)
                g.memset(tri[:, :, :, :], 1.0)
                link(g.memset(below[:, :], 1.0))
                g.affine_select(out=tri[:, :, :, :], in_=tri[:, :, :, :], compare_op=ALU.is_ge, fill=0.0, base=-1,
                                pattern=[[0, NT], [1, E], [-1, E]], channel_multiplier=0)
                g.affine_select(out=below[:, :], in_=below[:, :], compare_op=ALU.is_ge, fill=0.0, base=-1,
                                pattern=[[1, P]], channel_multiplier=-1)
                for e in range(1, E):
                    g.memset(region_far[:, :, e - 1:e], FAR + TOK * (e - 1))
                for m in range(MIN_TILES, TILES):
                    g.memset(limits[:, :, m - MIN_TILES:m - MIN_TILES + 1], float(TS * m))
                g.memset(no_id[:, :], 0)
                link(g.memset(pad[:, :, :], 0.0))
                g.iota(pad[:, :, 2 * ZR:2 * ZR + 1].bitcast(I32), pattern=[[P, 2], [0, 1]], base=TOK, channel_multiplier=1
                       ).then_inc(consts, 1)

            def inverse_root(pair, src, scale):
                link(nc.gpsimd.tensor_scalar(pair[:, 0, :], src, scale, EPS, ALU.mult, ALU.add))
                return nc.gpsimd.tensor_tensor(pair[:, 1, :], pair[:, 0, :], minus_half[:, :], ALU.pow)

            def second_lo(e):
                pool.wait_ge(w2_hi, e + 1)
                nc.gpsimd.tensor_tensor(W2[W2_OF[e]][:, 1, :, :], raw2[W2_OF[e]][:, :, :],
                                        W2[W2_OF[e]][:, 0, :, :].bitcast(F32), ALU.subtract).then_inc(w2_lo, 1)

            for item in order:
                kind = item[0]
                if kind == "gather":
                    gather(item[1])
                elif kind == "consts":
                    more_consts()
                elif kind == "rstd":
                    b = item[1]
                    pool.wait_ge(misc_read, misc_at[("H", b, 1)] + 1)
                    if b:
                        pool.wait_ge(ke_ready, b)
                    inverse_root(rstd, sq[:, :], 1.0 / D).then_inc(rstd_ready, 1)
                elif kind == "rstd2":
                    b = item[1]
                    pool.wait_ge(misc_read, misc_at[("H2", b, 1)] + 1)
                    if b:
                        pool.wait_ge(zab_ready, b)
                    inverse_root(rstd2, sq2[:, :], 1.0 / D).then_inc(rstd2_ready, 1)
                elif kind == "variants":
                    b = item[1]
                    pool.wait_ge(misc_read, misc_at[("KT", b)] + 1)
                    if b >= 2:
                        pool.wait_ge(t_ready, 12 * 2 * (b - 1))
                    for h in range(UH):
                        nc.gpsimd.tensor_scalar(UK[b % 2][:, h, :], KTs[:, :], head_mask[:, h:h + 1], 1.0,
                                                ALU.mult, ALU.mult).then_inc(keys_ready, 1)
                elif kind == "T" and item[2] % 3:
                    _, u, k = item
                    q, j = 2 * u + k // 6, 2 * ((k % 6) // 3)
                    pool.wait_ge(exp_done, 12 * u + k + 1)
                    for kb in PV_ORDER[:3] if k % 3 == 1 else PV_ORDER[3:]:
                        d = PQ[q % 2][:, j:j + 2, KB_AT[kb][0]:KB_AT[kb][0] + P]
                        nc.gpsimd.affine_select(out=d, in_=d, compare_op=ALU.is_ge, fill=0.0, base=0,
                                                pattern=[[0, 2], [1, P]], channel_multiplier=-1
                                                ).then_inc(mask_done, 1)
                elif kind == "places":
                    pool.wait_ge(w_ready, 1)
                    nc.gpsimd.iota(rows[:, :, 2 * ZR:2 * ZR + 1].bitcast(I32), pattern=[[P, NT], [0, 1]], base=0,
                                   channel_multiplier=1).then_inc(rows_ready, 1)
                    pool.wait_ge(rows_ready, 1)
                    pool.wait_ge(places_ready, 1)
                    pool.wait_ge(pads_in, 16 * 2 * (E - 1))
                    for t in range(NT):
                        for k in range(2):
                            pool.indirect_dma_start(X, bass.IndirectOffsetOnAxis(ap=dest_i[:, k, t:t + 1], axis=0),
                                                    rows[:, t, :], None, bounds_check=(E - 1) * TOK - 1,
                                                    oob_is_err=False).then_inc(scattered, 16)
                elif kind == "w2":
                    second_lo(item[1])

            last, tiles = tile_counts(pool)
            for e, (c0, c1) in enumerate(((0, 64), (64, 128), (128, D)), 1):
                pool.dma_start(stream[TOK:TOK + TS, c0:c1].rearrange("(s p) c -> p s c", p=P), pad[:, :, 0:c1 - c0]
                               ).then_inc(added[e], 16)
            for e in range(1, E):
                pool.wait_ge(added[e], 16)

            def load_rows(e):
                pool.dma_start(xe[e - 1][:, :, :], X[TOK * TURN[e]:TOK * (TURN[e] + 1), :].rearrange(
                    "(t p) c -> p t c", p=P)).then_inc(x_in[e], 16)

            def load_raw2(e):
                pool.dma_start(raw2[W2_OF[e]][:, :, :], We2[TURN[e]].rearrange("(p b) n -> p b n", b=EB)
                               ).then_inc(raw2_late, 16)

            pool.wait_ge(scattered, 16 * 2 * NT)
            load_rows(1)
            pool.wait_ge(down_done, BATCH * EB)
            load_raw2(2)
            pool.wait_ge(comb_done, TB * BATCH)
            pool.dma_start(stream[SEQ * 3:SEQ * 4, :].rearrange("(t p) d -> p t d", p=P), acc[:, TB * 3:TB * 4, :]
                           ).then_inc(last_in, 16)
            pool.wait_ge(stream_in, 16 * (BATCH - 1))
            pool.wait_ge(last_in, 16)
            load_rows(2)
            load_raw2(3), load_rows(3)

            def add_tile(e, m):
                pool.wait_ge(y_free[e], m + 3)
                nc.gpsimd.tensor_tensor(ids[:, :], xe[e - 1][:, bass.ds(2 * m, 2), 2 * ZR].bitcast(I32), no_id[:, :],
                                        ALU.add).then_inc(id_ready[e], 1)
                pool.wait_ge(id_ready[e], m + 1)
                for k in range(2):
                    pool.indirect_dma_start(stream, bass.IndirectOffsetOnAxis(ap=ids[:, k:k + 1], axis=0), Yo[e % 2][:, k, :],
                                            None, bounds_check=m + (TOK + TS - 1), compute_op=ALU.add
                                            ).then_inc(added[e], 16)

            for e in range(1, E):
                if e > 1:
                    pool.wait_ge(added[e - 1], 16 + 32 * tiles[e - 1])
                    link(nc.gpsimd.tensor_tensor(ids[:, :], no_id[:, :], no_id[:, :], ALU.add))
                if e < E - 1:
                    second_lo(e + 1)
                pool.wait_ge(x_in[e], 16)
                with pool.Fori(0, tiles[e]) as m:
                    add_tile(e, m)

        @block.tensor
        def _(pe):
            mm = nc.tensor.matmul

            def misc_begin(item):
                if misc_at[item]:
                    pe.wait_ge(misc_read, misc_at[item])

            def turn(src, rows, cols, n=TB):
                for t in range(n):
                    last = nc.tensor.transpose(psM[0:cols, P * t:P * t + rows], src(t), ident[0:rows, 0:rows])
                return last

            def fold(item):
                _, f, ch = item
                if f == 0:
                    pe.wait_ge(rawr_in, 16)
                    src = rawr
                else:
                    pe.wait_ge(raw1_in, 16 * f)
                    src = raw1
                for k in range(KD):
                    last = mm(psM[0:ZF, :], McT[:, k, :], src[:, k, 512 * ch:512 * (ch + 1)],
                              start=(k == 0), stop=(k == KD - 1))
                last.then_inc(misc_written, 1)

            pe.wait_ge(consts, 1)
            for item in order:
                kind = item[0]
                if kind in MISC:
                    misc_begin(item)
                if kind == "BcT":
                    pe.wait_ge(bases_ready, 1)
                    for k in range(KD):
                        last = nc.tensor.transpose(psM[:, P * k:P * k + NB], Bcr[0:NB, P * k:P * (k + 1)],
                                                   ident[0:NB, 0:NB])
                    last.then_inc(misc_written, 1)
                elif kind == "QKV":
                    pe.wait_ge(wqkv_in, 16)
                    for j in range(6):
                        for k in range(KD):
                            last = mm(psM[:, NB * j:NB * j + NB], wqkv[:, k, P * j:P * (j + 1)], BcT[:, k, :],
                                      start=(k == 0), stop=(k == KD - 1))
                    last.then_inc(misc_written, 1)
                elif kind == "Arep":
                    pe.wait_ge(bases_ready, 2)
                    for g in range(2):
                        last = mm(psM4[:, g, :], QBpad[:, g, :], KBexp[:, g, :, :].rearrange("p h r -> p (h r)"),
                                  start=True, stop=True)
                    last.then_inc(misc_written, 1)
                elif kind == "M":
                    pe.wait_ge(wproj_in, 16)
                    pe.wait_ge(bases_ready, 3)
                    for g in range(2):
                        last = mm(psM[0:4 * HEADS, 0:D], VBexp[:, g, :], wproj[:, g, :], start=(g == 0), stop=(g == 1))
                    last.then_inc(misc_written, 1)
                elif kind == "McT":
                    pe.wait_ge(bases_ready, 4)
                    turn(lambda k: M2c[0:ZF, P * k:P * (k + 1)], ZF, P, KD).then_inc(misc_written, 1)
                elif kind == "fold":
                    fold(item)
                elif kind == "places":
                    pe.wait_ge(w_ready, 1)
                    pe.wait_ge(consts, 6)
                    mm(psM[:, 0:NT * E], below[:, :], rank[:, :, :].rearrange("p t e -> p (t e)"), start=True, stop=False,
                       skip_group_check=True)
                    for t in range(NT):
                        last = mm(psM[:, E * (t + 1):E * (NT + 1)].rearrange("p (t e) -> p t e", e=E), ones[:, :],
                                  rank[:, t:t + 1, :].broadcast_to([P, NT - t, E]), start=False, stop=(t == NT - 1),
                                  skip_group_check=True)
                    last.then_inc(misc_written, 1)
                elif kind == "CT":
                    pe.wait_ge(coeff_ready, item[1] + 1)
                    turn(lambda t: CP[:, t, :], P, P).then_inc(misc_written, 1)
                elif kind == "H":
                    for t in range(2):
                        c0 = P * (2 * item[2] + t)
                        last = mm(psM2[:, t, :], CTs[:, c0:c0 + P], Bcr[:, :], start=True, stop=True)
                    last.then_inc(misc_written, 1)
                elif kind == "KT":
                    pe.wait_ge(ke_ready, item[1] + 1)
                    turn(lambda t: KE8[:, t, :, :].rearrange("p h r -> p (h r)"), P, P).then_inc(misc_written, 1)
                elif kind == "QA":
                    mm(psM[:, :], Arep[:, item[2], :], KTs[:, :], start=True, stop=True).then_inc(misc_written, 1)
                elif kind == "shift":
                    pe.wait_ge(mexp_ready, item[1] + 1)
                    turn(lambda t: mexp[:, t, :, :].rearrange("p h r -> p (h r)"), P, P).then_inc(misc_written, 1)
                elif kind == "ZT":
                    pe.wait_ge(zs_done, item[1] + 1)
                    turn(lambda t: Zs[:, P * t:P * (t + 1)], P, P).then_inc(misc_written, 1)
                elif kind == "ZF":
                    turn(lambda t: Z[:, TB * item[1] + t, :], P, P).then_inc(misc_written, 1)
                elif kind in ("H2", "FH"):
                    pe.wait_ge(be2_in, 16)
                    for t in range(2):
                        c0 = P * (2 * item[2] + t)
                        last = mm(psM2[:, t, :], ZTs[:, c0:c0 + P], (M2c if kind == "H2" else M2)[:, :], start=True, stop=True)
                    last.then_inc(misc_written, 1)
                elif kind == "ZA":
                    if item[2] == 0:
                        pe.wait_ge(zab_ready, item[1] + 1)
                    turn(lambda t: rows[:, TB * item[1] + t, ZR * item[2]:ZR * (item[2] + 1)], P, ZR).then_inc(misc_written, 1)
                elif kind == "S":
                    _, u, k = item
                    b, g = u // 2, u % 2
                    n = 20 * u + k
                    if k == 0:
                        pe.wait_ge(misc_read, misc_at[("QA", b, g)] + 1)
                        if u == 0:
                            pe.wait_ge(consts, 4)
                    if n >= 2:
                        pe.wait_ge(max_done, n - 1)
                    ps = psS[:, n % 2, :]
                    h = 4 * (k // 10) + 2 * ((k % 10) // 5)
                    kk = k % 5
                    if g == 0:
                        pe.wait_ge(keys_ready, UH * b + min(h + 1 + kk // 2, h + 2))

                    def score(cols, head, qb, width, start):
                        mm(cols, RQ1[g][:, P * qb:P * (qb + 1)], UK[b % 2][:, head, 0:width], start=start, stop=False,
                           skip_group_check=True)
                    def diagonal(cols):
                        return mm(cols, ident_b[:, :], neg_mask[:, 0:P], start=False, stop=True, skip_group_check=True)

                    if kk in (0, 2):
                        score(ps, h + kk // 2, 3, 512, True)
                        last = diagonal(ps[:, 384:512])
                    elif kk in (1, 3):
                        score(ps[:, 0:256], h + kk // 2, 0, 256, True)
                        diagonal(ps[:, 0:128])
                        score(ps[:, 128:512], h + kk // 2, 2, 384, True)
                        last = diagonal(ps[:, 384:512])
                    else:
                        score(ps[:, 0:256], h, 1, 256, True)
                        score(ps[:, 256:512], h + 1, 1, 256, False)
                        ends = ps.rearrange("p (n c) -> p n c", c=P)[:, 1:4:2, :]
                        last = mm(ends, ident_b[:, :], neg_mask[:, :].rearrange("p (n c) -> p n c", c=P),
                                  start=False, stop=True, skip_group_check=True)
                    last.then_inc(s_ready, 1)
                elif kind == "T":
                    _, u, k = item
                    b, g = u // 2, u % 2
                    n = 12 * u + k
                    if k == 0:
                        pe.wait_ge(misc_read, misc_at[("shift", u)] + 1)
                    if n >= 2:
                        pe.wait_ge(exp_done, n - 1)
                    ps = psT[:, 2 * (n % 2):2 * (n % 2) + 2, :]
                    h = 4 * (k // 6) + 2 * ((k % 6) // 3)

                    def score(cols, head, kb, q0):
                        return mm(cols, UK[b % 2][:, head, P * kb:P * (kb + 1)], RQ2[g][:, q0:SEQ], start=True,
                                  stop=True, skip_group_check=True)
                    if k % 3 < 2:
                        h += k % 3
                        score(ps[:, 0, :], h, 0, 0)
                        score(ps[:, 1, 256:512], h, 3, 256)
                        last = score(ps[:, 1, 0:384], h, 1, 128)
                    else:
                        score(ps[:, 0, 0:256], h, 2, 256)
                        last = score(ps[:, 0, 256:512], h + 1, 2, 256)
                    last.then_inc(t_ready, 1)
                elif kind == "PV":
                    _, q, kb = item
                    b, r = q // 4, q % 4
                    n = PV_ORDER.index(kb)
                    pe.wait_ge(mask_done, 8 * q + 4 + n + 1)
                    if kb == 0:
                        pe.wait_ge(vst_ready, b + 1)
                        if r == 0 and b:
                            pe.wait_ge(zs_done, b)
                    c0, c1 = KB_AT[kb]
                    for j in range(4):
                        last = mm(psV[32 * j:32 * j + 32, P * kb:SEQ], Vst[b % 2][:, kb, 32 * r:32 * r + 32],
                                  PQ[q % 2][:, j, c0:c1], start=(r == 0 and kb == 0), stop=(r == 3 and n == 3),
                                  skip_group_check=True)
                    if n == 3:
                        last.then_inc(pv_done, 1)
                elif kind == "up":
                    i = item[1]
                    if i == 0:
                        pe.wait_ge(max_done, 20 * UNITS)
                    if i < N_UP_R:
                        c, b, w = i // RB, i % RB, WR
                        if b == 0:
                            pe.wait_ge(misc_read, misc_at[("ZA", c, 1)] + 1)
                        if i == 0:
                            pe.wait_ge(w1_filled[0], 48)
                    else:
                        j = i - N_UP_R
                        e, c, b = j // (BATCH * EB), j // EB % BATCH, j % EB
                        w = W1[e % 2]
                        if c == 0 and b == 0:
                            pe.wait_ge(w1_filled[e + 1], 48)
                    if i >= 2:
                        pe.wait_ge(gelu_done, i - 1)
                    for a in range(2):
                        last = mm(psS[:, i % 2, :], w[0:ZR, a, b, :], ZAB[0:ZR, a, SEQ * c:SEQ * (c + 1)],
                                  start=(a == 0), stop=(a == 1))
                    last.then_inc(up_ready, 1)
                elif kind == "logits":
                    c = item[1]
                    pe.wait_ge(gelu_done, RB * (c + 1))
                    if c == 0:
                        pe.wait_ge(small_in, 64)
                        pe.wait_ge(exp_done, 12 * UNITS)
                    for b in range(RB):
                        last = mm(psT[32 * b:32 * b + 32, c, :], rW2p[:, b, :], rh[c % 2][:, b, :], start=True, stop=True)
                    last.then_inc(logits_ready, 1)
                elif kind == "LT":
                    pe.wait_ge(lg_done, item[1] + 1)
                    turn(lambda t: LG[:, P * t:P * (t + 1)], P, P).then_inc(misc_written, 1)
                elif kind == "FZ":
                    pe.wait_ge(w_ready, 1)
                    turn(lambda t: Z[:, TB * item[1] + t, :], P, P).then_inc(misc_written, 1)
                elif kind == "down":
                    j = item[1]
                    e, ec, b = j // (BATCH * EB), j // EB, j % EB
                    pe.wait_ge(split_done, j + 1)
                    if b == 0:
                        if ec % BATCH == 0:
                            pe.wait_ge(w2_lo, e + 1)
                        if ec == 0:
                            pe.wait_ge(lg_done, BATCH)
                        if ec >= 2:
                            pe.wait_ge(comb_done, TB * (ec - 1))
                    hi, lo = hl[j % 3][:, 0, :], hl[j % 3][:, 1, :]
                    w = W2[e % 2]
                    for t in range(TB):
                        o = psT[:, 2 * (ec % 2) + t // 2, D * (t % 2):D * (t % 2 + 1)]
                        c0 = P * t
                        mm(o, hi[:, c0:c0 + P], w[:, 0, b, :], start=(b == 0 and t % 2 == 0), stop=False,
                           skip_group_check=True)
                        mm(o, hi[:, c0:c0 + P], w[:, 1, b, :], start=False, stop=False, skip_group_check=True)
                        last = mm(o, lo[:, c0:c0 + P], w[:, 0, b, :], start=False, stop=(b == EB - 1),
                                  skip_group_check=True)
                    last.then_inc(down_done, 1)

            last, tiles = tile_counts(pe)

            def turn_rows(e, i):
                if i is FIRST:
                    pe.wait_ge(misc_read, len(misc_at) - len(LATE) + 2 * (e - 1))
                    if e > 1:
                        pe.wait_ge(xt_read[e - 1], tiles[e - 1])
                else:
                    pe.wait_ge(xt_read[e], upto(i, 1))
                pe.wait_ge(tile_in[e], upto(i, 16, 16))
                for a in range(2):
                    for k in range(2):
                        done = nc.tensor.transpose(psM[0:ZR, TS * a + P * k:TS * a + P * (k + 1)],
                                                   tile_rows[e % 2][:, k, ZR * a:ZR * (a + 1)], ident[:, :])
                done.then_inc(xt_written[e], 1)

            def up(e, i, b):
                if b == 0:
                    pe.wait_ge(xt_read[e], upto(i, 1, 1))
                if i is not FIRST or b >= 2:
                    pe.wait_ge(s_gelu[e], upto(i, EB, b - 1))
                elif e > 1:
                    pe.wait_ge(s_gelu[e - 1], EB * tiles[e - 1])
                else:
                    pe.wait_ge(gelu_done, N_UP_R + BATCH * EB)
                for a in range(2):
                    done = mm(psS[:, b % 2, 0:TS], W1[e % 2][0:ZR, a, b, :], Xt[0:ZR, a, :],
                              start=(a == 0), stop=(a == 1))
                done.then_inc(s_up[e], 1)

            def down(e, m, b):
                pe.wait_ge(s_split[e], upto(m, EB // 2, b // 2 + 1))
                if b == 0:
                    pe.wait_ge(y_free[e], upto(m, 1, 1))
                for k in range(2):
                    o = psT[:, bass.ds(upto(m, 1) % 2 + 2 * (e % 2), 1), D * k:D * (k + 1)].rearrange("p o c -> p (o c)")
                    for n, (x, w) in enumerate(((0, 0), (0, 1), (1, 0))):
                        done = mm(o, hs[:, b, x, P * k:P * (k + 1)], W2[W2_OF[e]][:, w, b, :],
                                  start=(b == 0 and k == 0 and n == 0), stop=(b == EB - 1 and n == 2), skip_group_check=True)
                done.then_inc(s_down[e], 1)

            def step(new, old):
                if new:
                    turn_rows(*new)
                if old:
                    down(*old, 0), down(*old, 1)
                for b in range(EB):
                    if new:
                        up(*new, b)
                        if new[1] is FIRST and (new[0], b) in FOLD_AT:
                            item = FOLD_AT[new[0], b]
                            pe.wait_ge(misc_read, misc_at[item])
                            fold(item)
                    if old and b + 2 < EB:
                        down(*old, b + 2)

            for e in range(1, E):
                pe.wait_ge(w1_filled[e + 1], 48)
                step((e, FIRST), (e - 1, (last[e - 1], 0)) if e > 1 else None)
                if e < E - 1:
                    pe.wait_ge(misc_read, misc_at[("fold", e + 2, 1)] + 1)
                if e == 1:
                    pe.wait_ge(comb_done, TB * BATCH)
                pe.wait_ge(w2_lo, e + 1)
                with pe.If(last[e] > 0):
                    with pe.Fori(0, last[e]) as m:
                        step((e, (m, 1)), (e, (m, 0)))
            step(None, (E - 1, (last[E - 1], 0)))

        @block.scalar
        def _(act):
            A = nc.scalar.activation

            act.dma_start(wqkv[:, :, :], w_qkv.rearrange("(k p) n -> p k n", p=P)).then_inc(wqkv_in, 16)

            def out_of_misc(item, dst, src):
                act.wait_ge(misc_written, misc_at[item] + 1)
                A(dst, src, ACT.Copy).then_inc(misc_read, 1)

            def fold_hi(item):
                _, f, ch = item
                act.wait_ge(misc_written, misc_at[item] + 1)
                nb = RB if f == 0 else EB
                dst = WR if f == 0 else W1[(f - 1) % 2]
                np_ = 512 // nb
                A(dst[0:ZF, 0, :, np_ * ch:np_ * (ch + 1)],
                  psM[0:ZF, :].rearrange("z (p b) -> z b p", b=nb), ACT.Copy).then_inc(hi_ready, 1)

            for item in order:
                kind = item[0]
                if kind == "soft":
                    act.wait_ge(logit_shift, item[1] + 1)
                    A(soft_x[:, :, :], soft_e[:, :, :], ACT.Exp).then_inc(base_exp, 1)
                elif kind == "CT":
                    out_of_misc(item, CTs[:, :], psM[:, :])
                elif kind == "H":
                    act.wait_ge(misc_written, misc_at[item] + 1)
                    if item[1] and item[2] == 0:
                        act.wait_ge(rstd_ready, item[1])
                    for t in range(2):
                        last = A(psM2[:, t, :], psM2[:, t, :], ACT.Square,
                                 accum_out=sq[:, 2 * item[2] + t:2 * item[2] + t + 1])
                    last.then_inc(misc_read, 1)
                elif kind == "KT":
                    if item[1]:
                        act.wait_ge(keys_ready, UH * item[1])
                    out_of_misc(item, KTs[:, :], psM[:, :])
                elif kind == "QA":
                    act.wait_ge(misc_written, misc_at[item] + 1)
                    A(RQh[:, :], psM[:, :], ACT.Copy).then_inc(qh_ready, 1)
                elif kind == "fold":
                    fold_hi(item)
                elif kind == "T":
                    _, u, k = item
                    n, q = 12 * u + k, 2 * u + k // 6
                    act.wait_ge(t_ready, n + 1)
                    if k % 6 == 0 and q >= 2:
                        act.wait_ge(pv_done, q - 1)
                    j = 2 * ((k % 6) // 3)
                    ps = psT[:, 2 * (n % 2):2 * (n % 2) + 2, :]
                    if k % 3 < 2:
                        A(PQ[q % 2][:, j + k % 3, 0:1024], ps.rearrange("p n c -> p (n c)"), ACT.Exp
                          ).then_inc(exp_done, 1)
                    else:
                        A(PQ[q % 2][:, j:j + 2, 1024:PT], ps[:, 0, :].rearrange("p (n c) -> p n c", c=256), ACT.Exp
                          ).then_inc(exp_done, 1)
                elif kind == "Zs":
                    b = item[1]
                    act.wait_ge(pv_done, 4 * (b + 1))
                    if b:
                        act.wait_ge(misc_written, misc_at[("ZT", b - 1)] + 1)
                    A(Zs[:, :], psV[:, :], ACT.Copy).then_inc(zs_done, 1)
                elif kind == "H2":
                    act.wait_ge(misc_written, misc_at[item] + 1)
                    if item[1] and item[2] == 0:
                        act.wait_ge(rstd2_ready, item[1])
                    for t in range(2):
                        last = A(psM2[:, t, :], psM2[:, t, :], ACT.Square,
                                 accum_out=sq2[:, 2 * item[2] + t:2 * item[2] + t + 1])
                    last.then_inc(misc_read, 1)
                elif kind in ("ZF", "FZ"):
                    out_of_misc(item, ZTs[:, :], psM[:, :])
                elif kind == "ZA":
                    out_of_misc(item, ZAB[0:ZR, item[2], SEQ * item[1]:SEQ * (item[1] + 1)], psM[0:ZR, :])
                elif kind == "FH":
                    t0 = TB * item[1] + 2 * item[2]
                    if item[1] == 0 and item[2] == 0:
                        act.wait_ge(t_ready, 12 * UNITS)
                    out_of_misc(item, acc[:, t0:t0 + 2, :], psM2[:, :, :])
                elif kind == "up":
                    i = item[1]
                    act.wait_ge(up_ready, i + 1)
                    if i == 0:
                        act.wait_ge(pv_done, 2 * UNITS)
                        act.wait_ge(small_in, 64)
                    if i < N_UP_R:
                        c, b = i // RB, i % RB
                        if c >= 2 and b == 0:
                            act.wait_ge(logits_ready, c - 1)
                        A(rh[c % 2][:, b, :], psS[:, i % 2, :], ACT.Gelu, bias=b1r[:, b:b + 1]).then_inc(gelu_done, 1)
                    else:
                        j = i - N_UP_R
                        e, b = j // (BATCH * EB), j % EB
                        if j >= 2:
                            act.wait_ge(split_done, j - 1)
                        A(hbuf[j % 2][:, :], psS[:, i % 2, :], ACT.Gelu, bias=b1e[:, TURN[e], b:b + 1]).then_inc(gelu_done, 1)
                elif kind == "route":
                    act.wait_ge(rl_ready, 1)
                    A(Lx[:, :, :], L[:, :, :], ACT.Exp).then_inc(rexp_done, 1)

            last, tiles = tile_counts(act)

            def copy_rows(e, i):
                act.wait_ge(xt_written[e], upto(i, 1, 1))
                if i is not FIRST:
                    act.wait_ge(s_up[e], upto(i, EB))
                elif e > 1:
                    act.wait_ge(s_up[e - 1], EB * tiles[e - 1])
                A(Xt[0:ZR, :, :], psM[0:ZR, :].rearrange("p (a c) -> p a c", a=2), ACT.Copy).then_inc(xt_read[e], 1)

            def gelu(e, i, b):
                act.wait_ge(s_up[e], upto(i, EB, b + 1))
                if b % 2 == 0:
                    if i is not FIRST or b >= 4:
                        act.wait_ge(s_split[e], upto(i, EB // 2, b // 2 - 1))
                    elif e > 1:
                        act.wait_ge(s_split[e - 1], EB // 2 * tiles[e - 1])
                    else:
                        act.wait_ge(split_done, BATCH * EB)
                A(hbuf[b // 2 % 2][:, TS * (b % 2):TS * (b % 2 + 1)], psS[:, b % 2, 0:TS],
                  ACT.Gelu, bias=b1e[:, TURN[e], b:b + 1]).then_inc(s_gelu[e], 1)

            def outputs(e, m):
                if e > 2:
                    act.wait_ge(added[e - 2], 16 + 32 * tiles[e - 2])
                act.wait_ge(s_down[e], upto(m, EB, EB))
                act.wait_ge(added[e], upto(m, 32, 16))
                for k in range(2):
                    done = A(Yo[e % 2][:, k, :],
                             psT[:, bass.ds(upto(m, 1) % 2 + 2 * (e % 2), 1), D * k:D * (k + 1)].rearrange("p o c -> p (o c)"),
                             ACT.Copy, scale=xe[e - 1][:, bass.ds(upto(m, 2, k), 1), 2 * ZR + 1 + TURN[e]])
                done.then_inc(y_free[e], 1)

            def step(new, old):
                if new:
                    copy_rows(*new)
                for b in range(EB):
                    if new:
                        gelu(*new, b)
                        if new[1] is FIRST and (new[0], b) in FOLD_AT:
                            fold_hi(FOLD_AT[new[0], b])
                    if b == EB - 2 and old:
                        outputs(*old)

            for e in range(1, E):
                for k in range(2):
                    A(scrap[:, k:k + 1], ident[:, 0:1], ACT.Copy).then_inc(y_free[e], 1)
                step((e, FIRST), (e - 1, (last[e - 1], 0)) if e > 1 else None)
                act.wait_ge(x_in[e], 16)
                with act.If(last[e] > 0):
                    with act.Fori(0, last[e]) as m:
                        step((e, (m, 1)), (e, (m, 0)))
            step(None, (E - 1, (last[E - 1], 0)))

        @block.vector
        def _(dve):
            v = nc.vector
            links = [0]

            def link(ins):
                links[0] += 1
                ins.then_inc(dve_link, 1)
                dve.wait_ge(dve_link, links[0])

            def bc(ap, shape):
                return ap.broadcast_to(shape)

            v.memset(M2[:, :], 0.0).then_inc(zeroed, 1)
            v.memset(rW2p[:, :, :], 0.0).then_inc(zeroed, 1)
            v.memset(Bcr[:, :], 0.0).then_inc(zeroed, 1)
            v.memset(CP[:, :, :], 0.0).then_inc(zeroed, 1)
            v.memset(KE[:, :, :], 0.0).then_inc(zeroed, 1)
            v.memset(Z[:, :, :], 0.0)
            dve.wait_ge(zeroed, 5)
            v.memset(KE[:, :, 3 * NB:3 * NB + 2], 1.0)
            v.memset(QBpad[:, :, :], 0.0)
            v.memset(M2c[:, :], 0.0)
            v.memset(KBexp[:, :, :, :], 0.0)
            v.memset(VBexp[:, :, :], 0.0)
            dve.wait_ge(bases_in, 96)
            def base_rows(p0, dst):
                r = slice(p0, p0 + NB)
                v.tensor_tensor(rows_b[r, 0, :], raw_b[r, 0, :], raw_b[r, 1, :], ALU.add)
                link(v.tensor_scalar(rows_b[r, 1, :], raw_b[r, 2, :], 0.1, None, ALU.mult))
                return v.scalar_tensor_tensor(dst[r, :], rows_b[r, 0, :], SCALE_D, rows_b[r, 1, :], ALU.mult, ALU.add)

            def centre(dst, src, rows):
                link(v.tensor_reduce(stat[0:rows, 0:1], src, AX.X, ALU.add))
                link(v.tensor_scalar(stat[0:rows, 1:2], stat[0:rows, 0:1], 1.0 / D, None, ALU.mult))
                return v.tensor_scalar(dst, src, stat[0:rows, 1:2], None, ALU.subtract)

            link(base_rows(0, Bcr))
            centre(Bcr[0:NB, :], Bcr[0:NB, :], NB).then_inc(bases_ready, 1)
            link(base_rows(4 * HEADS, M2))
            dve.wait_ge(consts, 3)
            link(v.tensor_scalar(head_mask_q[:, :], head_mask[:, :], DH ** -0.5, None, ALU.mult))
            link(v.tensor_reduce(neg_lo_rows[:, :], lo_rows8[:, :], AX.X, ALU.add, negate=True))

            def misc_wait(item):
                dve.wait_ge(misc_written, misc_at[item] + 1)

            def fold_lo(item):
                _, f, ch = item
                nb = RB if f == 0 else EB
                np_ = 512 // nb
                dst = WR if f == 0 else W1[(f - 1) % 2]
                dve.wait_ge(hi_ready, fold_before[item] + 1)
                if f >= 1 and ch == 0:
                    dve.wait_ge(w1_filled[f - 1], 48)
                lo = flo[:, 0:512 * (1 if f == 0 else 2)].rearrange("z (b p) -> z b p", b=nb)
                v.tensor_tensor(lo[:, :, np_ * ch:np_ * (ch + 1)],
                                psM[0:ZF, :].rearrange("z (p b) -> z b p", b=nb),
                                dst[0:ZF, 0, :, np_ * ch:np_ * (ch + 1)].bitcast(F32), ALU.subtract
                                ).then_inc(misc_read, 1)
                dve.wait_ge(misc_read, misc_at[item] + 1)
                v.memset(stat[:, 4:5], 0.0).then_inc(lo_ready, 1)

            for item in order:
                kind = item[0]
                if kind == "BcT":
                    misc_wait(item)
                    v.tensor_copy(BcT[:, :, :], psM[:, 0:2 * P].rearrange("p (k c) -> p k c", c=P)[:, :, 0:NB]
                                  ).then_inc(misc_read, 1)
                elif kind == "QKV":
                    misc_wait(item)
                    v.tensor_copy(qkvb[:, :, :], psM[:, 0:6 * NB].rearrange("p (j n) -> p j n", n=NB)
                                  ).then_inc(misc_read, 1)
                    dve.wait_ge(misc_read, misc_at[item] + 1)
                    for g in range(2):
                        v.tensor_copy(QBpad[:, g, 0:NB], qkvb[:, g, :])
                        v.tensor_copy(QBpad[:, g, NB:2 * NB], qkvb[:, g, :])
                        for part in range(3):
                            last = v.tensor_tensor(KBexp[:, g, :, NB * part:NB * (part + 1)],
                                            bc(qkvb[:, 2 + g, :].rearrange("p (o n) -> p o n", o=1), [P, UH, NB]),
                                            bc(head_mask_q[:, :].rearrange("p (h o) -> p h o", o=1), [P, UH, NB]),
                                            ALU.mult)
                    last.then_inc(bases_ready, 1)
                    dve.wait_ge(bases_ready, 2)
                    for g in range(2):
                        last = v.tensor_tensor(
                            VBexp[:, g, 32 * g:32 * g + 32].rearrange("p (h n) -> p h n", n=NB),
                            bc(qkvb[:, 4 + g, :].rearrange("p (o n) -> p o n", o=1), [P, UH, NB]),
                            bc(head_mask[:, :].rearrange("p (h o) -> p h o", o=1), [P, UH, NB]), ALU.mult)
                    last.then_inc(bases_ready, 1)
                elif kind == "Arep":
                    misc_wait(item)
                    v.tensor_copy(Arep[:, :, :], psM4[:, 0:2, :]).then_inc(misc_read, 1)
                elif kind == "M":
                    misc_wait(item)
                    v.tensor_copy(M2[0:4 * HEADS, :], psM[0:4 * HEADS, 0:D]).then_inc(misc_read, 1)
                    dve.wait_ge(misc_read, misc_at[item] + 1)
                    centre(M2c[0:ZF, :], M2[0:ZF, :], ZF).then_inc(bases_ready, 1)
                elif kind == "McT":
                    misc_wait(item)
                    v.tensor_copy(McT[:, :, :], psM4[:, 0:KD, 0:ZF]).then_inc(misc_read, 1)
                elif kind == "fold":
                    fold_lo(item)
                elif kind == "soft":
                    b = item[1]
                    g = gathered[:, TB * b:TB * (b + 1), :]
                    dve.wait_ge(rows_in[b], 16 * TB)
                    if b:
                        dve.wait_ge(base_exp, b)
                    link(v.tensor_reduce(soft_s[:, 0, :], g, AX.X, ALU.max))
                    v.tensor_tensor(soft_e[:, :, :], g, bc(soft_s[:, 0, :].rearrange("p (t o) -> p t o", o=1),
                                                          [P, TB, NB]), ALU.subtract).then_inc(logit_shift, 1)
                elif kind == "mix":
                    b = item[1]
                    dve.wait_ge(base_exp, b + 1)
                    link(v.tensor_reduce(soft_s[:, 1, :], soft_x[:, :, :], AX.X, ALU.add))
                    link(v.reciprocal(soft_s[:, 2, :], soft_s[:, 1, :]))
                    inv = bc(soft_s[:, 2, :].rearrange("p (t o) -> p t o", o=1), [P, TB, NB])
                    v.tensor_tensor(Z[:, TB * b:TB * (b + 1), 4 * HEADS:ZF], soft_x[:, :, :], inv, ALU.mult)
                    if b:
                        dve.wait_ge(misc_written, misc_at[("CT", b - 1)] + 1)
                    v.tensor_tensor(CP[:, :, 0:NB], soft_x[:, :, :], inv, ALU.mult).then_inc(coeff_ready, 1)
                elif kind == "keys":
                    b = item[1]
                    dve.wait_ge(rstd_ready, b + 1)
                    dve.wait_ge(coeff_ready, b + 1)
                    if b:
                        dve.wait_ge(vst_ready, b)
                    link(v.tensor_tensor(U[:, :, :], Z[:, TB * b:TB * (b + 1), 4 * HEADS:ZF],
                                         bc(rstd[:, 1, :].rearrange("p (t o) -> p t o", o=1), [P, TB, NB]), ALU.mult))
                    link(v.tensor_copy(KE[:, :, 0:NB].bitcast(F32R), U[:, :, :]))
                    v.tensor_tensor(KE[:, :, NB:2 * NB], U[:, :, :], KE[:, :, 0:NB], ALU.subtract)
                    link(v.tensor_copy(KE[:, :, 2 * NB:3 * NB], KE[:, :, 0:NB]))
                    if b:
                        dve.wait_ge(misc_written, misc_at[("KT", b - 1)] + 1)
                    v.tensor_copy(KE8[:, :, :, :],
                                  bc(KE[:, :, :].rearrange("p t (o r) -> p t o r", o=1), [P, TB, UH, ROWS])
                                  ).then_inc(ke_ready, 1)
                elif kind == "values":
                    b = item[1]
                    if b >= 2:
                        dve.wait_ge(pv_done, 4 * (b - 1))
                    elif b == 0:
                        dve.wait_ge(consts, 5)
                    v.tensor_copy(Vst[b % 2][:, :, :].rearrange("p t (r s) -> p t r s", s=40)[:, :, :, 0:NB],
                                  bc(U[:, :, :].rearrange("p t (o n) -> p t o n", o=1), [P, TB, 4, NB])
                                  ).then_inc(vst_ready, 1)
                elif kind == "QA":
                    b, g = item[1:]
                    u = 2 * b + g
                    dve.wait_ge(qh_ready, u + 1)
                    if u >= 2:
                        dve.wait_ge(s_ready, 20 * (u - 1))
                    v.scalar_tensor_tensor(RQ1[g][:, :], RQh[:, :].bitcast(F32), neg_lo_rows[:, :], psM[:, :],
                                           ALU.mult, ALU.add).then_inc(misc_read, 1)
                elif kind == "S":
                    _, u, k = item
                    n = 20 * u + k
                    h = 4 * (k // 10) + 2 * ((k % 10) // 5)
                    kk = k % 5
                    dve.wait_ge(s_ready, n + 1)
                    m = maxp[u % 2]
                    src = psS[:, n % 2, :].rearrange("p (n c) -> p n c", c=P)
                    if kk < 4:
                        dst = m[:, h + kk // 2, 4 * (kk % 2):4 * (kk % 2) + 4]
                    else:
                        dst = m[:, h:h + 2, 8:10]
                        src = psS[:, n % 2, :].rearrange("p (a n c) -> p a n c", a=2, c=P)
                    v.tensor_reduce(dst, src, AX.X, ALU.max).then_inc(max_done, 1)
                elif kind == "max":
                    u = item[1]
                    m = maxp[u % 2]
                    dve.wait_ge(max_done, 20 * (u + 1))
                    if u:
                        dve.wait_ge(mexp_ready, u)
                    for qb, (a, z) in enumerate([(4, 5), (8, 10), (5, 8), (0, 4)]):
                        last = v.tensor_reduce(nm[:, qb, :], m[:, :, a:z], AX.X, ALU.max, negate=True)
                    link(last)
                    if u:
                        dve.wait_ge(misc_written, misc_at[("shift", u - 1)] + 1)
                    else:
                        dve.wait_ge(consts, 5)
                    hi = mexp[:, :, :, 3 * NB]
                    link(v.tensor_copy(hi.bitcast(F32R), nm[:, :, :]))
                    v.tensor_tensor(mexp[:, :, :, 3 * NB + 1], nm[:, :, :], hi, ALU.subtract).then_inc(mexp_ready, 1)
                elif kind == "shift":
                    u = item[1]
                    g = u % 2
                    misc_wait(item)
                    if u >= 2:
                        dve.wait_ge(t_ready, 12 * (u - 1))
                    v.tensor_tensor(RQ2[g][:, :], RQ1[g][:, :].bitcast(F32), psM[:, :], ALU.add
                                    ).then_inc(misc_read, 1)
                elif kind == "ZT":
                    b = item[1]
                    misc_wait(item)
                    link(v.reciprocal(rec[:, :, :], psM[:, :].rearrange("p (t h e) -> p t h e", t=TB, e=8)[:, :, :, NB]))
                    for t in range(TB):
                        last = v.tensor_tensor(
                            Z[:, TB * b + t, 0:4 * HEADS].rearrange("p (r j n) -> p j r n", j=4, n=NB),
                            psM4[:, t, :].rearrange("p (j r e) -> p j r e", j=4, e=8)[:, :, :, 0:NB],
                            bc(rec[:, t, :].rearrange("p (j r o) -> p j r o", j=4, o=1), [P, 4, 4, NB]), ALU.mult)
                    last.then_inc(misc_read, 1)
                elif kind == "zab":
                    b = item[1]
                    dve.wait_ge(rstd2_ready, b + 1)
                    link(v.tensor_tensor(Zr[:, :, :], Z[:, TB * b:TB * (b + 1), 0:ZF],
                                         bc(rstd2[:, 1, :].rearrange("p (t o) -> p t o", o=1), [P, TB, ZF]), ALU.mult))
                    half = ZF // 2
                    r = rows[:, TB * b:TB * (b + 1), :]
                    link(v.tensor_copy(r[:, :, 0:ZF].bitcast(F32R), Zr[:, :, :]))
                    v.tensor_copy(r[:, :, ZF:ZR], r[:, :, 0:half])
                    v.tensor_copy(r[:, :, ZR + ZF:2 * ZR], r[:, :, half:ZF])
                    v.tensor_tensor(r[:, :, ZR:ZR + ZF], Zr[:, :, :], r[:, :, 0:ZF], ALU.subtract
                                    ).then_inc(zab_ready, 1)
                elif kind == "w2":
                    e = item[1]
                    dve.wait_ge(raw2_in, 16 * (e + 1))
                    if e == 1:
                        dve.wait_ge(t_ready, 12 * UNITS)
                    v.tensor_copy(W2[W2_OF[e]][:, 0, :, :], raw2[W2_OF[e]][:, :, :]).then_inc(w2_hi, 1)
                elif kind == "logits":
                    c = item[1]
                    dve.wait_ge(logits_ready, c + 1)
                    if c:
                        dve.wait_ge(misc_written, misc_at[("LT", c - 1)] + 1)
                    v.tensor_copy(LG[:, :], psT[:, c, :]).then_inc(lg_done, 1)
                elif kind == "LT":
                    c = item[1]
                    misc_wait(item)
                    v.tensor_reduce(L[:, TB * c:TB * (c + 1), :],
                                    psM[:, :].rearrange("p (t b r) -> p t r b", t=TB, r=32)[:, :, 0:E, :],
                                    AX.X, ALU.add).then_inc(misc_read, 1)
                elif kind == "route":
                    dve.wait_ge(misc_read, misc_at[("LT", BATCH - 1)] + 1)
                    link(v.tensor_tensor(L[:, :, :], L[:, :, :],
                                         bc(rb2b[:, :].rearrange("p (o n) -> p o n", o=1), [P, NT, E]), ALU.add))
                    link(v.tensor_reduce(Ls[:, 0, :], L[:, :, :], AX.X, ALU.max))
                    v.tensor_tensor(L[:, :, :], L[:, :, :],
                                    bc(Ls[:, 0, :].rearrange("p (t o) -> p t o", o=1), [P, NT, E]), ALU.subtract
                                    ).then_inc(rl_ready, 1)
                    dve.wait_ge(rexp_done, 1)
                    link(v.tensor_reduce(Ls[:, 0, :], Lx[:, :, :], AX.X, ALU.add))
                    link(v.reciprocal(Ls[:, 1, :], Ls[:, 0, :]))
                    link(v.tensor_tensor(prob[:, :, :], Lx[:, :, :],
                                         bc(Ls[:, 1, :].rearrange("p (t o) -> p t o", o=1), [P, NT, E]), ALU.mult))
                    other = bc(prob[:, :, :].rearrange("p t (o j) -> p t o j", o=1), [P, NT, E, E])
                    own = bc(prob[:, :, :].rearrange("p t (e o) -> p t e o", o=1), [P, NT, E, E])
                    v.tensor_tensor(cmp_a[:, :, :, :], other, own, ALU.is_gt)
                    link(v.tensor_tensor(cmp_b[:, :, :, :], other, own, ALU.is_equal))
                    dve.wait_ge(consts, 6)
                    link(v.tensor_tensor(cmp_b[:, :, :, :], cmp_b[:, :, :, :], tri[:, :, :, :], ALU.mult))
                    link(v.tensor_tensor(cmp_a[:, :, :, :], cmp_a[:, :, :, :], cmp_b[:, :, :, :], ALU.add))
                    link(v.tensor_reduce(rank[:, :, :], cmp_a[:, :, :, :], AX.X, ALU.add))
                    link(v.tensor_scalar(rank[:, :, :], rank[:, :, :], 1.5, None, ALU.is_lt))
                    v.tensor_tensor(wgt[:, :, :], rank[:, :, :], prob[:, :, :], ALU.mult)
                    v.tensor_tensor(rows[:, :, 2 * ZR + 1:XR], rank[:, :, 0:E - 1], prob[:, :, 0:E - 1], ALU.mult)
                    v.tensor_tensor(Z[:, :, ZF:ZF + E], rank[:, :, :], prob[:, :, :], ALU.mult).then_inc(w_ready, 1)
                elif kind == "places":
                    misc_wait(item)
                    before = psM[:, 0:(NT + 1) * E].rearrange("p (t e) -> p t e", e=E)
                    v.tensor_tensor(more[:, :, :], bc(before[0:1, NT, 0:E - 1].rearrange("p (e o) -> p e o", o=1),
                                                      [1, E - 1, TILES - MIN_TILES]), limits[:, :, :], ALU.is_gt)
                    link(v.scalar_tensor_tensor(dest[:, :, :], rank[:, :, 0:E - 1], -FAR, region_far[:, :, :],
                                                ALU.mult, ALU.add))
                    link(v.tensor_reduce(tiles_f[:, :], more[:, :, :], AX.X, ALU.add))
                    v.tensor_scalar(last_i[:, :], tiles_f[:, :], float(MIN_TILES - 1), None, ALU.add).then_inc(tiles_ready, 1)
                    v.tensor_tensor(dest[:, :, :], dest[:, :, :], before[:, 0:NT, 0:E - 1], ALU.add).then_inc(misc_read, 1)
                    dve.wait_ge(misc_read, misc_at[item] + 1)
                    v.tensor_reduce(dest_s[:, 0, :], dest[:, :, :], AX.X, ALU.min)
                    v.tensor_reduce(dest_s[:, 1, :], dest[:, :, :], AX.X, ALU.max)
                    link(v.tensor_reduce(dest_s[:, 2, :], dest[:, :, :], AX.X, ALU.add))
                    link(v.tensor_tensor(dest_s[:, 2, :], dest_s[:, 2, :], dest_s[:, 0, :], ALU.subtract))
                    link(v.tensor_tensor(dest_s[:, 1, :], dest_s[:, 2, :], dest_s[:, 1, :], ALU.subtract))
                    v.tensor_copy(dest_i[:, :, :], dest_s[:, 0:2, :]).then_inc(places_ready, 1)
                elif kind == "split":
                    j = item[1]
                    dve.wait_ge(gelu_done, N_UP_R + j + 1)
                    if j >= 3:
                        dve.wait_ge(down_done, j - 2)
                    link(v.tensor_copy(hl[j % 3][:, 0, :], hbuf[j % 2][:, :]))
                    v.tensor_tensor(hl[j % 3][:, 1, :], hbuf[j % 2][:, :], hl[j % 3][:, 0, :].bitcast(F32), ALU.subtract
                                    ).then_inc(split_done, 1)
                elif kind == "combine":
                    ec = item[1]
                    e, c = ec // BATCH, ec % BATCH
                    dve.wait_ge(down_done, EB * (ec + 1))
                    if e == 0:
                        dve.wait_ge(misc_read, misc_at[("FH", c, 1)] + 1)
                        dve.wait_ge(w_ready, 1)
                    else:
                        dve.wait_ge(comb_done, TB * (ec - BATCH + 1))
                    for t in range(TB):
                        a = acc[:, TB * c + t, :]
                        o = psT[:, 2 * (ec % 2) + t // 2, D * (t % 2):D * (t % 2 + 1)]
                        v.scalar_tensor_tensor(a, o, wgt[:, TB * c + t, TURN[e]:TURN[e] + 1], a, ALU.mult, ALU.add
                                               ).then_inc(comb_done, 1)

            last, tiles = tile_counts(dve)

            def split_tile(e, i):
                for b in range(1, EB, 2):
                    dve.wait_ge(s_gelu[e], upto(i, EB, b + 1))
                    if i is FIRST:
                        if e > 1:
                            dve.wait_ge(s_down[e - 1], upto((last[e - 1], 0), EB, b + 1))
                    else:
                        dve.wait_ge(s_down[e], upto((i[0], 0), EB, b + 1))
                    h = hbuf[b // 2 % 2][:, :].rearrange("p (b c) -> p b c", b=2)
                    v.tensor_copy(hs[:, b - 1:b + 1, 0, :], h).then_inc(hi_done[e], 1)
                    dve.wait_ge(hi_done[e], upto(i, EB // 2, b // 2 + 1))
                    v.tensor_tensor(hs[:, b - 1:b + 1, 1, :], h, hs[:, b - 1:b + 1, 0, :].bitcast(F32), ALU.subtract
                                    ).then_inc(s_split[e], 1)
                    if i is FIRST and (e, b) in FOLD_AT:
                        fold_lo(FOLD_AT[e, b])

            for e in range(1, E):
                split_tile(e, FIRST)
                if e < E - 1:
                    dve.wait_ge(raw2_late, 16 * e)
                    v.tensor_copy(W2[W2_OF[e + 1]][:, 0, :, :], raw2[W2_OF[e + 1]][:, :, :]).then_inc(w2_hi, 1)
                with dve.If(last[e] > 0):
                    with dve.Fori(0, last[e]) as m:
                        split_tile(e, (m, 1))


_INS = ["x", "L0_tok_coeff_weight", "L0_tok_base_embed_weight", "L0_tok_lang_bias", "L0_attn_w_qkv", "L0_attn_w_proj",
        "L0_ffn_rW1", "L0_ffn_rb1", "L0_ffn_rW2", "L0_ffn_rb2", "L0_ffn_We1", "L0_ffn_be1", "L0_ffn_We2", "L0_ffn_be2"]


def kernel(**inputs):
    import concourse.bacc as bacc
    from concourse.bass_utils import run_bass_kernel_spmd

    nc = bacc.Bacc("TRN2", target_bir_lowering=False, num_devices=1)
    arrays, args = {}, []
    for name in _INS:
        a = np.ascontiguousarray(inputs[name])
        arrays[f"in_{name}"] = a
        args.append(nc.dram_tensor(f"in_{name}", a.shape, mybir.dt.from_np(a.dtype), kind="ExternalInput").ap())
    out = nc.dram_tensor("out", (BATCH, SEQ, D), F32, kind="ExternalOutput").ap()
    tower_kernel(nc, *args, out)
    r = run_bass_kernel_spmd(nc, [arrays], core_ids=[0])
    return r.results[0]["out"]
```
